# Optimizing a Trainium2 kernel written in Bass

```python
import numpy as np
import jax
import jax.numpy as jnp

def _softmax(x, axis=-1):
    return jax.nn.softmax(x, axis=axis)

def _gelu(x):
    return jax.nn.gelu(x, approximate=True)

def _silu(x):
    return jax.nn.silu(x)

def _sigmoid(x):
    return jax.nn.sigmoid(x)

def _layernorm(x, axis=-1, eps=1e-05):
    m = jnp.mean(x, axis=axis, keepdims=True)
    v = jnp.var(x, axis=axis, keepdims=True)
    return (x - m) / jnp.sqrt(v + eps)

def _scatter_add(tgt, idx, src, axis=0):
    return tgt.at[idx].add(src)

def _segment_sum(src, seg, n):
    return jax.ops.segment_sum(src, seg, n)
kernel_name = 'mk_xattn_ffn_d2_seqx_r4_8eee9a'

def setup_inputs(seed: int=0):
    np.random.seed(seed)
    _w = jnp.asarray

    def _rec_inputs():
        import jax
        import jax.numpy as jnp
        _rk = jax.random.key(seed)
        x = 7.22e-05 + 1 * jax.random.normal(jax.random.fold_in(_rk, 1), (4, 512, 512), jnp.float32)
        _lenS = 512 - jax.random.randint(jax.random.fold_in(_rk, 7), (4,), 0, max(1, 512 // 4) + 1, jnp.int32)
        _lenS2 = 512 - jax.random.randint(jax.random.fold_in(_rk, 8), (4,), 0, max(1, 512 // 4) + 1, jnp.int32)
        _ctx_2048P = jax.random.normal(jax.random.fold_in(_rk, 11), (4, 16, 512), jnp.float32)
        _ctx_2048c = jax.random.dirichlet(jax.random.fold_in(_rk, 511), 0.3 * jnp.ones((16,), jnp.float32), (4, 512))
        _ctx_2048t = jnp.einsum('bsk,bkd->bsd', _ctx_2048c, _ctx_2048P)
        _ctx_2048t = _ctx_2048t * jax.lax.rsqrt(jnp.mean(jnp.square(_ctx_2048t)) + 1e-12) * 0.953939
        ctx_2048 = 4.13588e-05 + 0.999923 * (_ctx_2048t + 0.3 * jax.random.normal(jax.random.fold_in(_rk, 611), (4, 512, 512), jnp.float32))
        return (x, ctx_2048)
    x, ctx_2048 = _rec_inputs()

    def _L0_xattn_setup():
        import jax, jax.numpy as jnp
        import numpy as np
        N_HEAD = 8
        key = jax.random.key(seed)
        k1, k2, k3 = jax.random.split(key, 3)
        B, D, L = (4, 256, 512)
        q = jax.random.normal(k1, (B, D, L), dtype=jnp.float32)
        k = jax.random.normal(k2, (B, D, L), dtype=jnp.float32)
        v = jax.random.normal(k3, (B, D, L), dtype=jnp.float32)
        gamma = jnp.ones((), dtype=jnp.float32)
        return {'q': q, 'k': k, 'v': v, 'gamma': gamma}
    _L0_xattn_all = _L0_xattn_setup()
    _L0_xattn_in = {k: v for k, v in _L0_xattn_all.items() if k in ('gamma',)}
    del _L0_xattn_all

    def _L0_ffn_setup():
        import jax, jax.numpy as jnp
        import numpy as np
        TOP_K = 2
        SCALING = 2.0
        key = jax.random.key(seed)
        ks = jax.random.split(key, 10)
        B, S, H, I, E, R = (1, 128, 512, 256, 8, 16)
        w = 1.0 / np.sqrt(H)
        inp = {'x': jax.random.normal(ks[0], (B, S, H), jnp.float32), 'gate_weight': jax.random.normal(ks[1], (E, H), jnp.float32) * w, 'gate_lora_A': jax.random.normal(ks[2], (R, H), jnp.float32) * 0.02, 'gate_lora_B': jax.random.normal(ks[3], (E, R), jnp.float32) * 0.02, 'gate_up_proj': jax.random.normal(ks[4], (E, H, 2 * I), jnp.float32) * w, 'down_proj': jax.random.normal(ks[5], (E, I, H), jnp.float32) * (1.0 / np.sqrt(I)), 'gup_lora_A': jax.random.normal(ks[6], (E, R, H), jnp.float32) * 0.02, 'gup_lora_B': jax.random.normal(ks[7], (E, 2 * I, R), jnp.float32) * 0.02, 'down_lora_A': jax.random.normal(ks[8], (E, R, I), jnp.float32) * 0.02, 'down_lora_B': jax.random.normal(ks[9], (E, H, R), jnp.float32) * 0.02}
        return inp
    _L0_ffn_all = _L0_ffn_setup()
    _L0_ffn_in = {k: v for k, v in _L0_ffn_all.items() if k in ('gate_weight', 'gate_lora_A', 'gate_lora_B', 'gate_up_proj', 'down_proj', 'gup_lora_A', 'gup_lora_B', 'down_lora_A', 'down_lora_B')}
    del _L0_ffn_all

    def _L1_xattn_setup():
        import jax, jax.numpy as jnp
        import numpy as np
        D_MODEL = 512
        NUM_HEADS = 16
        HEAD_DIM = D_MODEL // NUM_HEADS

        def _fq_sym(x, axis):
            s = jnp.max(jnp.abs(x), axis=axis, keepdims=True) / 127.0
            s = jnp.maximum(s, 1e-08)
            q = jnp.clip(jnp.round(x / s), -127.0, 127.0) * s
            return x + jax.lax.stop_gradient(q - x)

        def _fq_unsigned(x, axis):
            s = jnp.max(x, axis=axis, keepdims=True) / 255.0
            s = jnp.maximum(s, 1e-08)
            q = jnp.clip(jnp.round(x / s), 0.0, 255.0) * s
            return x + jax.lax.stop_gradient(q - x)
        key = jax.random.key(seed)
        ks = jax.random.split(key, 8)
        B, N, M, C = (2, 512, 128, D_MODEL)
        return {'x': jax.random.normal(ks[0], (B, N, C), jnp.float32), 'cond': jax.random.normal(ks[1], (B, M, C), jnp.float32), 'Wq': jax.random.normal(ks[2], (C, C), jnp.float32) * 0.02, 'bq': jnp.zeros((C,), jnp.float32), 'Wkv': jax.random.normal(ks[3], (C, 2 * C), jnp.float32) * 0.02, 'bkv': jnp.zeros((2 * C,), jnp.float32), 'Wp': jax.random.normal(ks[4], (C, C), jnp.float32) * 0.02, 'bp': jnp.zeros((C,), jnp.float32)}
    _L1_xattn_all = _L1_xattn_setup()
    _L1_xattn_in = {k: v for k, v in _L1_xattn_all.items() if k in ('Wq', 'bq', 'Wkv', 'bkv', 'Wp', 'bp')}
    del _L1_xattn_all

    def _L1_ffn_setup():
        import jax, jax.numpy as jnp
        import numpy as np
        HIDDEN = 512
        INTER = 1376
        LUT_SIZE = 16

        def _ghost_linear(x, idx, lut):
            w = lut[idx]
            return jnp.einsum('bsh,oh->bso', x, w)
        key = jax.random.key(seed)
        k_x, k_lut, k_g, k_u, k_d = jax.random.split(key, 5)
        x = jax.random.normal(k_x, (2, 1024, HIDDEN), dtype=jnp.float32)
        lut = jax.random.normal(k_lut, (LUT_SIZE,), dtype=jnp.float32) * 0.02
        gate_idx = jax.random.randint(k_g, (INTER, HIDDEN), 0, LUT_SIZE, dtype=jnp.int32)
        up_idx = jax.random.randint(k_u, (INTER, HIDDEN), 0, LUT_SIZE, dtype=jnp.int32)
        down_idx = jax.random.randint(k_d, (HIDDEN, INTER), 0, LUT_SIZE, dtype=jnp.int32)
        return {'x': x, 'lut': lut, 'gate_idx': gate_idx, 'up_idx': up_idx, 'down_idx': down_idx}
    _L1_ffn_all = _L1_ffn_setup()
    _L1_ffn_in = {k: v for k, v in _L1_ffn_all.items() if k in ('lut', 'gate_idx', 'up_idx', 'down_idx')}
    del _L1_ffn_all
    return {'x': x, 'ctx_2048': ctx_2048, 'L0_xattn_gamma': _L0_xattn_in['gamma'], 'L0_ffn_gate_weight': _L0_ffn_in['gate_weight'], 'L0_ffn_gate_lora_A': _L0_ffn_in['gate_lora_A'], 'L0_ffn_gate_lora_B': _L0_ffn_in['gate_lora_B'], 'L0_ffn_gate_up_proj': _L0_ffn_in['gate_up_proj'], 'L0_ffn_down_proj': _L0_ffn_in['down_proj'], 'L0_ffn_gup_lora_A': _L0_ffn_in['gup_lora_A'], 'L0_ffn_gup_lora_B': _L0_ffn_in['gup_lora_B'], 'L0_ffn_down_lora_A': _L0_ffn_in['down_lora_A'], 'L0_ffn_down_lora_B': _L0_ffn_in['down_lora_B'], 'L1_xattn_Wq': _L1_xattn_in['Wq'], 'L1_xattn_bq': _L1_xattn_in['bq'], 'L1_xattn_Wkv': _L1_xattn_in['Wkv'], 'L1_xattn_bkv': _L1_xattn_in['bkv'], 'L1_xattn_Wp': _L1_xattn_in['Wp'], 'L1_xattn_bp': _L1_xattn_in['bp'], 'L1_ffn_lut': _L1_ffn_in['lut'], 'L1_ffn_gate_idx': _L1_ffn_in['gate_idx'], 'L1_ffn_up_idx': _L1_ffn_in['up_idx'], 'L1_ffn_down_idx': _L1_ffn_in['down_idx']}

def reference(x, ctx_2048, L0_xattn_gamma, L0_ffn_gate_weight, L0_ffn_gate_lora_A, L0_ffn_gate_lora_B, L0_ffn_gate_up_proj, L0_ffn_down_proj, L0_ffn_gup_lora_A, L0_ffn_gup_lora_B, L0_ffn_down_lora_A, L0_ffn_down_lora_B, L1_xattn_Wq, L1_xattn_bq, L1_xattn_Wkv, L1_xattn_bkv, L1_xattn_Wp, L1_xattn_bp, L1_ffn_lut, L1_ffn_gate_idx, L1_ffn_up_idx, L1_ffn_down_idx):
    import jax
    import jax.numpy as jnp

    def _L0_xattn_ref(q, k, v, gamma):
        import jax, jax.numpy as jnp
        import numpy as np
        N_HEAD = 8
        B, Dq, Lq = q.shape
        Dv, Lk = (v.shape[-2], v.shape[-1])
        h = N_HEAD
        dq = Dq // h
        dv = Dv // h
        qh = q.reshape(B, h, dq, Lq)
        kh = k.reshape(B, h, dq, Lk)
        vh = v.reshape(B, h, dv, Lk)
        scale = 1.0 / jnp.sqrt(jnp.asarray(dq, dtype=q.dtype))
        qk = jnp.einsum('bhdq,bhdl->bhql', qh, kh) * scale
        sm = jax.nn.softmax(qk, axis=-1)
        ret = jnp.einsum('bhql,bhdl->bhdq', sm, vh)
        ret = ret.reshape(B, Dv, Lq)
        return gamma * ret

    def _L0_ffn_ref(x, gate_weight, gate_lora_A, gate_lora_B, gate_up_proj, down_proj, gup_lora_A, gup_lora_B, down_lora_A, down_lora_B):
        import jax, jax.numpy as jnp
        import numpy as np
        TOP_K = 2
        SCALING = 2.0
        B, S, H = x.shape
        xf = x.reshape(-1, H)
        gate_delta = SCALING * (gate_lora_B @ gate_lora_A)
        router_logits = xf @ gate_weight.T + xf @ gate_delta.T
        probs = jax.nn.softmax(router_logits.astype(jnp.float32), axis=-1)
        routing_weights, selected = jax.lax.top_k(probs, TOP_K)
        routing_weights = routing_weights / routing_weights.sum(-1, keepdims=True)
        routing_weights = routing_weights.astype(xf.dtype)
        gup = jnp.einsum('th,eho->teo', xf, gate_up_proj)
        gup = gup + SCALING * jnp.einsum('ter,eor->teo', jnp.einsum('th,erh->ter', xf, gup_lora_A), gup_lora_B)
        gates, h = jnp.split(gup, 2, axis=-1)
        h = jax.nn.silu(gates) * h
        out = jnp.einsum('tei,eih->teh', h, down_proj)
        out = out + SCALING * jnp.einsum('ter,ehr->teh', jnp.einsum('tei,eri->ter', h, down_lora_A), down_lora_B)
        out_sel = jnp.take_along_axis(out, selected[:, :, None], axis=1)
        y = jnp.einsum('tkh,tk->th', out_sel, routing_weights)
        return y.reshape(B, S, H)

    def _L1_xattn_ref(x, cond, Wq, bq, Wkv, bkv, Wp, bp):
        import jax, jax.numpy as jnp
        import numpy as np
        D_MODEL = 512
        NUM_HEADS = 16
        HEAD_DIM = D_MODEL // NUM_HEADS

        def _fq_sym(x, axis):
            s = jnp.max(jnp.abs(x), axis=axis, keepdims=True) / 127.0
            s = jnp.maximum(s, 1e-08)
            q = jnp.clip(jnp.round(x / s), -127.0, 127.0) * s
            return x + jax.lax.stop_gradient(q - x)

        def _fq_unsigned(x, axis):
            s = jnp.max(x, axis=axis, keepdims=True) / 255.0
            s = jnp.maximum(s, 1e-08)
            q = jnp.clip(jnp.round(x / s), 0.0, 255.0) * s
            return x + jax.lax.stop_gradient(q - x)
        B, N, C = x.shape
        H, hd = (NUM_HEADS, HEAD_DIM)
        q = (x @ Wq + bq).reshape(1, B * N, H, hd)
        kv = (cond @ Wkv + bkv).reshape(1, -1, 2, H, hd)
        k, v = (kv[:, :, 0], kv[:, :, 1])
        scale = 1.0 / np.sqrt(hd).astype(np.float32)
        q = jnp.transpose(q * scale, (0, 2, 1, 3))
        k = jnp.transpose(k, (0, 2, 1, 3))
        v = jnp.transpose(v, (0, 2, 1, 3))
        q = _fq_sym(q, axis=-1)
        k = _fq_sym(k, axis=-1)
        v = _fq_sym(v, axis=2)
        attn = jnp.einsum('bhqd,bhkd->bhqk', q, k)
        attn = jax.nn.softmax(attn.astype(jnp.float32), axis=-1)
        attn = _fq_unsigned(attn, axis=-1)
        out = jnp.einsum('bhqk,bhkd->bhqd', attn, v)
        out = jnp.transpose(out, (0, 2, 1, 3)).reshape(B, N, C)
        return out @ Wp + bp

    def _L1_ffn_ref(x, lut, gate_idx, up_idx, down_idx):
        import jax, jax.numpy as jnp
        import numpy as np
        HIDDEN = 512
        INTER = 1376
        LUT_SIZE = 16

        def _ghost_linear(x, idx, lut):
            w = lut[idx]
            return jnp.einsum('bsh,oh->bso', x, w)
        gate = _ghost_linear(x, gate_idx, lut)
        up = _ghost_linear(x, up_idx, lut)
        h = jax.nn.silu(gate) * up
        return _ghost_linear(h, down_idx, lut)
    x = x + _L0_xattn_ref(_layernorm(x, axis=-1), ctx_2048, ctx_2048, L0_xattn_gamma)
    x = x + _L0_ffn_ref(_layernorm(x, axis=-1), L0_ffn_gate_weight, L0_ffn_gate_lora_A, L0_ffn_gate_lora_B, L0_ffn_gate_up_proj, L0_ffn_down_proj, L0_ffn_gup_lora_A, L0_ffn_gup_lora_B, L0_ffn_down_lora_A, L0_ffn_down_lora_B)
    x = x + _L1_xattn_ref(_layernorm(x, axis=-1), ctx_2048, L1_xattn_Wq, L1_xattn_bq, L1_xattn_Wkv, L1_xattn_bkv, L1_xattn_Wp, L1_xattn_bp)
    x = x + _L1_ffn_ref(_layernorm(x, axis=-1), L1_ffn_lut, L1_ffn_gate_idx, L1_ffn_up_idx, L1_ffn_down_idx)
    return x

_drawn_inputs = setup_inputs


def setup_inputs(seed=0):
    import zlib

    import numpy as np

    out = dict(_drawn_inputs(seed))
    spreads = {'L1_xattn_bq': (0.0, 2.0), 'L1_xattn_bkv': (0.0, 0.1), 'L1_xattn_bp': (0.0, 0.1)}
    factors = {'L0_ffn_down_lora_A': 3.112, 'L0_ffn_down_lora_B': 3.114, 'L1_xattn_Wq': 8.0}
    for name, (base, spread) in spreads.items():
        noise = np.random.default_rng([zlib.crc32(name.encode()), seed]).standard_normal(out[name].shape)
        drawn = base * np.exp(spread * noise) if base else spread * noise
        out[name] = jnp.asarray(drawn.astype(out[name].dtype))
    for name, factor in factors.items():
        out[name] = (out[name] * factor).astype(out[name].dtype)
    return out
```

```python
import math
from contextlib import ExitStack

import concourse.bass as bass
from concourse import mybir

F32 = mybir.dt.float32
F32R = mybir.dt.float32r
BF16 = mybir.dt.bfloat16
I16 = mybir.dt.int16
I32 = mybir.dt.int32
ALU = mybir.AluOpType
ACT = mybir.ActivationFunctionType
AX = mybir.AxisListType

P = 128
D = 512
T = 2048
NT = T // P
DC = D // P
TT = T // 512
EPS = 1e-5

H0 = 8
HROWS = 512 // H0
E = 8
R = 16
INTER = 1376
GROUP = 256
NG1 = -(-INTER // GROUP)
LAST = INTER - (NG1 - 1) * GROUP
WPARTS = DC + GROUP // P
LUT = 16

H1 = 16
HD = D // H1
QSCALE = 1.0 / math.sqrt(HD)
QMAX = 127.0
PMAX = 255.0
SMIN = 1e-8
KROWS = 3 * HD


class Chain:

    def __init__(self, eng, sem, passed=None):
        self.eng, self.sem, self.base, self.n, self.passed = eng, sem, 0, 0, passed

    def enter(self, base):
        self.base, self.n = base, 0

    def link(self, ins):
        self.n += 1
        ins.then_inc(self.sem, 1)
        self.eng.wait_ge(self.sem, self.base + self.n)
        if self.passed:
            self.eng.sem_inc(self.passed, 1)


STOPAT = 9


def build(nc, a, out, STOP=None):
    STOP = STOPAT if STOP is None else STOP
    with ExitStack() as ctx:
        def sem(name):
            return ctx.enter_context(nc.semaphore(name))

        def dram(name, shape, dt):
            return nc.dram_tensor(name, shape, dt, kind="Internal").ap()

        def sb(stack, name, shape, dt):
            return stack.enter_context(nc.sbuf_tensor(name, shape, dt))

        X = sb(ctx, "X", [P, NT, D], F32)
        idf = sb(ctx, "idf", [P, P], F32)
        idb = sb(ctx, "idb", [P, P], BF16)
        ones = sb(ctx, "ones", [P, P], F32)
        gam = sb(ctx, "gam", [P, 1], F32)
        st = sb(ctx, "st", [P, NT, 6], F32)
        mu = sb(ctx, "mu", [P, NT], F32)
        rstd = sb(ctx, "rstd", [P, NT], F32)
        lnt = sb(ctx, "lnt", [P, 4, NT], F32)
        W8 = sb(ctx, "W8", [P, NT, E], F32)
        lut = sb(ctx, "lut", [P, LUT], F32)
        ix = sb(ctx, "ix", [P, D], I32)
        pick = sb(ctx, "pick", [P, 2, D], F32)
        dec = sb(ctx, "dec", [P, D], F32)

        PS = ctx.enter_context(nc.psum_tensor("PS", [P, 8, 512], F32))

        with ExitStack() as s:
            Kf = sb(s, "Kf", [P, 2, D], F32)
            Vf = sb(s, "Vf", [P, 2, D], F32)
            Qf = sb(s, "Qf", [P, D], F32)
            QH = sb(s, "QH", [P, 2, D], F32R)
            QL = sb(s, "QL", [P, 2, D], F32R)
            KH = sb(s, "KH", [P, 2, D], F32R)
            KL = sb(s, "KL", [P, 2, D], F32R)
            VH = sb(s, "VH", [P, 2, D], F32R)
            VL = sb(s, "VL", [P, 2, D], F32R)
            pr = sb(s, "pr", [P, 2, D], F32)
            nmx = sb(s, "nmx", [P, 2], F32)
            psm = sb(s, "psm", [P, 2], F32)
            rsm = sb(s, "rsm", [P, 2], F32)
            PTH = sb(s, "PTH", [P, 2, 4, D], F32R)
            PTL = sb(s, "PTL", [P, 2, 4, D], F32R)
        with ExitStack() as s:
            XTH = sb(s, "XTH", [P, DC, T], F32R)
            XTL = sb(s, "XTL", [P, DC, T], F32R)
            WR = sb(s, "WR", [P, WPARTS, D], F32)
            WH = sb(s, "WH", [P, 2, WPARTS, D], F32R)
            WL = sb(s, "WL", [P, 2, WPARTS, D], F32R)
            xn = sb(s, "xn", [P, 2, D], F32)
            sg = sb(s, "sg", [P, 2, 512], F32)
            HF = sb(s, "HF", [P, 512], F32)
            HH = sb(s, "HH", [P, 2, 2, 512], F32R)
            HL = sb(s, "HL", [P, 2, 2, 512], F32R)
            lA = sb(s, "lA", [R, D + GROUP], F32)
            lB = sb(s, "lB", [R, 2, D], F32)
        with ExitStack() as s:
            s.enter_context(nc.sbuf_tensor("below_WR", [P, 2 * DC * T], F32))
            gA = sb(s, "gA", [R, D], F32)
            gB = sb(s, "gB", [R, E], F32)
            gW = sb(s, "gW", [P, DC, E], F32)
            gH = sb(s, "gH", [P, DC, P], F32R)
            gL = sb(s, "gL", [P, DC, P], F32R)
            gF = sb(s, "gF", [P, DC, P], F32)
            lgT = sb(s, "lgT", [E, T], F32)
            rt = sb(s, "rt", [P, 6, NT, E], F32)
            rm = sb(s, "rm", [P, 4, NT], F32)
            rev = sb(s, "rev", [P, NT, E], F32)
        with ExitStack() as s:
            VI = sb(s, "VI", [P, NT, D], BF16)
            SQ = sb(s, "SQ", [P, NT, H1], F32)
            svb = sb(s, "svb", [P, D], F32)
            AO = sb(s, "AO", [P, NT, D], F32)
            bq = sb(s, "bq", [P, D], F32)
            bkv = sb(s, "bkv", [P, 2 * D], F32)
            bp = sb(s, "bp", [P, D], F32)
            with ExitStack() as s2:
                wr = sb(s2, "wr", [P, DC, D], F32)
                wH = sb(s2, "wH", [P, 2, DC, D], F32R)
                wL = sb(s2, "wL", [P, 2, DC, D], F32R)
                CT = sb(s2, "CT", [P, 2, D], F32)
                CH = sb(s2, "CH", [P, 2, DC, P], F32R)
                CL = sb(s2, "CL", [P, 2, DC, P], F32R)
                kf = sb(s2, "kf", [P, D], F32)
                ki = sb(s2, "ki", [P, D], I16)
                kd = sb(s2, "kd", [P, D], F32)
                kp = sb(s2, "kp", [P, 2, 3, D], BF16)
                ksc = sb(s2, "ksc", [P, 4, H1], F32)
                kts = sb(s2, "kts", [P, 2, 3, D], BF16)
                vmx = sb(s2, "vmx", [P, D], F32)
                vdg = sb(s2, "vdg", [P, DC, P], F32)
                vsc = sb(s2, "vsc", [P, 2, DC], F32)
                rvb = sb(s2, "rvb", [P, D], F32)
                vii = sb(s2, "vii", [P, NT, D], I16)
            with ExitStack() as s2:
                KS = sb(s2, "KS", [P, 2, T], BF16)
                QS = sb(s2, "QS", [P, 2, T], BF16)
                ei = sb(s2, "ei", [P, 2, T], I16)
                pt = sb(s2, "pt", [P, 2, T], BF16)
                tm = sb(s2, "tm", [P, 2, 2], F32)
                tmn = sb(s2, "tmn", [P, 2], F32)
                tb = sb(s2, "tb", [P, 2], F32)
                sqc = sb(s2, "sqc", [P, 2], F32)
                esm = sb(s2, "esm", [P, 2, 2], F32)
                est = sb(s2, "est", [P, 2], F32)
                esr = sb(s2, "esr", [P, 2], F32)
        VF = AO

        kt_d = dram("kt_scratch", (3, D, T), BF16)
        qt_d = dram("qt_scratch", (D, T), BF16)
        w1_d = dram("w1_scratch", (NG1, P, WPARTS, D), F32)

        S = {n: sem(n) for n in (
            "x_in gam_in lut_in kv_in0 kv_in1 ident ones_set "
            "dve_own act_own pool_own sqrt_in sqrt_done "
            "q_split kv_hi kv_split s_ready nmax_ready exp_done p_ready pt_done pt_hi pt_lo pv0_done o0_used stats0 "
            "xn_ready xt_done xt_hi xt_lo router_in gW_ready gmerge g_hi g_lo lg_done lgT_copied lgt_done rt_e rt_done rexp "
            "w_in lora_in merge_done merged w_hi w_ready g_done silu_done u_used h_hi h_ready y_done y_added "
            "w1_in m1_merged w1_hi w1_ready g1_done silu1_done u1_used h1_hi h1_ready y1_done y1_added "
            "xn1_ready xt1_done xt1_hi xt1_lo "
            "bias_in wkv_in wkv_hi wkv_ready c_in0 c_in1 c_hi c_ready kv_done kv_used kp_ready kt_done kt_out kt_saved0 kt_saved1 "
            "vmx_ready vt_done vdg_ready svb_done v_ready "
            "wq_in wq_hi wq_ready qn_ready qx_done qx_hi qx_ready q_done q_used qp_ready qt_done qt_out qt_saved0 qt_saved1 "
            "wp_in wp_hi wp_ready ao_staged ao_t ao_hi ao_ready o_done o_used "
            "head_in0 head_in1 t_half t_max t_exp0 t_exp1 e_turned pt0_out pt1_out pv_done pv_used "
            "gp_passed pe_passed ix_in w1_saved out_stored "
        ).split()}

        def bank(i):
            return PS[:, i, :]

        def ln_finish(dve, ch):
            me, mo, ve, vo = st[:, :, 1], st[:, :, 4], st[:, :, 2], st[:, :, 5]
            ch.link(nc.vector.tensor_tensor(lnt[:, 0], me, mo, ALU.add))
            ch.link(nc.vector.tensor_tensor(lnt[:, 1], me, mo, ALU.subtract))
            ch.link(nc.vector.tensor_scalar(mu[:], lnt[:, 0], 0.5, None, ALU.mult))
            ch.link(nc.vector.tensor_tensor(lnt[:, 2], lnt[:, 1], lnt[:, 1], ALU.mult))
            ch.link(nc.vector.tensor_tensor(lnt[:, 0], ve, vo, ALU.add))
            ch.link(nc.vector.tensor_scalar(lnt[:, 1], lnt[:, 0], 1.0 / D, EPS, ALU.mult, ALU.add))
            nc.vector.scalar_tensor_tensor(out=lnt[:, 3], in0=lnt[:, 2], scalar=0.25, in1=lnt[:, 1],
                                           op0=ALU.mult, op1=ALU.add).then_inc(S["sqrt_in"], 1)

        def ln_root(act, n):
            act.wait_ge(S["sqrt_in"], n)
            nc.scalar.activation(lnt[:, 0], lnt[:, 3], ACT.Sqrt).then_inc(S["sqrt_done"], 1)

        def ln_invert(dve, ch, n, scale=None):
            dve.wait_ge(S["sqrt_done"], n)
            ch.link(nc.vector.reciprocal(rstd[:], lnt[:, 0]))
            if scale is not None:
                ch.link(nc.vector.tensor_scalar(rstd[:], rstd[:], scale, None, ALU.mult))

        def mm3(o, lh, ll, rh, rl, start, stop):
            nc.tensor.matmul(o, lh, rh, start=start, stop=False)
            nc.tensor.matmul(o, lh, rl, start=False, stop=False)
            return nc.tensor.matmul(o, ll, rh, start=False, stop=stop)

        block = ctx.enter_context(nc.Block())

        def store_x(sp, added, n):
            sp.wait_ge(S[added], n)
            for q in range(4):
                sp.dma_start(out[4 * q:4 * q + 4].rearrange("t p d -> p t d"), X[:, 4 * q:4 * q + 4, :]).then_inc(S["out_stored"], 16)
            sp.wait_ge(S["out_stored"], 64)

        def unit(g, tt, j, cols):
            return 2 * TT * g + (2 * tt + j if len(cols) == 2 else tt)

        MLP0 = dict(w_ready="w_ready", g_done="g_done", silu="silu_done", u_used="u_used", h_hi="h_hi", h_ready="h_ready",
                    y_done="y_done", y_added="y_added")
        MLP1 = dict(w_ready="w1_ready", g_done="g1_done", silu="silu1_done", u_used="u1_used", h_hi="h1_hi", h_ready="h1_ready",
                    y_done="y1_done", y_added="y1_added")

        @block.sync
        def _(sp):
            def attn0_in(t, par, n):
                if n is not None:
                    sp.wait_ge(S["kv_split"], n)
                sp.dma_start(Kf[:, par], a["ctx"][bass.ds(t, 1)].rearrange("o p d -> p (o d)")).then_inc(S[f"kv_in{par}"], 16)
                sp.dma_start(Vf[:, par], a["ctxT"][bass.ds(t, 1)].rearrange("o p d -> p (o d)")).then_inc(S[f"kv_in{par}"], 16)

            for q in range(4):
                sp.dma_start(X[:, 4 * q:4 * q + 4, :], a["x"][4 * q:4 * q + 4].rearrange("t p d -> p t d")).then_inc(S["x_in"], 16)
                if q == 0:
                    attn0_in(0, 0, None)
                    attn0_in(1, 1, None)
            sp.dma_start(gam[:], a["gamma"].partition_broadcast(P)).then_inc(S["gam_in"], 16)
            with sp.Fori(1, NT // 2) as i:
                for par in range(2):
                    attn0_in(2 * i + par, par, 2 * i + par - 1)
            if STOP == 1:
                return store_x(sp, "o0_used", 2 * NT)
            sp.wait_ge(S["pv0_done"], 2 * NT)
            for dst, src in ((gA[:], a["gA"]), (gB[:], a["gBT"]), (gW[:], a["gWT"].rearrange("(c p) e -> p c e", p=P))):
                sp.dma_start(dst, src).then_inc(S["router_in"], 16)
            sp.wait_ge(S["rt_done"], 1)

            def expert_in(e, n, m):
                if n is not None:
                    sp.wait_ge(S["w_ready"], n)
                sp.dma_start(WR[:, 0:DC, :], a["gup"][bass.ds(e, 1)].rearrange("o (c p) n -> p (o c) n", p=P)).then_inc(S["w_in"], 16)
                sp.dma_start(WR[:, DC:WPARTS, :], a["down"][bass.ds(e, 1)].rearrange("o (c p) n -> p (o c) n", p=P)).then_inc(S["w_in"], 16)
                sp.dma_start(lA[:], a["lA"][bass.ds(e, 1)].rearrange("o r n -> r (o n)")).then_inc(S["w_in"], 16)
                sp.dma_start(lB[:], a["lB"][bass.ds(e, 1)].rearrange("o r k n -> r (o k) n")).then_inc(S["w_in"], 16)

            expert_in(0, None, None)
            with sp.Fori(1, E) as e:
                expert_in(e, e, e)
            if STOP == 2:
                return store_x(sp, "y_added", 4 * TT * E)
            sp.wait_ge(S["y_done"], 4 * TT * E)
            for dst, src in ((bq, "bq"), (bkv, "bkv"), (bp, "bp")):
                sp.dma_start(dst[:], a[src].partition_broadcast(P)).then_inc(S["bias_in"], 16)

            def weight_in(name, col, s_in, freed, n):
                if freed:
                    sp.wait_ge(S[freed], n)
                sp.dma_start(wr[:], a[name][:, col:col + D].rearrange("(c p) n -> p c n", p=P)).then_inc(S[s_in], 16)

            weight_in("Wkv", 0, "wkv_in", None, 0)
            weight_in("Wkv", D, "wkv_in", "wkv_ready", 1)
            weight_in("Wq", 0, "wq_in", "wkv_ready", 2)

            def ctx_in(t, par, n):
                if n is not None:
                    sp.wait_ge(S["c_ready"], n)
                sp.dma_start(CT[:, par], a["ctxT"][bass.ds(t, 1)].rearrange("o p d -> p (o d)")).then_inc(S[f"c_in{par}"], 16)

            def save(src, dst, t, s_out, n, s_saved):
                sp.wait_ge(S[s_out], n)
                sp.dma_start(dst.rearrange("(c p) n -> p c n", p=P)[:, :, bass.ds(t * P, P)],
                             src.rearrange("p (c n) -> p c n", c=DC)).then_inc(S[s_saved], 16)

            ctx_in(0, 0, None)
            ctx_in(1, 1, None)
            with sp.Fori(0, NT // 2 - 1) as i:
                for par in range(2):
                    ctx_in(2 * i + par + 2, par, 2 * i + par + 1)
                    for k in range(3):
                        save(kts[:, par, k], kt_d[k], 2 * i + par, "kt_out", 2 * i + par + 1, f"kt_saved{par}")
            for par in range(2):
                for k in range(3):
                    save(kts[:, par, k], kt_d[k], NT - 2 + par, "kt_out", NT - 1 + par, f"kt_saved{par}")
            with sp.Fori(0, NT // 2) as i:
                for par in range(2):
                    save(kts[:, par, 0], qt_d, 2 * i + par, "qt_out", 2 * i + par + 1, f"qt_saved{par}")
            for par in range(2):
                sp.wait_ge(S[f"kt_saved{par}"], 16 * 3 * NT // 2)
                sp.wait_ge(S[f"qt_saved{par}"], 16 * NT // 2)

            def head_in(h, par, n):
                if n is not None:
                    sp.wait_ge(S["t_half"], n)
                for k in range(3):
                    sp.dma_start(KS[HD * k:HD * (k + 1), par], kt_d[k, bass.ds(h * HD, HD)]).then_inc(S[f"head_in{par}"], 16)
                    sp.dma_start(QS[HD * k:HD * (k + 1), par], qt_d[bass.ds(h * HD, HD)]).then_inc(S[f"head_in{par}"], 16)

            head_in(0, 0, None)
            head_in(1, 1, None)
            with sp.Fori(1, H1 // 2) as i:
                for par in range(2):
                    head_in(2 * i + par, par, (2 * i + par - 1) * 2 * NT)
            sp.wait_ge(S["pv_used"], H1 * NT)
            sp.dma_start(wr[:], a["Wp"].rearrange("(c p) n -> p c n", p=P)).then_inc(S["wp_in"], 16)
            if STOP == 3:
                return store_x(sp, "o_used", NT)
            sp.wait_ge(S["o_used"], NT)
            sp.wait_ge(S["w1_saved"], 16 * NG1 * WPARTS)

            def group_in(g, n):
                if n is not None:
                    sp.wait_ge(S["w1_ready"], n)
                sp.dma_start(WR[:], w1_d[bass.ds(g, 1)].rearrange("o p c n -> p (o c) n")).then_inc(S["w1_in"], 16)

            group_in(0, None)
            with sp.Fori(1, NG1) as g:
                group_in(g, g)
            store_x(sp, "y1_added", 4 * TT * NG1)

        @block.gpsimd
        def _(gp):
            nc.gpsimd.memset(ones[:], 1.0).then_inc(S["pool_own"], 1)
            nc.gpsimd.memset(idf[:], 0.0).then_inc(S["pool_own"], 1)
            nc.gpsimd.memset(idb[:], 0.0).then_inc(S["pool_own"], 1)
            gp.wait_ge(S["pool_own"], 3)
            for m in (idf, idb):
                nc.gpsimd.affine_select(out=m[:], in_=m[:], compare_op=ALU.not_equal, fill=1.0, base=0,
                                        pattern=[[-1, P]], channel_multiplier=1).then_inc(S["ident"], 1)
            if STOP >= 3:
                gp.dma_start(lut[:], a["lut"].partition_broadcast(P)).then_inc(S["lut_in"], 16)
                gp.wait_ge(S["lut_in"], 16)
                ch = Chain(gp, S["pool_own"], passed=S["gp_passed"])
                per = 2 * LUT - 1

                def decode(g, c, first, k):
                    gp.dma_start(ix[:], a["idx"][bass.ds(g, 1), :, c].rearrange("o p n -> p (o n)")).then_inc(S["ix_in"], 16)
                    gp.wait_ge(S["ix_in"], 16 * k + 16)
                    if not first:
                        gp.wait_ge(S["w1_saved"], 16 * k)
                    gp.sem_inc(S["gp_passed"], 1)
                    ch.enter(3 + per * k)
                    for j in range(LUT):
                        dst = dec[:] if j == 0 else pick[:, j % 2]
                        ch.link(nc.gpsimd.tensor_scalar(dst, ix[:], float(j), lut[:, j:j + 1], ALU.is_equal, ALU.mult))
                        if j:
                            ch.link(nc.gpsimd.tensor_tensor(dec[:], dec[:], pick[:, j % 2], ALU.add))
                    gp.dma_start(w1_d[bass.ds(g, 1), :, c].rearrange("o p n -> p (o n)"), dec[:]).then_inc(S["w1_saved"], 16)

                for c in range(WPARTS):
                    decode(0, c, c == 0, c)
                with gp.Fori(1, NG1) as g:
                    for c in range(WPARTS):
                        decode(g, c, False, g * WPARTS + c)

        NU = H1 * NT

        @block.tensor
        def _(pe):
            pe.wait_ge(S["ident"], 2)

            def scores0(i, k):
                n, tile, par, hh, c = 16 * i + k, 2 * i + k // 8, (k // 8) % 2, (k // 4) % 2, k % 4
                if k % 8 == 0:
                    pe.wait_ge(S["q_split"], tile + 1)
                    pe.wait_ge(S["kv_split"], tile + 1)
                if not (isinstance(n, int) and n < 2):
                    pe.wait_ge(S["exp_done"], n - 1)
                rows = slice(HROWS * hh, HROWS * (hh + 1))
                mm3(bank(k % 2), QH[rows, par, c * P:(c + 1) * P], QL[rows, par, c * P:(c + 1) * P],
                    KH[rows, par], KL[rows, par], True, True).then_inc(S["s_ready"], 1)

            def turn0(i, k):
                n = 16 * i + k
                pe.wait_ge(S["p_ready"], n + 1)
                if not (isinstance(n, int) and n < 2):
                    pe.wait_ge(S["pt_lo"], n - 1)
                for lc in range(4):
                    m = nc.tensor.transpose(bank(2 + k % 2)[:, lc * P:(lc + 1) * P], pr[:, k % 2, lc * P:(lc + 1) * P], idf[:])
                m.then_inc(S["pt_done"], 1)

            def pv0(i, g):
                n = 4 * i + g
                pe.wait_ge(S["pt_lo"], 4 * n + 4)
                if not (isinstance(n, int) and n < 2):
                    pe.wait_ge(S["o0_used"], n - 1)
                par = (g // 2) % 2
                for lc in range(4):
                    m = mm3(bank(4 + g % 2), VH[:, par, lc * P:(lc + 1) * P], VL[:, par, lc * P:(lc + 1) * P],
                            PTH[:, g % 2, lc], PTL[:, g % 2, lc], lc == 0, lc == 3)
                m.then_inc(S["pv0_done"], 1)

            def attn0(i, first=False, last=False):
                for k in range(16):
                    if not (last and k >= 14):
                        scores0(i, k + 2)
                    turn0(i, k)
                    if k % 4 == 0 and not (first and k == 0):
                        pv0(i, k // 4 - 1)

            scores0(0, 0)
            scores0(0, 1)
            attn0(0, first=True)
            with pe.Fori(1, NT // 2 - 1) as i:
                attn0(i)
            attn0(NT // 2 - 1, last=True)
            pv0(NT // 2 - 1, 3)
            if STOP == 1:
                return

            def xt_tile(t, k, s_ready, s_lo, s_done):
                pe.wait_ge(S[s_ready], t + 1)
                if not (isinstance(t, int) and t < 2):
                    pe.wait_ge(S[s_lo], t - 1)
                for c in range(DC):
                    m = nc.tensor.transpose(bank(k % 2)[:, c * P:(c + 1) * P], xn[:, k % 2, c * P:(c + 1) * P], idf[:])
                m.then_inc(S[s_done], 1)

            def xt(s_ready, s_lo, s_done):
                for k in range(2):
                    xt_tile(k, k, s_ready, s_lo, s_done)
                with pe.Fori(1, NT // 2) as i:
                    for k in range(2):
                        xt_tile(2 * i + k, k, s_ready, s_lo, s_done)

            xt("xn_ready", "xt_lo", "xt_done")
            pe.wait_ge(S["router_in"], 48)
            pe.wait_ge(S["o0_used"], 2 * NT)
            for c in range(DC):
                m = nc.tensor.matmul(bank(4)[:, c * E:(c + 1) * E], gA[:, c * P:(c + 1) * P], gB[:], start=True, stop=True)
            m.then_inc(S["gmerge"], 1)
            pe.wait_ge(S["g_lo"], 1)
            pe.wait_ge(S["xt_lo"], NT)
            for tt in range(TT):
                if tt >= 2:
                    pe.wait_ge(S["lgT_copied"], tt - 1)
                for c in range(DC):
                    m = mm3(bank(2 + tt % 2), gH[:, c], gL[:, c], XTH[:, c, tt * 512:(tt + 1) * 512],
                            XTL[:, c, tt * 512:(tt + 1) * 512], c == 0, c == DC - 1)
                m.then_inc(S["lg_done"], 1)
            pe.wait_ge(S["lgT_copied"], TT)
            for t in range(NT):
                m = nc.tensor.transpose(bank(5)[:, t * E:(t + 1) * E], lgT[:, t * P:(t + 1) * P], idf[0:E, 0:E])
            m.then_inc(S["lgt_done"], 1)

            def merge(e, n_used):
                pe.wait_ge(S["w_in"], 64 * (e + 1))
                for c in range(WPARTS):
                    v = n_used + c - 1
                    if not (isinstance(v, int) and v <= 0):
                        pe.wait_ge(S["merged"], v)
                    lhs = lA[:, c * P:(c + 1) * P]
                    nc.tensor.matmul(bank(6 + c % 2), lhs, lB[:, 0 if c < DC else 1], start=True, stop=True) \
                        .then_inc(S["merge_done"], 1)

            def gate_up(g, tt, par, names, cols, first):
                rdy, used, done = names["w_ready"], names["u_used"], names["g_done"]
                if tt == 0:
                    pe.wait_ge(S[rdy], g + 1)
                for j, m_ in enumerate(cols):
                    if not (first and tt == 0):
                        pe.wait_ge(S[used], unit(g, tt, j, cols) - (1 if len(cols) == 2 else 0))
                    for b, off in ((j, 0), (2 + j, GROUP)):
                        for c in range(DC):
                            w = slice(off + j * P, off + j * P + m_)
                            m = mm3(PS[0:m_, b, :], WH[:, par, c, w], WL[:, par, c, w],
                                    XTH[:, c, tt * 512:(tt + 1) * 512], XTL[:, c, tt * 512:(tt + 1) * 512],
                                    c == 0, c == DC - 1)
                    m.then_inc(S[done], 1)

            def down(g, tt, par, names, cols, first):
                pe.wait_ge(S[names["h_ready"]], unit(g, tt, len(cols) - 1, cols) + 1)
                for q in range(4):
                    n = 4 * (g * TT + tt) + q
                    if not (first and tt == 0 and q < 2):
                        pe.wait_ge(S[names["y_added"]], n - 1)
                    for j, m_ in enumerate(cols):
                        m = mm3(bank(4 + q % 2), HH[0:m_, tt % 2, j, q * P:(q + 1) * P], HL[0:m_, tt % 2, j, q * P:(q + 1) * P],
                                WH[0:m_, par, DC + j], WL[0:m_, par, DC + j], j == 0, j == len(cols) - 1)
                    m.then_inc(S[names["y_done"]], 1)

            def group(g, par, names, cols, first=False, merge_next=False):
                gate_up(g, 0, par, names, cols, first)
                gate_up(g, 1, par, names, cols, False)
                down(g, 0, par, names, cols, first)
                gate_up(g, 2, par, names, cols, False)
                down(g, 1, par, names, cols, False)
                if merge_next:
                    merge(g + 1, WPARTS * (g + 1))
                gate_up(g, 3, par, names, cols, False)
                down(g, 2, par, names, cols, False)
                down(g, 3, par, names, cols, False)

            both = [P, P]
            pe.wait_ge(S["rt_done"], 1)
            merge(0, 0)
            group(0, 0, MLP0, both, first=True, merge_next=True)
            with pe.Fori(0, E // 2 - 1) as i:
                group(2 * i + 1, 1, MLP0, both, merge_next=True)
                group(2 * i + 2, 0, MLP0, both, merge_next=True)
            group(E - 1, 1, MLP0, both)
            if STOP == 2:
                return

            pe.wait_ge(S["wkv_ready"], 2)
            pe.wait_ge(S["y_added"], 4 * TT * E)

            def kv(t, par, first):
                pe.wait_ge(S["c_ready"], t + 1)
                if not first:
                    pe.wait_ge(S["kv_used"], 2 * (t - 1))
                for w in range(2):
                    for c in range(DC):
                        m = mm3(bank(2 * w + par), CH[:, par, c], CL[:, par, c], wH[:, w, c], wL[:, w, c], c == 0, c == DC - 1)
                    m.then_inc(S["kv_done"], 1)

            def kparts(t, par, first):
                pe.wait_ge(S["kp_ready"], t + 1)
                if not first:
                    pe.wait_ge(S["kt_out"], t)
                for k in range(3):
                    o = bank(4 + k).bitcast(BF16)
                    for c in range(DC):
                        m = nc.tensor.transpose(o[:, c * P:(c + 1) * P], kp[:, par, k, c * P:(c + 1) * P], idb[:])
                m.then_inc(S["kt_done"], 1)

            kv(0, 0, True)
            kv(1, 1, True)
            kparts(0, 0, True)
            with pe.Fori(1, NT // 2) as i:
                kv(2 * i, 0, False)
                kparts(2 * i - 1, 1, False)
                kv(2 * i + 1, 1, False)
                kparts(2 * i, 0, False)
            kparts(NT - 1, 1, False)
            pe.wait_ge(S["vmx_ready"], NT)
            for c in range(DC):
                m = nc.tensor.transpose(bank(7)[:, c * P:(c + 1) * P], vmx[:, c * P:(c + 1) * P], idf[:])
            m.then_inc(S["vt_done"], 1)
            pe.wait_ge(S["vdg_ready"], DC)
            for c in range(DC):
                m = nc.tensor.matmul(bank(7)[:, c * P:(c + 1) * P], ones[:], vdg[:, c], start=True, stop=True)
            m.then_inc(S["svb_done"], 1)

            pe.wait_ge(S["kv_used"], 2 * NT)
            pe.wait_ge(S["wq_ready"], 1)
            pe.wait_ge(S["kt_out"], NT)

            def qx(t, par, first):
                pe.wait_ge(S["qn_ready"], t + 1)
                if not first:
                    pe.wait_ge(S["qx_ready"], t - 1)
                for c in range(DC):
                    m = nc.tensor.transpose(bank(par)[:, c * P:(c + 1) * P], CT[:, par, c * P:(c + 1) * P], idf[:])
                m.then_inc(S["qx_done"], 1)

            def qmm(t, par, first):
                pe.wait_ge(S["qx_ready"], t + 1)
                if not first:
                    pe.wait_ge(S["q_used"], t - 1)
                for c in range(DC):
                    m = mm3(bank(2 + par), CH[:, par, c], CL[:, par, c], wH[:, 0, c], wL[:, 0, c], c == 0, c == DC - 1)
                m.then_inc(S["q_done"], 1)

            def qturn(t, par, first):
                pe.wait_ge(S["qp_ready"], t + 1)
                if not first:
                    pe.wait_ge(S["qt_out"], t)
                o = bank(4).bitcast(BF16)
                for c in range(DC):
                    m = nc.tensor.transpose(o[:, c * P:(c + 1) * P], kp[:, par, 0, c * P:(c + 1) * P], idb[:])
                m.then_inc(S["qt_done"], 1)

            qx(0, 0, True)
            qx(1, 1, True)
            qmm(0, 0, True)
            with pe.Fori(1, NT // 2) as i:
                qx(2 * i, 0, False)
                qmm(2 * i - 1, 1, False)
                qturn(2 * i - 2, 0, False)
                qx(2 * i + 1, 1, False)
                qmm(2 * i, 0, False)
                qturn(2 * i - 1, 1, False)
            qmm(NT - 1, 1, False)
            qturn(NT - 2, 0, False)
            qturn(NT - 1, 1, False)

            pe.wait_ge(S["qt_out"], NT)
            pe.wait_ge(S["v_ready"], 1)

            def scores(u, par, first):
                for half in range(2):
                    if not first:
                        pe.wait_ge(S[f"t_exp{half}"], u)
                    for b in (2 * half, 2 * half + 1):
                        m = nc.tensor.matmul(bank(b), QS[0:KROWS].rearrange("p a n -> p (a n)")[:, bass.ds((u % 32) * P, P)],
                                             KS[0:KROWS].rearrange("p a n -> p (a n)")[:, bass.ds(((u // NT) % 2) * T + b * 512, 512)],
                                             start=True, stop=True)
                    m.then_inc(S["t_half"], 1)

            def turn(u, par, first):
                for half in range(2):
                    pe.wait_ge(S[f"t_exp{half}"], u + 1)
                    if not first:
                        pe.wait_ge(S[f"pt{half}_out"], u)
                    o = bank(4 + half).bitcast(BF16)
                    for c in range(8):
                        m = nc.tensor.transpose(o[:, c * P:(c + 1) * P],
                                                ei[:, par, half * 1024 + c * P:half * 1024 + (c + 1) * P].bitcast(BF16), idb[:])
                    m.then_inc(S["e_turned"], 1)

            def pv(u, par, first):
                pe.wait_ge(S["pt0_out"], u + 1)
                pe.wait_ge(S["pt1_out"], u + 1)
                if not first:
                    pe.wait_ge(S["pv_used"], u - 1)
                for kt in range(NT):
                    m = nc.tensor.matmul(bank(6 + par)[:, 0:HD], pt[:, par, kt * P:(kt + 1) * P],
                                         VI[:, kt, bass.ds((u // 16) * HD, HD)], start=(kt == 0), stop=(kt == NT - 1))
                m.then_inc(S["pv_done"], 1)

            def pair(v, first=False):
                scores(2 * v, 0, False)
                turn(2 * v - 1, 1, False)
                pv(2 * v - 2, 0, first)
                scores(2 * v + 1, 1, False)
                turn(2 * v, 0, False)
                pv(2 * v - 1, 1, first)

            NV = NT // 2
            pe.wait_ge(S["head_in0"], 96)
            scores(0, 0, True)
            scores(1, 1, False)
            turn(0, 0, True)
            pair(1, first=True)
            with pe.Fori(2, NV) as v:
                pair(v)
            pe.wait_ge(S["head_in1"], 96)
            with pe.Fori(NV, 2 * NV) as v:
                pair(v)
            with pe.Fori(1, H1 // 2) as i:
                for par in range(2):
                    pe.wait_ge(S[f"head_in{par}"], 96 * (i + 1))
                    pe.sem_inc(S["pe_passed"], 1)
                    with pe.Fori(0, NV) as q:
                        pair(i * 2 * NV + par * NV + q)
            turn(NU - 1, 1, False)
            pv(NU - 2, 0, False)
            pv(NU - 1, 1, False)

            pe.wait_ge(S["wp_ready"], 1)
            pe.wait_ge(S["pv_used"], NU)

            def oturn(t, par, first):
                if not first:
                    pe.wait_ge(S["ao_ready"], t - 1)
                for c in range(DC):
                    m = nc.tensor.transpose(bank(par)[:, c * P:(c + 1) * P], CT[:, par, c * P:(c + 1) * P], idf[:])
                m.then_inc(S["ao_t"], 1)

            def oturn_in(t):
                pe.wait_ge(S["ao_staged"], t + 1)

            def omm(t, par, first):
                pe.wait_ge(S["ao_ready"], t + 1)
                if not first:
                    pe.wait_ge(S["o_used"], t - 1)
                for c in range(DC):
                    m = mm3(bank(2 + par), CH[:, par, c], CL[:, par, c], wH[:, 0, c], wL[:, 0, c], c == 0, c == DC - 1)
                m.then_inc(S["o_done"], 1)

            oturn_in(0)
            oturn(0, 0, True)
            oturn_in(1)
            oturn(1, 1, True)
            omm(0, 0, True)
            omm(1, 1, True)
            with pe.Fori(1, NT // 2) as i:
                for par in range(2):
                    oturn_in(2 * i + par)
                    oturn(2 * i + par, par, False)
                for par in range(2):
                    omm(2 * i + par, par, False)
            if STOP == 3:
                return
            pe.wait_ge(S["o_used"], NT)
            xt("xn1_ready", "xt1_lo", "xt1_done")
            pe.wait_ge(S["xt1_lo"], NT)
            group(0, 0, MLP1, both, first=True)
            with pe.Fori(0, (NG1 - 2) // 2) as i:
                group(2 * i + 1, 1, MLP1, both)
                group(2 * i + 2, 0, MLP1, both)
            group(NG1 - 1, 1, MLP1, [LAST])

        @block.scalar
        def _(act):
            ln_root(act, 1)

            def split_kv(i, par, first):
                act.wait_ge(S[f"kv_in{par}"], 32 * (i + 1))
                if not first:
                    act.wait_ge(S["pv0_done"], 2 * (2 * i + par) - 2)
                nc.scalar.copy(KH[:, par], Kf[:, par]).then_inc(S["kv_hi"], 1)
                nc.scalar.copy(VH[:, par], Vf[:, par]).then_inc(S["kv_hi"], 1)

            def exp0(i, k):
                n = 16 * i + k
                act.wait_ge(S["nmax_ready"], n + 1)
                if not (isinstance(n, int) and n < 2):
                    act.wait_ge(S["pt_done"], n - 1)
                nc.scalar.activation(pr[:, k % 2], bank(k % 2), ACT.Exp, bias=nmx[:, k % 2:k % 2 + 1],
                                     accum_out=psm[:, k % 2:k % 2 + 1]).then_inc(S["exp_done"], 1)

            def pt_hi(i, k):
                n, g, c = 16 * i + k, (k // 4) % 2, k % 4
                act.wait_ge(S["pt_done"], n + 1)
                gg = 4 * i + k // 4
                if c == 0 and not (isinstance(gg, int) and gg < 2):
                    act.wait_ge(S["pv0_done"], gg - 1)
                nc.scalar.copy(PTH[:, g, :, c * P:(c + 1) * P], bank(2 + k % 2).rearrange("p (l q) -> p l q", l=4)).then_inc(S["pt_hi"], 1)

            def attn0(i, first=False, last=False):
                for k in range(16):
                    exp0(i, k)
                    if not (first and k == 0):
                        pt_hi(i, k - 1)
                    if k == 6:
                        if not first:
                            split_kv(i, 1, False)
                    if k == 14 and not last:
                        split_kv(i + 1, 0, False)

            split_kv(0, 0, True)
            split_kv(0, 1, True)
            attn0(0, first=True)
            with act.Fori(1, NT // 2 - 1) as i:
                attn0(i)
            attn0(NT // 2 - 1, last=True)
            pt_hi(NT // 2 - 1, 15)
            if STOP == 1:
                return

            def xt(s_done, s_hi):
                def tile(t, k):
                    act.wait_ge(S[s_done], t + 1)
                    nc.scalar.copy(XTH[:, :, bass.ds(t * P, P)], bank(k).rearrange("p (c q) -> p c q", c=DC)).then_inc(S[s_hi], 1)
                with act.Fori(0, NT // 2) as i:
                    for k in range(2):
                        tile(2 * i + k, k)

            ln_root(act, 2)
            xt("xt_done", "xt_hi")
            act.wait_ge(S["gW_ready"], 1)
            nc.scalar.copy(gH[:], gF[:]).then_inc(S["g_hi"], 1)
            for tt in range(TT):
                act.wait_ge(S["lg_done"], tt + 1)
                nc.scalar.copy(lgT[:, tt * 512:(tt + 1) * 512], PS[0:E, 2 + tt % 2, :]).then_inc(S["lgT_copied"], 1)
            act.wait_ge(S["rt_e"], 1)
            nc.scalar.activation(rt[:, 1], rt[:, 0], ACT.Exp).then_inc(S["rexp"], 1)

            def weights_hi(g, par, s_in, v, s_free, n_free, s_out):
                act.wait_ge(S[s_in], v)
                if n_free is not None:
                    act.wait_ge(S[s_free], n_free)
                nc.scalar.copy(WH[:, par], WR[:]).then_inc(S[s_out], 1)

            def hidden(g, tt, names, cols, first):
                for j, m_ in enumerate(cols):
                    n = unit(g, tt, j, cols)
                    act.wait_ge(S[names["g_done"]], n + 1)
                    if not (first and tt == 0):
                        act.wait_ge(S[names["u_used"]], n - (1 if len(cols) == 2 else 0))
                    nc.scalar.activation(sg[0:m_, j], PS[0:m_, j, :], ACT.Silu).then_inc(S[names["silu"]], 1)
                    act.wait_ge(S[names["u_used"]], n + 1)
                    if not (first and tt < 2):
                        act.wait_ge(S[names["y_done"]], 4 * (g * TT + tt) - 4)
                    nc.scalar.copy(HH[0:m_, tt % 2, j], HF[0:m_]).then_inc(S[names["h_hi"]], 1)

            def group(g, par, names, cols, first=False, nxt=None):
                hidden(g, 0, names, cols, first)
                hidden(g, 1, names, cols, first)
                hidden(g, 2, names, cols, False)
                if nxt:
                    nxt(g + 1, 1 - par, first)
                hidden(g, 3, names, cols, False)

            def next0(g, par, first):
                weights_hi(g, par, "merged", WPARTS * (g + 1), "y_done", None if first else 4 * TT * (g - 1), "w_hi")

            def next1(g, par, first):
                weights_hi(g, par, "w1_in", 16 * (g + 1), "y1_done", None if first else 4 * TT * (g - 1), "w1_hi")

            both = [P, P]
            next0(0, 0, True)
            group(0, 0, MLP0, both, True, next0)
            with act.Fori(0, E // 2 - 1) as i:
                group(2 * i + 1, 1, MLP0, both, False, next0)
                group(2 * i + 2, 0, MLP0, both, False, next0)
            group(E - 1, 1, MLP0, both)
            if STOP == 2:
                return

            for w in range(2):
                act.wait_ge(S["wkv_in"], 16 * (w + 1))
                nc.scalar.copy(wH[:, w], wr[:]).then_inc(S["wkv_hi"], 1)

            def copy_parts(t, par, s_done, s_saved, n_saved, parts, first_bank, s_out):
                act.wait_ge(S[s_done], t + 1)
                if n_saved is not None:
                    act.wait_ge(S[s_saved], n_saved)
                for k in range(parts):
                    m = nc.scalar.copy(kts[:, par, k], bank(first_bank + k).bitcast(BF16)[:, 0:D])
                m.then_inc(S[s_out], 1)

            def c_hi(i, par, first):
                act.wait_ge(S[f"c_in{par}"], 16 * (i + 1))
                if not first:
                    act.wait_ge(S["kv_done"], 2 * (2 * i + par - 1))
                nc.scalar.copy(CH[:, par].rearrange("p c n -> p (c n)"), CT[:, par]).then_inc(S["c_hi"], 1)

            c_hi(0, 0, True)
            c_hi(0, 1, True)
            copy_parts(0, 0, "kt_done", None, None, 3, 4, "kt_out")
            c_hi(1, 0, False)
            copy_parts(1, 1, "kt_done", None, None, 3, 4, "kt_out")
            c_hi(1, 1, False)
            with act.Fori(1, NT // 2 - 1) as i:
                for par in range(2):
                    copy_parts(2 * i + par, par, "kt_done", f"kt_saved{par}", 48 * i, 3, 4, "kt_out")
                    c_hi(i + 1, par, False)
            for par in range(2):
                copy_parts(NT - 2 + par, par, "kt_done", f"kt_saved{par}", 48 * (NT // 2 - 1), 3, 4, "kt_out")

            ln_root(act, 3)
            act.wait_ge(S["wq_in"], 16)
            act.wait_ge(S["kv_done"], 2 * NT)
            nc.scalar.copy(wH[:, 0], wr[:]).then_inc(S["wq_hi"], 1)

            def x_hi(t, par, s_done, s_hi, s_free, n_free):
                act.wait_ge(S[s_done], t + 1)
                if n_free is not None:
                    act.wait_ge(S[s_free], n_free)
                nc.scalar.copy(CH[:, par].rearrange("p c n -> p (c n)"), bank(par)).then_inc(S[s_hi], 1)

            x_hi(0, 0, "qx_done", "qx_hi", None, None)
            x_hi(1, 1, "qx_done", "qx_hi", None, None)
            for par in range(2):
                x_hi(2 + par, par, "qx_done", "qx_hi", "q_done", 1 + par)
                copy_parts(par, par, "qt_done", f"kt_saved{par}", 48 * (NT // 2), 1, 4, "qt_out")
            with act.Fori(2, NT // 2) as i:
                for par in range(2):
                    x_hi(2 * i + par, par, "qx_done", "qx_hi", "q_done", 2 * i + par - 1)
                    copy_parts(2 * i - 2 + par, par, "qt_done", f"qt_saved{par}", 16 * (i - 1), 1, 4, "qt_out")
            for par in range(2):
                copy_parts(NT - 2 + par, par, "qt_done", f"qt_saved{par}", 16 * (NT // 2 - 1), 1, 4, "qt_out")

            def exps(u, par, first):
                act.wait_ge(S["t_max"], u + 1)
                if not first:
                    act.wait_ge(S["e_turned"], 2 * (u - 1))
                    act.wait_ge(S["pv_used"], u - 1)
                for half in range(2):
                    nc.scalar.activation(ei[:, par, half * 1024:(half + 1) * 1024],
                                         PS[:, 2 * half:2 * half + 2, :].rearrange("p b n -> p (b n)"), ACT.Exp,
                                         bias=tb[:, par:par + 1], scale=sqc[:, par:par + 1],
                                         accum_out=esm[:, par, half:half + 1]).then_inc(S[f"t_exp{half}"], 1)

            def turned_out(u, par, first):
                act.wait_ge(S["e_turned"], 2 * u + 1)
                if not first:
                    act.wait_ge(S["pv_done"], u - 1)
                nc.scalar.copy(pt[:, par, 0:1024], bank(4).bitcast(I16)).then_inc(S["pt0_out"], 1)

            exps(0, 0, True)
            exps(1, 1, True)
            turned_out(0, 0, True)
            exps(2, 0, False)
            turned_out(1, 1, True)
            exps(3, 1, False)
            turned_out(2, 0, False)
            with act.Fori(2, NU // 2) as v:
                for par in range(2):
                    exps(2 * v + par, par, False)
                    turned_out(2 * v + par - 1, 1 - par, False)
            turned_out(NU - 1, 1, False)

            act.wait_ge(S["wp_in"], 16)
            act.wait_ge(S["q_done"], NT)
            nc.scalar.copy(wH[:, 0], wr[:]).then_inc(S["wp_hi"], 1)
            x_hi(0, 0, "ao_t", "ao_hi", None, None)
            x_hi(1, 1, "ao_t", "ao_hi", None, None)
            with act.Fori(1, NT // 2) as i:
                for par in range(2):
                    x_hi(2 * i + par, par, "ao_t", "ao_hi", "o_done", 2 * i + par - 1)
            if STOP == 3:
                return
            ln_root(act, 4)
            xt("xt1_done", "xt1_hi")
            next1(0, 0, True)
            group(0, 0, MLP1, both, True, next1)
            with act.Fori(0, (NG1 - 2) // 2) as i:
                group(2 * i + 1, 1, MLP1, both, False, next1)
                group(2 * i + 2, 0, MLP1, both, False, next1)
            group(NG1 - 1, 1, MLP1, [LAST])

        @block.vector
        def _(dve):
            ch = Chain(dve, S["dve_own"])
            total = [0]

            def straight():
                ch.enter(total[0])

            def ended(loops=1):
                total[0] += loops * ch.n

            straight()
            dve.wait_ge(S["x_in"], 16 * 4)
            for t in range(NT):
                m = nc.vector.bn_stats(st[:, t], X[:, t])
            ch.link(m)
            ln_finish(dve, ch)
            ln_invert(dve, ch, 1, scale=1.0 / math.sqrt(HROWS))

            def prep(i, par, first):
                t = 2 * i + par
                if not first:
                    dve.wait_ge(S["s_ready"], 8 * (t - 1))
                    dve.wait_ge(S["pv0_done"], 2 * (t - 1))
                if not (isinstance(t, int) and t == 0):
                    dve.wait_ge(S["q_split"], t)
                ch.link(nc.vector.tensor_scalar(Qf[:], X[:, bass.ds(t, 1)].rearrange("p o d -> p (o d)"),
                                                mu[:, bass.ds(t, 1)], rstd[:, bass.ds(t, 1)], ALU.subtract, ALU.mult))
                ch.link(nc.vector.tensor_copy(QH[:, par], Qf[:]))
                nc.vector.tensor_tensor(QL[:, par], Qf[:], QH[:, par].bitcast(F32), ALU.subtract).then_inc(S["q_split"], 1)
                dve.wait_ge(S["kv_hi"], 2 * (t + 1))
                nc.vector.tensor_tensor(KL[:, par], Kf[:, par], KH[:, par].bitcast(F32), ALU.subtract)
                nc.vector.tensor_tensor(VL[:, par], Vf[:, par], VH[:, par].bitcast(F32), ALU.subtract).then_inc(S["kv_split"], 1)

            def rowmax(i, k):
                n = 16 * i + k
                dve.wait_ge(S["s_ready"], n + 1)
                nc.vector.tensor_reduce(nmx[:, k % 2:k % 2 + 1], bank(k % 2), AX.X, ALU.max, negate=True).then_inc(S["nmax_ready"], 1)

            def norm(i, k):
                n = 16 * i + k
                dve.wait_ge(S["exp_done"], n + 1)
                c = slice(k % 2, k % 2 + 1)
                ch.link(nc.vector.reciprocal(rsm[:, c], psm[:, c]))
                nc.vector.tensor_scalar(pr[:, k % 2], pr[:, k % 2], rsm[:, c], None, ALU.mult).then_inc(S["p_ready"], 1)

            def pt_lo(i, k):
                n, g, c = 16 * i + k, (k // 4) % 2, k % 4
                dve.wait_ge(S["pt_hi"], n + 1)
                o = (slice(None), g, slice(None), slice(c * P, (c + 1) * P))
                nc.vector.tensor_tensor(PTL[o], bank(2 + k % 2).rearrange("p (l q) -> p l q", l=4), PTH[o].bitcast(F32),
                                        ALU.subtract).then_inc(S["pt_lo"], 1)

            def add0(i, g):
                t, rows = 2 * i + g // 2, slice(HROWS * (g % 2), HROWS * (g % 2 + 1))
                n = 4 * i + g
                dve.wait_ge(S["pv0_done"], n + 1)
                x = X[rows, bass.ds(t, 1)].rearrange("p o d -> p (o d)")
                m = nc.vector.scalar_tensor_tensor(out=x, in0=PS[rows, 4 + g % 2, :], scalar=gam[rows], in1=x,
                                                   op0=ALU.mult, op1=ALU.add)
                m.then_inc(S["o0_used"], 1)
                if g % 2:
                    dve.wait_ge(S["o0_used"], n + 1)
                    nc.vector.bn_stats(st[:, bass.ds(t, 1)].rearrange("p o s -> p (o s)"),
                                       X[:, bass.ds(t, 1)].rearrange("p o d -> p (o d)")).then_inc(S["stats0"], 1)

            def attn0(i, first=False, last=False):
                for k in range(16):
                    if not (last and k == 15):
                        rowmax(i, k + 1)
                    norm(i, k)
                    if not (first and k == 0):
                        pt_lo(i, k - 1)
                    if k % 4 == 1 and not (first and k == 1):
                        add0(i, k // 4 - 1)
                    if k == 6 and not first:
                        prep(i, 1, False)
                    if k == 14 and not last:
                        prep(i + 1, 0, False)

            prep(0, 0, True)
            prep(0, 1, True)
            dve.wait_ge(S["gam_in"], 16)
            rowmax(0, 0)
            attn0(0, first=True)
            ended()
            per = 16 + 4
            with dve.Fori(1, NT // 2 - 1) as i:
                ch.enter(total[0] + per * (i - 1))
                attn0(i)
                assert ch.n == per
            total[0] += per * (NT // 2 - 2)
            straight()
            attn0(NT // 2 - 1, last=True)
            pt_lo(NT // 2 - 1, 15)
            add0(NT // 2 - 1, 3)
            if STOP == 1:
                return

            def flat(x, t):
                return x[:, bass.ds(t, 1)].rearrange("p o d -> p (o d)")

            dve.wait_ge(S["stats0"], NT)
            ln_finish(dve, ch)
            ln_invert(dve, ch, 2)
            ended()

            def xt(s_ready, s_done, s_hi, s_lo):
                def tile(t, k, first):
                    if not first:
                        dve.wait_ge(S[s_done], t - 1)
                    nc.vector.tensor_scalar(xn[:, k], flat(X, t), mu[:, bass.ds(t, 1)], rstd[:, bass.ds(t, 1)],
                                            ALU.subtract, ALU.mult).then_inc(S[s_ready], 1)

                def low(t, k):
                    dve.wait_ge(S[s_hi], t + 1)
                    nc.vector.tensor_tensor(XTL[:, :, bass.ds(t * P, P)], bank(k).rearrange("p (c q) -> p c q", c=DC),
                                            XTH[:, :, bass.ds(t * P, P)].bitcast(F32), ALU.subtract).then_inc(S[s_lo], 1)
                tile(0, 0, True)
                tile(1, 1, True)
                with dve.Fori(0, NT // 2 - 1) as i:
                    for k in range(2):
                        low(2 * i + k, k)
                        tile(2 * i + k + 2, k, False)
                for k in range(2):
                    low(NT - 2 + k, k)

            xt("xn_ready", "xt_done", "xt_hi", "xt_lo")
            straight()
            dve.wait_ge(S["router_in"], 48)
            ch.link(nc.vector.memset(gF[:], 0.0))
            dve.wait_ge(S["gmerge"], 1)
            nc.vector.scalar_tensor_tensor(out=gF[:, :, 0:E], in0=bank(4)[:, 0:DC * E].rearrange("p (c e) -> p c e", c=DC),
                                           scalar=2.0, in1=gW[:], op0=ALU.mult, op1=ALU.add).then_inc(S["gW_ready"], 1)
            dve.wait_ge(S["g_hi"], 1)
            nc.vector.tensor_tensor(gL[:], gF[:], gH[:].bitcast(F32), ALU.subtract).then_inc(S["g_lo"], 1)
            for e in range(E):
                m = nc.vector.memset(rev[:, :, e:e + 1], float(E - e))
            ch.link(m)
            dve.wait_ge(S["lgt_done"], 1)
            ch.link(nc.vector.tensor_copy(rt[:, 2], bank(5)[:, 0:NT * E].rearrange("p (t e) -> p t e", e=E)))

            def wide(x):
                return x.rearrange("p (t o) -> p t o", o=1).broadcast_to([P, NT, E])

            ch.link(nc.vector.tensor_reduce(rm[:, 0], rt[:, 2], AX.X, ALU.max))
            nc.vector.tensor_tensor(rt[:, 0], rt[:, 2], wide(rm[:, 0]), ALU.subtract).then_inc(S["rt_e"], 1)
            dve.wait_ge(S["rexp"], 1)

            def largest(src, mask, m, k):
                ch.link(nc.vector.tensor_reduce(rm[:, m], src, AX.X, ALU.max))
                ch.link(nc.vector.tensor_tensor(mask, src, wide(rm[:, m]), ALU.is_equal))
                ch.link(nc.vector.tensor_tensor(mask, mask, rev[:], ALU.mult))
                ch.link(nc.vector.tensor_reduce(rm[:, k], mask, AX.X, ALU.max))
                ch.link(nc.vector.tensor_tensor(mask, mask, wide(rm[:, k]), ALU.is_equal))

            largest(rt[:, 1], rt[:, 3], 0, 1)
            ch.link(nc.vector.scalar_tensor_tensor(out=rt[:, 4], in0=rt[:, 3], scalar=-2.0, in1=rt[:, 1], op0=ALU.mult, op1=ALU.add))
            largest(rt[:, 4], rt[:, 5], 2, 3)
            ch.link(nc.vector.tensor_tensor(rm[:, 1], rm[:, 0], rm[:, 2], ALU.add))
            ch.link(nc.vector.reciprocal(rm[:, 3], rm[:, 1]))
            ch.link(nc.vector.tensor_tensor(rt[:, 3], rt[:, 3], rt[:, 5], ALU.add))
            ch.link(nc.vector.tensor_tensor(rt[:, 4], rt[:, 3], rt[:, 1], ALU.mult))
            nc.vector.tensor_tensor(W8[:], rt[:, 4], wide(rm[:, 3]), ALU.mult).then_inc(S["rt_done"], 1)
            dve.wait_ge(S["rt_done"], 1)
            ended()

            def merged0(g, par, first):
                for c in range(WPARTS):
                    v = WPARTS * g + c + 1
                    dve.wait_ge(S["merge_done"], v)
                    nc.vector.scalar_tensor_tensor(out=WR[:, c], in0=bank(6 + c % 2), scalar=2.0, in1=WR[:, c],
                                                   op0=ALU.mult, op1=ALU.add).then_inc(S["merged"], 1)
                low_weights(g, par, "w_hi", "w_ready")

            def low_weights(g, par, s_hi, s_out):
                dve.wait_ge(S[s_hi], g + 1)
                nc.vector.tensor_tensor(WL[:, par], WR[:], WH[:, par].bitcast(F32), ALU.subtract).then_inc(S[s_out], 1)

            def merged1(g, par, first):
                low_weights(g, par, "w1_hi", "w1_ready")

            def hidden(g, tt, names, cols, first):
                for j, m_ in enumerate(cols):
                    n = unit(g, tt, j, cols)
                    dve.wait_ge(S[names["silu"]], n + 1)
                    if not (first and tt == 0 and j == 0):
                        dve.wait_ge(S[names["h_ready"]], n)
                    nc.vector.tensor_tensor(HF[0:m_], sg[0:m_, j], PS[0:m_, 2 + j, :], ALU.mult).then_inc(S[names["u_used"]], 1)
                    dve.wait_ge(S[names["h_hi"]], n + 1)
                    nc.vector.tensor_tensor(HL[0:m_, tt % 2, j], HF[0:m_], HH[0:m_, tt % 2, j].bitcast(F32),
                                            ALU.subtract).then_inc(S[names["h_ready"]], 1)

            def add(g, tt, names, weighted):
                for q in range(4):
                    n, t = 4 * (g * TT + tt) + q, 4 * tt + q
                    dve.wait_ge(S[names["y_done"]], n + 1)
                    if weighted:
                        w = W8[:, t, bass.ds(g, 1)]
                        m = nc.vector.scalar_tensor_tensor(out=X[:, t], in0=bank(4 + q % 2), scalar=w, in1=X[:, t],
                                                           op0=ALU.mult, op1=ALU.add)
                    else:
                        m = nc.vector.tensor_tensor(X[:, t], bank(4 + q % 2), X[:, t], ALU.add)
                    m.then_inc(S[names["y_added"]], 1)

            def group(g, par, names, cols, first=False, nxt=None, weighted=False):
                hidden(g, 0, names, cols, first)
                hidden(g, 1, names, cols, first)
                add(g, 0, names, weighted)
                hidden(g, 2, names, cols, False)
                add(g, 1, names, weighted)
                if nxt:
                    nxt(g + 1, 1 - par, first)
                hidden(g, 3, names, cols, False)
                add(g, 2, names, weighted)
                add(g, 3, names, weighted)

            both = [P, P]
            merged0(0, 0, True)
            group(0, 0, MLP0, both, True, merged0, True)
            with dve.Fori(0, E // 2 - 1) as i:
                group(2 * i + 1, 1, MLP0, both, False, merged0, True)
                group(2 * i + 2, 0, MLP0, both, False, merged0, True)
            group(E - 1, 1, MLP0, both, False, None, True)

            if STOP == 2:
                return

            def stats(added, n):
                straight()
                dve.wait_ge(S[added], n)
                for t in range(NT):
                    m = nc.vector.bn_stats(st[:, t], X[:, t])
                ch.link(m)
                ln_finish(dve, ch)

            stats("y_added", 4 * TT * E)
            ended()
            for w in range(2):
                dve.wait_ge(S["wkv_hi"], w + 1)
                nc.vector.tensor_tensor(wL[:, w], wr[:], wH[:, w].bitcast(F32), ALU.subtract).then_inc(S["wkv_ready"], 1)
            dve.wait_ge(S["bias_in"], 48)

            def c_lo(t, par, first):
                dve.wait_ge(S["c_hi"], t + 1)
                nc.vector.tensor_tensor(CL[:, par].rearrange("p c n -> p (c n)"), CT[:, par],
                                        CH[:, par].rearrange("p c n -> p (c n)").bitcast(F32), ALU.subtract).then_inc(S["c_ready"], 1)

            def heads(x):
                return x.rearrange("p (h d) -> p h d", d=HD)

            def by_head(x):
                return x.rearrange("p (h o) -> p h o", o=1).broadcast_to([P, H1, HD])

            def quantise(src, scale, s_dst):
                ch.link(nc.vector.tensor_reduce(ksc[:, 0], heads(src), AX.X, ALU.max, apply_absolute_value=True))
                ch.link(nc.vector.tensor_scalar(s_dst, ksc[:, 0], scale / QMAX, SMIN, ALU.mult, ALU.max))
                ch.link(nc.vector.reciprocal(ksc[:, 1], s_dst))
                if scale != 1.0:
                    ch.link(nc.vector.tensor_scalar(ksc[:, 1], ksc[:, 1], scale, None, ALU.mult))
                ch.link(nc.vector.tensor_tensor(heads(ki[:]), heads(src), by_head(ksc[:, 1]), ALU.mult))

            def kv(t, par, first, first_tile):
                dve.wait_ge(S["kv_done"], 2 * t + 1)
                nc.vector.tensor_tensor(kf[:], bank(par), bkv[:, 0:D], ALU.add).then_inc(S["kv_used"], 1)
                dve.wait_ge(S["kv_used"], 2 * t + 1)
                quantise(kf[:], 1.0, ksc[:, 2])
                ch.link(nc.vector.tensor_tensor(heads(kd[:]), heads(ki[:]), by_head(ksc[:, 2]), ALU.mult))
                if not first:
                    dve.wait_ge(S["kt_done"], t - 1)
                ch.link(nc.vector.tensor_copy(kp[:, par, 0], kd[:]))
                ch.link(nc.vector.tensor_tensor(kf[:], kd[:], kp[:, par, 0], ALU.subtract))
                ch.link(nc.vector.tensor_copy(kp[:, par, 1], kf[:]))
                nc.vector.tensor_tensor(kp[:, par, 2], kf[:], kp[:, par, 1], ALU.subtract).then_inc(S["kp_ready"], 1)
                dve.wait_ge(S["kp_ready"], t + 1)
                dve.wait_ge(S["kv_done"], 2 * t + 2)
                nc.vector.tensor_tensor(flat(VF, t), bank(2 + par), bkv[:, D:2 * D], ALU.add).then_inc(S["kv_used"], 1)
                dve.wait_ge(S["kv_used"], 2 * t + 2)
                size = vmx if first_tile else kd
                m = nc.vector.scalar_tensor_tensor(out=size[:], in0=flat(VF, t), scalar=-1.0, in1=flat(VF, t),
                                                   op0=ALU.mult, op1=ALU.max)
                if not first_tile:
                    ch.link(m)
                    m = nc.vector.tensor_tensor(vmx[:], vmx[:], kd[:], ALU.max)
                m.then_inc(S["vmx_ready"], 1)
                dve.wait_ge(S["vmx_ready"], t + 1)

            straight()
            c_lo(0, 0, True)
            c_lo(1, 1, True)
            kv(0, 0, True, True)
            c_lo(2, 0, False)
            kv(1, 1, True, False)
            c_lo(3, 1, False)
            ended()
            def kv_pair(i, more):
                for par in range(2):
                    kv(2 * i + par, par, False, False)
                    if more:
                        c_lo(2 * i + par + 2, par, False)
            per = 18
            with dve.Fori(1, NT // 2 - 1) as i:
                ch.enter(total[0] + per * (i - 1))
                kv_pair(i, True)
                assert ch.n == per, ch.n
            total[0] += per * (NT // 2 - 2)
            straight()
            kv_pair(NT // 2 - 1, False)
            dve.wait_ge(S["vt_done"], 1)
            ch.link(nc.vector.tensor_reduce(vsc[:, 0], bank(7).rearrange("p (c n) -> p c n", c=DC), AX.X, ALU.max,
                                            apply_absolute_value=True))
            ch.link(nc.vector.tensor_scalar(vsc[:, 1], vsc[:, 0], 1.0 / QMAX, SMIN, ALU.mult, ALU.max))
            for c in range(DC):
                nc.vector.tensor_scalar(vdg[:, c], idf[:], vsc[:, 1, c:c + 1], None, ALU.mult).then_inc(S["vdg_ready"], 1)
            dve.wait_ge(S["svb_done"], 1)
            ch.link(nc.vector.tensor_copy(svb[:], bank(7)))
            ch.link(nc.vector.reciprocal(rvb[:], svb[:]))
            for t in range(NT):
                m = nc.vector.tensor_tensor(vii[:, t], VF[:, t], rvb[:], ALU.mult)
            ch.link(m)
            nc.vector.tensor_copy(VI[:], vii[:]).then_inc(S["v_ready"], 1)
            ended()

            straight()
            ln_invert(dve, ch, 3)
            ended()
            dve.wait_ge(S["wq_hi"], 1)
            nc.vector.tensor_tensor(wL[:, 0], wr[:], wH[:, 0].bitcast(F32), ALU.subtract).then_inc(S["wq_ready"], 1)

            def qn(t, par, first):
                if not first:
                    dve.wait_ge(S["qx_done"], t - 1)
                nc.vector.tensor_scalar(CT[:, par], flat(X, t), mu[:, bass.ds(t, 1)], rstd[:, bass.ds(t, 1)],
                                        ALU.subtract, ALU.mult).then_inc(S["qn_ready"], 1)

            def x_lo(t, par, s_hi, s_out):
                dve.wait_ge(S[s_hi], t + 1)
                nc.vector.tensor_tensor(CL[:, par].rearrange("p c n -> p (c n)"), bank(par),
                                        CH[:, par].rearrange("p c n -> p (c n)").bitcast(F32), ALU.subtract).then_inc(S[s_out], 1)

            def q(t, par, first):
                dve.wait_ge(S["q_done"], t + 1)
                nc.vector.tensor_tensor(kf[:], bank(2 + par), bq[:], ALU.add).then_inc(S["q_used"], 1)
                dve.wait_ge(S["q_used"], t + 1)
                quantise(kf[:], QSCALE, ksc[:, 2])
                nc.vector.tensor_copy(flat(SQ, t), ksc[:, 2])
                if not first:
                    dve.wait_ge(S["qt_done"], t - 1)
                nc.vector.tensor_copy(kp[:, par, 0], ki[:]).then_inc(S["qp_ready"], 1)
                dve.wait_ge(S["qp_ready"], t + 1)

            straight()
            qn(0, 0, True)
            qn(1, 1, True)
            x_lo(0, 0, "qx_hi", "qx_ready")
            x_lo(1, 1, "qx_hi", "qx_ready")
            qn(2, 0, False)
            q(0, 0, True)
            qn(3, 1, False)
            q(1, 1, True)
            ended()

            def q_pair(i, more):
                for par in range(2):
                    x_lo(2 * i + par, par, "qx_hi", "qx_ready")
                    if more:
                        qn(2 * i + 2 + par, par, False)
                for par in range(2):
                    q(2 * i + par, par, False)
            per = 10
            with dve.Fori(1, NT // 2 - 1) as i:
                ch.enter(total[0] + per * (i - 1))
                q_pair(i, True)
                assert ch.n == per, ch.n
            total[0] += per * (NT // 2 - 2)
            straight()
            q_pair(NT // 2 - 1, False)
            ended()

            def tmax(u, par, first):
                c = slice(par, par + 1)
                if not first:
                    dve.wait_ge(S["t_exp1"], u - 1)
                nc.vector.tensor_copy(sqc[:, c], SQ[:, bass.ds(u % NT, 1), bass.ds(u // NT, 1)].rearrange("p a b -> p (a b)"))
                for half in range(2):
                    dve.wait_ge(S["t_half"], 2 * u + half + 1)
                    m = nc.vector.tensor_reduce(tm[:, par, half:half + 1], PS[:, 2 * half:2 * half + 2, :].rearrange("p b n -> p (b n)"),
                                                AX.X, ALU.max, negate=True)
                ch.link(m)
                ch.link(nc.vector.tensor_scalar(tmn[:, c], tm[:, par, 0:1], tm[:, par, 1:2], None, ALU.min))
                nc.vector.tensor_scalar(tb[:, c], tmn[:, c], sqc[:, c], math.log(PMAX), ALU.mult, ALU.add).then_inc(S["t_max"], 1)

            def turned_out(u, par, first):
                dve.wait_ge(S["e_turned"], 2 * u + 2)
                if not first:
                    dve.wait_ge(S["pv_done"], u - 1)
                nc.vector.tensor_copy(pt[:, par, 1024:2048], bank(5).bitcast(I16)).then_inc(S["pt1_out"], 1)

            def result(u, par):
                c = slice(par, par + 1)
                dve.wait_ge(S["t_exp1"], u + 1)
                ch.link(nc.vector.tensor_scalar(est[:, c], esm[:, par, 0:1], esm[:, par, 1:2], None, ALU.add))
                ch.link(nc.vector.reciprocal(esr[:, c], est[:, c]))
                dve.wait_ge(S["pv_done"], u + 1)
                h = bass.ds((u // NT) * HD, HD)
                nc.vector.scalar_tensor_tensor(out=AO[:, bass.ds(u % NT, 1), h].rearrange("p a b -> p (a b)"),
                                               in0=bank(6 + par)[:, 0:HD], scalar=esr[:, c], in1=svb[:, h],
                                               op0=ALU.mult, op1=ALU.mult).then_inc(S["pv_used"], 1)

            dve.wait_ge(S["v_ready"], 1)
            straight()
            tmax(0, 0, True)
            tmax(1, 1, True)
            turned_out(0, 0, True)
            tmax(2, 0, False)
            turned_out(1, 1, True)
            result(0, 0)
            tmax(3, 1, False)
            turned_out(2, 0, False)
            result(1, 1)
            ended()
            per = 8
            with dve.Fori(2, NU // 2) as v:
                ch.enter(total[0] + per * (v - 2))
                for par in range(2):
                    u = 2 * v + par
                    tmax(u, par, False)
                    turned_out(u - 1, 1 - par, False)
                    result(u - 2, par)
                assert ch.n == per, ch.n
            total[0] += per * (NU // 2 - 2)
            straight()
            turned_out(NU - 1, 1, False)
            result(NU - 2, 0)
            result(NU - 1, 1)

            dve.wait_ge(S["wp_hi"], 1)
            nc.vector.tensor_tensor(wL[:, 0], wr[:], wH[:, 0].bitcast(F32), ALU.subtract).then_inc(S["wp_ready"], 1)
            dve.wait_ge(S["pv_used"], NU)
            ended()

            def stage(t, par, first):
                if not first:
                    dve.wait_ge(S["ao_t"], t - 1)
                nc.vector.tensor_copy(CT[:, par], flat(AO, t)).then_inc(S["ao_staged"], 1)

            def project(t, par):
                dve.wait_ge(S["o_done"], t + 1)
                ch.link(nc.vector.tensor_tensor(kf[:], bank(2 + par), bp[:], ALU.add))
                nc.vector.tensor_tensor(flat(X, t), kf[:], flat(X, t), ALU.add).then_inc(S["o_used"], 1)
                dve.wait_ge(S["o_used"], t + 1)

            straight()
            stage(0, 0, True)
            stage(1, 1, True)
            x_lo(0, 0, "ao_hi", "ao_ready")
            x_lo(1, 1, "ao_hi", "ao_ready")
            project(0, 0)
            project(1, 1)
            ended()
            with dve.Fori(1, NT // 2) as i:
                ch.enter(total[0] + 2 * (i - 1))
                for par in range(2):
                    stage(2 * i + par, par, False)
                for par in range(2):
                    x_lo(2 * i + par, par, "ao_hi", "ao_ready")
                for par in range(2):
                    project(2 * i + par, par)
            total[0] += 2 * (NT // 2 - 1)
            if STOP == 3:
                return

            stats("o_used", NT)
            ln_invert(dve, ch, 4)
            ended()
            xt("xn1_ready", "xt1_done", "xt1_hi", "xt1_lo")
            merged1(0, 0, True)
            group(0, 0, MLP1, both, True, merged1)
            with dve.Fori(0, (NG1 - 2) // 2) as i:
                group(2 * i + 1, 1, MLP1, both, False, merged1)
                group(2 * i + 2, 0, MLP1, both, False, merged1)
            group(NG1 - 1, 1, MLP1, [LAST])


_INS = dict(x=None)


def kernel(**inputs):
    import numpy as np
    import concourse.bacc as bacc
    from concourse.bass_utils import run_bass_kernel_spmd

    v = {k: np.asarray(x) for k, x in inputs.items()}
    idx = np.zeros((NG1, P, WPARTS, D), np.int32)
    for half, name in ((0, "L1_ffn_gate_idx"), (GROUP, "L1_ffn_up_idx")):
        t = np.zeros((NG1 * GROUP, D), np.int32)
        t[:INTER] = v[name]
        idx[:, :, 0:DC, half:half + GROUP] = t.reshape(NG1, GROUP, DC, P).transpose(0, 3, 2, 1)
    t = np.zeros((NG1 * GROUP, D), np.int32)
    t[:INTER] = v["L1_ffn_down_idx"].T
    idx[:, :, DC:] = t.reshape(NG1, GROUP // P, P, D).transpose(0, 2, 1, 3)
    laid = {
        "x": v["x"].reshape(NT, P, D),
        "ctx": v["ctx_2048"].reshape(NT, P, D),
        "ctxT": v["ctx_2048"].reshape(NT, P, DC, P).transpose(0, 3, 2, 1).reshape(NT, P, D),
        "gamma": v["L0_xattn_gamma"].reshape(1),
        "gWT": v["L0_ffn_gate_weight"].T,
        "gA": v["L0_ffn_gate_lora_A"],
        "gBT": v["L0_ffn_gate_lora_B"].T,
        "gup": v["L0_ffn_gate_up_proj"],
        "down": v["L0_ffn_down_proj"],
        "lA": np.concatenate([v["L0_ffn_gup_lora_A"], v["L0_ffn_down_lora_A"]], axis=2),
        "lB": np.stack([v["L0_ffn_gup_lora_B"].transpose(0, 2, 1), v["L0_ffn_down_lora_B"].transpose(0, 2, 1)], axis=2),
        "Wq": v["L1_xattn_Wq"], "bq": v["L1_xattn_bq"],
        "Wkv": v["L1_xattn_Wkv"], "bkv": v["L1_xattn_bkv"],
        "Wp": v["L1_xattn_Wp"], "bp": v["L1_xattn_bp"],
        "lut": v["L1_ffn_lut"],
        "idx": idx,
    }
    nc = bacc.Bacc("TRN2", target_bir_lowering=False, num_devices=1)
    arrays, aps = {}, {}
    for name, x in laid.items():
        x = np.ascontiguousarray(x)
        arrays[f"in_{name}"] = x
        aps[name] = nc.dram_tensor(f"in_{name}", x.shape, mybir.dt.from_np(x.dtype), kind="ExternalInput").ap()
    out = nc.dram_tensor("out", (NT, P, D), F32, kind="ExternalOutput").ap()
    build(nc, aps, out)
    r = run_bass_kernel_spmd(nc, [arrays], core_ids=[0])
    return r.results[0]["out"].reshape(4, 512, D)
```

```python
import math
from contextlib import ExitStack

import concourse.bass as bass
from concourse import mybir

F32 = mybir.dt.float32
F32R = mybir.dt.float32r
BF16 = mybir.dt.bfloat16
I16 = mybir.dt.int16
I32 = mybir.dt.int32
ALU = mybir.AluOpType
ACT = mybir.ActivationFunctionType
AX = mybir.AxisListType

P = 128
D = 512
T = 2048
NT = T // P
DC = D // P
TT = T // 512
EPS = 1e-5

H0 = 8
HROWS = 512 // H0
E = 8
R = 16
INTER = 1376
GROUP = 256
NG1 = -(-INTER // GROUP)
LAST = INTER - (NG1 - 1) * GROUP
WPARTS = DC + GROUP // P
LUT = 16

H1 = 16
HD = D // H1
QSCALE = 1.0 / math.sqrt(HD)
QMAX = 127.0
PMAX = 255.0
SMIN = 1e-8
KROWS = 3 * HD


class Chain:

    def __init__(self, eng, sem, passed=None):
        self.eng, self.sem, self.base, self.n, self.passed = eng, sem, 0, 0, passed

    def enter(self, base):
        self.base, self.n = base, 0

    def link(self, ins):
        self.n += 1
        ins.then_inc(self.sem, 1)
        self.eng.wait_ge(self.sem, self.base + self.n)
        if self.passed:
            self.eng.sem_inc(self.passed, 1)


STOPAT = 9


def build(nc, a, out, STOP=None):
    STOP = STOPAT if STOP is None else STOP
    with ExitStack() as ctx:
        def sem(name):
            return ctx.enter_context(nc.semaphore(name))

        def dram(name, shape, dt):
            return nc.dram_tensor(name, shape, dt, kind="Internal").ap()

        def sb(stack, name, shape, dt):
            return stack.enter_context(nc.sbuf_tensor(name, shape, dt))

        X = sb(ctx, "X", [P, NT, D], F32)
        idf = sb(ctx, "idf", [P, P], F32)
        idb = sb(ctx, "idb", [P, P], BF16)
        ones = sb(ctx, "ones", [P, P], F32)
        gam = sb(ctx, "gam", [P, 1], F32)
        st = sb(ctx, "st", [P, NT, 6], F32)
        mu = sb(ctx, "mu", [P, NT], F32)
        rstd = sb(ctx, "rstd", [P, NT], F32)
        lnt = sb(ctx, "lnt", [P, 4, NT], F32)
        W8 = sb(ctx, "W8", [P, NT, E], F32)
        lut = sb(ctx, "lut", [P, LUT], F32)
        ix = sb(ctx, "ix", [P, D], I32)
        pick = sb(ctx, "pick", [P, 2, D], F32)
        dec = sb(ctx, "dec", [P, D], F32)

        PS = ctx.enter_context(nc.psum_tensor("PS", [P, 8, 512], F32))

        with ExitStack() as s:
            Kf = sb(s, "Kf", [P, 2, D], F32)
            Vf = sb(s, "Vf", [P, 2, D], F32)
            Qf = sb(s, "Qf", [P, D], F32)
            QH = sb(s, "QH", [P, 2, D], F32R)
            QL = sb(s, "QL", [P, 2, D], F32R)
            KH = sb(s, "KH", [P, 2, D], F32R)
            KL = sb(s, "KL", [P, 2, D], F32R)
            VH = sb(s, "VH", [P, 2, D], F32R)
            VL = sb(s, "VL", [P, 2, D], F32R)
            pr = sb(s, "pr", [P, 2, D], F32)
            nmx = sb(s, "nmx", [P, 2], F32)
            psm = sb(s, "psm", [P, 2], F32)
            rsm = sb(s, "rsm", [P, 2], F32)
            PTH = sb(s, "PTH", [P, 2, 4, D], F32R)
            PTL = sb(s, "PTL", [P, 2, 4, D], F32R)
        with ExitStack() as s:
            XTH = sb(s, "XTH", [P, DC, T], F32R)
            XTL = sb(s, "XTL", [P, DC, T], F32R)
            WR = sb(s, "WR", [P, WPARTS, D], F32)
            WH = sb(s, "WH", [P, 2, WPARTS, D], F32R)
            WL = sb(s, "WL", [P, 2, WPARTS, D], F32R)
            xn = sb(s, "xn", [P, 2, D], F32)
            sg = sb(s, "sg", [P, 2, 512], F32)
            HF = sb(s, "HF", [P, 512], F32)
            HH = sb(s, "HH", [P, 2, 2, 512], F32R)
            HL = sb(s, "HL", [P, 2, 2, 512], F32R)
            lA = sb(s, "lA", [R, D + GROUP], F32)
            lB = sb(s, "lB", [R, 2, D], F32)
        with ExitStack() as s:
            s.enter_context(nc.sbuf_tensor("below_WR", [P, 2 * DC * T], F32))
            gA = sb(s, "gA", [R, D], F32)
            gB = sb(s, "gB", [R, E], F32)
            gW = sb(s, "gW", [P, DC, E], F32)
            gH = sb(s, "gH", [P, DC, P], F32R)
            gL = sb(s, "gL", [P, DC, P], F32R)
            gF = sb(s, "gF", [P, DC, P], F32)
            lgT = sb(s, "lgT", [E, T], F32)
            rt = sb(s, "rt", [P, 6, NT, E], F32)
            rm = sb(s, "rm", [P, 4, NT], F32)
            rev = sb(s, "rev", [P, NT, E], F32)
        with ExitStack() as s:
            VI = sb(s, "VI", [P, H1, NT, HD], BF16)
            SQ = sb(s, "SQ", [P, H1, NT], F32)
            svb = sb(s, "svb", [P, D], F32)
            AO = sb(s, "AO", [P, H1, NT, HD], F32)
            bq = sb(s, "bq", [P, D], F32)
            bkv = sb(s, "bkv", [P, 2 * D], F32)
            bp = sb(s, "bp", [P, D], F32)
            with ExitStack() as s2:
                wr = sb(s2, "wr", [P, DC, D], F32)
                wH = sb(s2, "wH", [P, 2, DC, D], F32R)
                wL = sb(s2, "wL", [P, 2, DC, D], F32R)
                CT = sb(s2, "CT", [P, 2, D], F32)
                CH = sb(s2, "CH", [P, 2, DC, P], F32R)
                CL = sb(s2, "CL", [P, 2, DC, P], F32R)
                kf = sb(s2, "kf", [P, D], F32)
                ki = sb(s2, "ki", [P, D], I16)
                kd = sb(s2, "kd", [P, D], F32)
                kp = sb(s2, "kp", [P, 2, 3, D], BF16)
                ksc = sb(s2, "ksc", [P, 4, H1], F32)
                kts = sb(s2, "kts", [P, 2, 3, D], BF16)
                vmx = sb(s2, "vmx", [P, D], F32)
                vdg = sb(s2, "vdg", [P, DC, P], F32)
                vsc = sb(s2, "vsc", [P, 2, DC], F32)
                rvb = sb(s2, "rvb", [P, D], F32)
                vii = sb(s2, "vii", [P, 2, D], I16)
            with ExitStack() as s2:
                KS = sb(s2, "KS", [P, 2, T], BF16)
                QS = sb(s2, "QS", [P, 2, T], BF16)
                ei = sb(s2, "ei", [P, 3, T], I16)
                pt = sb(s2, "pt", [P, 3, T], BF16)
                VK = sb(s2, "VK", [P, 3, NT, HD], BF16)
                tm = sb(s2, "tm", [P, 3, 2], F32)
                tmn = sb(s2, "tmn", [P, 3], F32)
                tb = sb(s2, "tb", [P, 3], F32)
                esr = sb(s2, "esr", [P, 3], F32)
                sqc = sb(s2, "sqc", [P, 3], F32)
                esm = sb(s2, "esm", [P, 3, 2], F32)
                est = sb(s2, "est", [P, 3], F32)
        VF = AO[:].rearrange("p h t d -> p (h t d)").rearrange("p (t n) -> p t n", t=NT)

        kt_d = dram("kt_scratch", (3, D, T), BF16)
        qt_d = dram("qt_scratch", (D, T), BF16)
        w1_d = dram("w1_scratch", (NG1, P, WPARTS, D), F32)

        S = {n: sem(n) for n in (
            "x_in gam_in lut_in kv_in0 kv_in1 ident ones_set "
            "dve_own act_own pool_own sqrt_in sqrt_done "
            "q_split kv_hi kv_split s_ready nmax_ready exp_done p_ready pt_done pt_hi pt_lo pv0_done o0_used stats0 "
            "xn_ready xt_done xt_hi xt_lo router_in gW_ready gmerge g_hi g_lo lg_done lgT_copied lgt_done rt_e rt_done rexp "
            "w_in lora_in merge_done merged w_hi w_ready g_done silu_done u_used h_hi h_ready y_done y_added "
            "w1_in m1_merged w1_hi w1_ready g1_done silu1_done u1_used h1_hi h1_ready y1_done y1_added "
            "xn1_ready xt1_done xt1_hi xt1_lo "
            "bias_in wkv_in wkv_hi wkv_ready c_in0 c_in1 c_hi c_ready kv_done kv_used kp_ready kt_done kt_out kt_saved0 kt_saved1 "
            "vmx_ready vt_done vdg_ready svb_done v_ready "
            "wq_in wq_hi wq_ready qn_ready qx_done qx_hi qx_ready q_done q_used qp_ready qt_done qt_out qt_saved0 qt_saved1 "
            "wp_in wp_hi wp_ready ao_staged ao_t ao_hi ao_ready o_done o_used "
            "sqc_ready head_in vh_in0 vh_in1 vh_in2 sp_passed t_half t_max t_exp e_turned pt0_out pt1_out pv_done pv_used "
            "gp_passed pe_passed ix_in w1_saved out_stored "
        ).split()}

        def bank(i):
            return PS[:, i, :]

        def ln_finish(dve, ch):
            me, mo, ve, vo = st[:, :, 1], st[:, :, 4], st[:, :, 2], st[:, :, 5]
            ch.link(nc.vector.tensor_tensor(lnt[:, 0], me, mo, ALU.add))
            ch.link(nc.vector.tensor_tensor(lnt[:, 1], me, mo, ALU.subtract))
            ch.link(nc.vector.tensor_scalar(mu[:], lnt[:, 0], 0.5, None, ALU.mult))
            ch.link(nc.vector.tensor_tensor(lnt[:, 2], lnt[:, 1], lnt[:, 1], ALU.mult))
            ch.link(nc.vector.tensor_tensor(lnt[:, 0], ve, vo, ALU.add))
            ch.link(nc.vector.tensor_scalar(lnt[:, 1], lnt[:, 0], 1.0 / D, EPS, ALU.mult, ALU.add))
            nc.vector.scalar_tensor_tensor(out=lnt[:, 3], in0=lnt[:, 2], scalar=0.25, in1=lnt[:, 1],
                                           op0=ALU.mult, op1=ALU.add).then_inc(S["sqrt_in"], 1)

        def ln_root(act, n):
            act.wait_ge(S["sqrt_in"], n)
            nc.scalar.activation(lnt[:, 0], lnt[:, 3], ACT.Sqrt).then_inc(S["sqrt_done"], 1)

        def ln_invert(dve, ch, n, scale=None):
            dve.wait_ge(S["sqrt_done"], n)
            ch.link(nc.vector.reciprocal(rstd[:], lnt[:, 0]))
            if scale is not None:
                ch.link(nc.vector.tensor_scalar(rstd[:], rstd[:], scale, None, ALU.mult))

        def mm3(o, lh, ll, rh, rl, start, stop):
            nc.tensor.matmul(o, lh, rh, start=start, stop=False)
            nc.tensor.matmul(o, lh, rl, start=False, stop=False)
            return nc.tensor.matmul(o, ll, rh, start=False, stop=stop)

        block = ctx.enter_context(nc.Block())

        def store_x(sp, added, n):
            sp.wait_ge(S[added], n)
            for q in range(4):
                sp.dma_start(out[4 * q:4 * q + 4].rearrange("t p d -> p t d"), X[:, 4 * q:4 * q + 4, :]).then_inc(S["out_stored"], 16)
            sp.wait_ge(S["out_stored"], 64)

        def unit(g, tt, j, cols):
            return 2 * TT * g + (2 * tt + j if len(cols) == 2 else tt)

        MLP0 = dict(w_ready="w_ready", g_done="g_done", silu="silu_done", u_used="u_used", h_hi="h_hi", h_ready="h_ready",
                    y_done="y_done", y_added="y_added")
        MLP1 = dict(w_ready="w1_ready", g_done="g1_done", silu="silu1_done", u_used="u1_used", h_hi="h1_hi", h_ready="h1_ready",
                    y_done="y1_done", y_added="y1_added")

        @block.sync
        def _(sp):
            def attn0_in(t, par, n):
                if n is not None:
                    sp.wait_ge(S["kv_split"], n)
                sp.dma_start(Kf[:, par], a["ctx"][bass.ds(t, 1)].rearrange("o p d -> p (o d)")).then_inc(S[f"kv_in{par}"], 16)
                sp.dma_start(Vf[:, par], a["ctxT"][bass.ds(t, 1)].rearrange("o p d -> p (o d)")).then_inc(S[f"kv_in{par}"], 16)

            for q in range(4):
                sp.dma_start(X[:, 4 * q:4 * q + 4, :], a["x"][4 * q:4 * q + 4].rearrange("t p d -> p t d")).then_inc(S["x_in"], 16)
                if q == 0:
                    attn0_in(0, 0, None)
                    attn0_in(1, 1, None)
            sp.dma_start(gam[:], a["gamma"].partition_broadcast(P)).then_inc(S["gam_in"], 16)
            with sp.Fori(1, NT // 2) as i:
                for par in range(2):
                    attn0_in(2 * i + par, par, 2 * i + par - 1)
            if STOP == 1:
                return store_x(sp, "o0_used", 2 * NT)
            sp.wait_ge(S["pv0_done"], 2 * NT)
            for dst, src in ((gA[:], a["gA"]), (gB[:], a["gBT"]), (gW[:], a["gWT"].rearrange("(c p) e -> p c e", p=P))):
                sp.dma_start(dst, src).then_inc(S["router_in"], 16)
            sp.wait_ge(S["rt_done"], 1)

            def expert_in(e, n, m):
                if n is not None:
                    sp.wait_ge(S["w_ready"], n)
                sp.dma_start(WR[:, 0:DC, :], a["gup"][bass.ds(e, 1)].rearrange("o (c p) n -> p (o c) n", p=P)).then_inc(S["w_in"], 16)
                sp.dma_start(WR[:, DC:WPARTS, :], a["down"][bass.ds(e, 1)].rearrange("o (c p) n -> p (o c) n", p=P)).then_inc(S["w_in"], 16)
                sp.dma_start(lA[:], a["lA"][bass.ds(e, 1)].rearrange("o r n -> r (o n)")).then_inc(S["w_in"], 16)
                sp.dma_start(lB[:], a["lB"][bass.ds(e, 1)].rearrange("o r k n -> r (o k) n")).then_inc(S["w_in"], 16)

            expert_in(0, None, None)
            with sp.Fori(1, E) as e:
                expert_in(e, e, e)
            if STOP == 2:
                return store_x(sp, "y_added", 4 * TT * E)
            sp.wait_ge(S["y_done"], 4 * TT * E)
            for dst, src in ((bq, "bq"), (bkv, "bkv"), (bp, "bp")):
                sp.dma_start(dst[:], a[src].partition_broadcast(P)).then_inc(S["bias_in"], 16)

            def weight_in(name, col, s_in, freed, n):
                if freed:
                    sp.wait_ge(S[freed], n)
                sp.dma_start(wr[:], a[name][:, col:col + D].rearrange("(c p) n -> p c n", p=P)).then_inc(S[s_in], 16)

            weight_in("Wkv", 0, "wkv_in", None, 0)
            weight_in("Wkv", D, "wkv_in", "wkv_ready", 1)
            weight_in("Wq", 0, "wq_in", "wkv_ready", 2)

            def ctx_in(t, par, n):
                if n is not None:
                    sp.wait_ge(S["c_ready"], n)
                sp.dma_start(CT[:, par], a["ctxT"][bass.ds(t, 1)].rearrange("o p d -> p (o d)")).then_inc(S[f"c_in{par}"], 16)

            def save(src, dst, t, s_out, n, s_saved):
                sp.wait_ge(S[s_out], n)
                sp.dma_start(dst.rearrange("(c p) n -> p c n", p=P)[:, :, bass.ds(t * P, P)],
                             src.rearrange("p (c n) -> p c n", c=DC)).then_inc(S[s_saved], 16)

            ctx_in(0, 0, None)
            ctx_in(1, 1, None)
            with sp.Fori(0, NT // 2 - 1) as i:
                for par in range(2):
                    ctx_in(2 * i + par + 2, par, 2 * i + par + 1)
                    for k in range(3):
                        save(kts[:, par, k], kt_d[k], 2 * i + par, "kt_out", 2 * i + par + 1, f"kt_saved{par}")
            for par in range(2):
                for k in range(3):
                    save(kts[:, par, k], kt_d[k], NT - 2 + par, "kt_out", NT - 1 + par, f"kt_saved{par}")
            with sp.Fori(0, NT // 2) as i:
                for par in range(2):
                    save(kts[:, par, 0], qt_d, 2 * i + par, "qt_out", 2 * i + par + 1, f"qt_saved{par}")
            for par in range(2):
                sp.wait_ge(S[f"kt_saved{par}"], 16 * 3 * NT // 2)
                sp.wait_ge(S[f"qt_saved{par}"], 16 * NT // 2)

            def head_in(h):
                par = bass.ds(h % 2, 1)
                for k in range(3):
                    sp.dma_start(KS[HD * k:HD * (k + 1), par], kt_d[k:k + 1, bass.ds(h * HD, HD)].rearrange("a d n -> d a n")).then_inc(S["head_in"], 16)
                    sp.dma_start(QS[HD * k:HD * (k + 1), par], qt_d[bass.ds(h * HD, HD)].rearrange("(a d) n -> d a n", a=1)).then_inc(S["head_in"], 16)

            def values_in(h, k):
                sp.dma_start(VK[:, k:k + 1].rearrange("p a t d -> p a (t d)"),
                             VI[:, bass.ds(h, 1)].rearrange("p a t d -> p a (t d)")).then_inc(S[f"vh_in{k}"], 16)

            def next_head(h, r, load=True):
                if load:
                    sp.wait_ge(S["head_in"], 96 * h + 96)
                    sp.sem_inc(S["sp_passed"], 1)
                    sp.wait_ge(S["t_half"], h * 2 * NT)
                    head_in(h + 1)
                for m in range(3):
                    sp.wait_ge(S["pv_done"], NT * h - 2 + m)
                    values_in(h, (1 + r + m) % 3)

            head_in(0)
            sp.wait_ge(S["head_in"], 96)
            head_in(1)
            sp.wait_ge(S["v_ready"], 1)
            for k in range(3):
                values_in(0, k)
            with sp.Fori(0, H1 // 3 - 1) as g:
                for r in range(3):
                    next_head(3 * g + 1 + r, r)
            for r in range(3):
                next_head(H1 - 3 + r, r, load=(r < 2))
            sp.wait_ge(S["pv_used"], H1 * NT)
            sp.dma_start(wr[:], a["Wp"].rearrange("(c p) n -> p c n", p=P)).then_inc(S["wp_in"], 16)
            if STOP == 3:
                return store_x(sp, "o_used", NT)
            sp.wait_ge(S["o_used"], NT)
            sp.wait_ge(S["w1_saved"], 16 * NG1 * WPARTS)

            def group_in(g, n):
                if n is not None:
                    sp.wait_ge(S["w1_ready"], n)
                sp.dma_start(WR[:], w1_d[bass.ds(g, 1)].rearrange("o p c n -> p (o c) n")).then_inc(S["w1_in"], 16)

            group_in(0, None)
            with sp.Fori(1, NG1) as g:
                group_in(g, g)
            store_x(sp, "y1_added", 4 * TT * NG1)

        @block.gpsimd
        def _(gp):
            nc.gpsimd.memset(ones[:], 1.0).then_inc(S["pool_own"], 1)
            nc.gpsimd.memset(idf[:], 0.0).then_inc(S["pool_own"], 1)
            nc.gpsimd.memset(idb[:], 0.0).then_inc(S["pool_own"], 1)
            gp.wait_ge(S["pool_own"], 3)
            for m in (idf, idb):
                nc.gpsimd.affine_select(out=m[:], in_=m[:], compare_op=ALU.not_equal, fill=1.0, base=0,
                                        pattern=[[-1, P]], channel_multiplier=1).then_inc(S["ident"], 1)
            if STOP >= 3:
                gp.dma_start(lut[:], a["lut"].partition_broadcast(P)).then_inc(S["lut_in"], 16)
                gp.wait_ge(S["lut_in"], 16)
                ch = Chain(gp, S["pool_own"], passed=S["gp_passed"])
                per = 2 * LUT - 1

                def decode(g, c, first, k):
                    gp.dma_start(ix[:], a["idx"][bass.ds(g, 1), :, c].rearrange("o p n -> p (o n)")).then_inc(S["ix_in"], 16)
                    gp.wait_ge(S["ix_in"], 16 * k + 16)
                    if not first:
                        gp.wait_ge(S["w1_saved"], 16 * k)
                    gp.sem_inc(S["gp_passed"], 1)
                    ch.enter(3 + per * k)
                    for j in range(LUT):
                        dst = dec[:] if j == 0 else pick[:, j % 2]
                        ch.link(nc.gpsimd.tensor_scalar(dst, ix[:], float(j), lut[:, j:j + 1], ALU.is_equal, ALU.mult))
                        if j:
                            ch.link(nc.gpsimd.tensor_tensor(dec[:], dec[:], pick[:, j % 2], ALU.add))
                    gp.dma_start(w1_d[bass.ds(g, 1), :, c].rearrange("o p n -> p (o n)"), dec[:]).then_inc(S["w1_saved"], 16)

                for c in range(WPARTS):
                    decode(0, c, c == 0, c)
                with gp.Fori(1, NG1) as g:
                    for c in range(WPARTS):
                        decode(g, c, False, g * WPARTS + c)

        NU = H1 * NT

        @block.tensor
        def _(pe):
            pe.wait_ge(S["ident"], 2)

            def scores0(i, k):
                n, tile, par, hh, c = 16 * i + k, 2 * i + k // 8, (k // 8) % 2, (k // 4) % 2, k % 4
                if k % 8 == 0:
                    pe.wait_ge(S["q_split"], tile + 1)
                    pe.wait_ge(S["kv_split"], tile + 1)
                if not (isinstance(n, int) and n < 2):
                    pe.wait_ge(S["exp_done"], n - 1)
                rows = slice(HROWS * hh, HROWS * (hh + 1))
                mm3(bank(k % 2), QH[rows, par, c * P:(c + 1) * P], QL[rows, par, c * P:(c + 1) * P],
                    KH[rows, par], KL[rows, par], True, True).then_inc(S["s_ready"], 1)

            def turn0(i, k):
                n = 16 * i + k
                pe.wait_ge(S["p_ready"], n + 1)
                if not (isinstance(n, int) and n < 2):
                    pe.wait_ge(S["pt_lo"], n - 1)
                for lc in range(4):
                    m = nc.tensor.transpose(bank(2 + k % 2)[:, lc * P:(lc + 1) * P], pr[:, k % 2, lc * P:(lc + 1) * P], idf[:])
                m.then_inc(S["pt_done"], 1)

            def pv0(i, g):
                n = 4 * i + g
                pe.wait_ge(S["pt_lo"], 4 * n + 4)
                if not (isinstance(n, int) and n < 2):
                    pe.wait_ge(S["o0_used"], n - 1)
                par = (g // 2) % 2
                for lc in range(4):
                    m = mm3(bank(4 + g % 2), VH[:, par, lc * P:(lc + 1) * P], VL[:, par, lc * P:(lc + 1) * P],
                            PTH[:, g % 2, lc], PTL[:, g % 2, lc], lc == 0, lc == 3)
                m.then_inc(S["pv0_done"], 1)

            def attn0(i, first=False, last=False):
                for k in range(16):
                    if not (last and k >= 14):
                        scores0(i, k + 2)
                    turn0(i, k)
                    if k % 4 == 0 and not (first and k == 0):
                        pv0(i, k // 4 - 1)

            scores0(0, 0)
            scores0(0, 1)
            attn0(0, first=True)
            with pe.Fori(1, NT // 2 - 1) as i:
                attn0(i)
            attn0(NT // 2 - 1, last=True)
            pv0(NT // 2 - 1, 3)
            if STOP == 1:
                return

            def xt_tile(t, k, s_ready, s_lo, s_done):
                pe.wait_ge(S[s_ready], t + 1)
                if not (isinstance(t, int) and t < 2):
                    pe.wait_ge(S[s_lo], t - 1)
                for c in range(DC):
                    m = nc.tensor.transpose(bank(k % 2)[:, c * P:(c + 1) * P], xn[:, k % 2, c * P:(c + 1) * P], idf[:])
                m.then_inc(S[s_done], 1)

            def xt(s_ready, s_lo, s_done):
                for k in range(2):
                    xt_tile(k, k, s_ready, s_lo, s_done)
                with pe.Fori(1, NT // 2) as i:
                    for k in range(2):
                        xt_tile(2 * i + k, k, s_ready, s_lo, s_done)

            xt("xn_ready", "xt_lo", "xt_done")
            pe.wait_ge(S["router_in"], 48)
            pe.wait_ge(S["o0_used"], 2 * NT)
            for c in range(DC):
                m = nc.tensor.matmul(bank(4)[:, c * E:(c + 1) * E], gA[:, c * P:(c + 1) * P], gB[:], start=True, stop=True)
            m.then_inc(S["gmerge"], 1)
            pe.wait_ge(S["g_lo"], 1)
            pe.wait_ge(S["xt_lo"], NT)
            for tt in range(TT):
                if tt >= 2:
                    pe.wait_ge(S["lgT_copied"], tt - 1)
                for c in range(DC):
                    m = mm3(bank(2 + tt % 2), gH[:, c], gL[:, c], XTH[:, c, tt * 512:(tt + 1) * 512],
                            XTL[:, c, tt * 512:(tt + 1) * 512], c == 0, c == DC - 1)
                m.then_inc(S["lg_done"], 1)
            pe.wait_ge(S["lgT_copied"], TT)
            for t in range(NT):
                m = nc.tensor.transpose(bank(5)[:, t * E:(t + 1) * E], lgT[:, t * P:(t + 1) * P], idf[0:E, 0:E])
            m.then_inc(S["lgt_done"], 1)

            def merge(e, n_used):
                pe.wait_ge(S["w_in"], 64 * (e + 1))
                for c in range(WPARTS):
                    v = n_used + c - 1
                    if not (isinstance(v, int) and v <= 0):
                        pe.wait_ge(S["merged"], v)
                    lhs = lA[:, c * P:(c + 1) * P]
                    nc.tensor.matmul(bank(6 + c % 2), lhs, lB[:, 0 if c < DC else 1], start=True, stop=True) \
                        .then_inc(S["merge_done"], 1)

            def gate_up(g, tt, par, names, cols, first):
                rdy, used, done = names["w_ready"], names["u_used"], names["g_done"]
                if tt == 0:
                    pe.wait_ge(S[rdy], g + 1)
                for j, m_ in enumerate(cols):
                    if not (first and tt == 0):
                        pe.wait_ge(S[used], unit(g, tt, j, cols) - (1 if len(cols) == 2 else 0))
                    for b, off in ((j, 0), (2 + j, GROUP)):
                        for c in range(DC):
                            w = slice(off + j * P, off + j * P + m_)
                            m = mm3(PS[0:m_, b, :], WH[:, par, c, w], WL[:, par, c, w],
                                    XTH[:, c, tt * 512:(tt + 1) * 512], XTL[:, c, tt * 512:(tt + 1) * 512],
                                    c == 0, c == DC - 1)
                    m.then_inc(S[done], 1)

            def down(g, tt, par, names, cols, first):
                pe.wait_ge(S[names["h_ready"]], unit(g, tt, len(cols) - 1, cols) + 1)
                for q in range(4):
                    n = 4 * (g * TT + tt) + q
                    if not (first and tt == 0 and q < 2):
                        pe.wait_ge(S[names["y_added"]], n - 1)
                    for j, m_ in enumerate(cols):
                        m = mm3(bank(4 + q % 2), HH[0:m_, tt % 2, j, q * P:(q + 1) * P], HL[0:m_, tt % 2, j, q * P:(q + 1) * P],
                                WH[0:m_, par, DC + j], WL[0:m_, par, DC + j], j == 0, j == len(cols) - 1)
                    m.then_inc(S[names["y_done"]], 1)

            def group(g, par, names, cols, first=False, merge_next=False):
                gate_up(g, 0, par, names, cols, first)
                gate_up(g, 1, par, names, cols, False)
                down(g, 0, par, names, cols, first)
                gate_up(g, 2, par, names, cols, False)
                down(g, 1, par, names, cols, False)
                if merge_next:
                    merge(g + 1, WPARTS * (g + 1))
                gate_up(g, 3, par, names, cols, False)
                down(g, 2, par, names, cols, False)
                down(g, 3, par, names, cols, False)

            both = [P, P]
            pe.wait_ge(S["rt_done"], 1)
            merge(0, 0)
            group(0, 0, MLP0, both, first=True, merge_next=True)
            with pe.Fori(0, E // 2 - 1) as i:
                group(2 * i + 1, 1, MLP0, both, merge_next=True)
                group(2 * i + 2, 0, MLP0, both, merge_next=True)
            group(E - 1, 1, MLP0, both)
            if STOP == 2:
                return

            pe.wait_ge(S["wkv_ready"], 2)
            pe.wait_ge(S["y_added"], 4 * TT * E)

            def kv(t, par, first):
                pe.wait_ge(S["c_ready"], t + 1)
                if not first:
                    pe.wait_ge(S["kv_used"], 2 * (t - 1))
                for w in range(2):
                    for c in range(DC):
                        m = mm3(bank(2 * w + par), CH[:, par, c], CL[:, par, c], wH[:, w, c], wL[:, w, c], c == 0, c == DC - 1)
                    m.then_inc(S["kv_done"], 1)

            def kparts(t, par, first):
                pe.wait_ge(S["kp_ready"], t + 1)
                if not first:
                    pe.wait_ge(S["kt_out"], t)
                for k in range(3):
                    o = bank(4 + k).bitcast(BF16)
                    for c in range(DC):
                        m = nc.tensor.transpose(o[:, c * P:(c + 1) * P], kp[:, par, k, c * P:(c + 1) * P], idb[:])
                m.then_inc(S["kt_done"], 1)

            kv(0, 0, True)
            kv(1, 1, True)
            kparts(0, 0, True)
            with pe.Fori(1, NT // 2) as i:
                kv(2 * i, 0, False)
                kparts(2 * i - 1, 1, False)
                kv(2 * i + 1, 1, False)
                kparts(2 * i, 0, False)
            kparts(NT - 1, 1, False)
            pe.wait_ge(S["vmx_ready"], NT)
            for c in range(DC):
                m = nc.tensor.transpose(bank(7)[:, c * P:(c + 1) * P], vmx[:, c * P:(c + 1) * P], idf[:])
            m.then_inc(S["vt_done"], 1)
            pe.wait_ge(S["vdg_ready"], DC)
            for c in range(DC):
                m = nc.tensor.matmul(bank(7)[:, c * P:(c + 1) * P], ones[:], vdg[:, c], start=True, stop=True)
            m.then_inc(S["svb_done"], 1)

            pe.wait_ge(S["kv_used"], 2 * NT)
            pe.wait_ge(S["wq_ready"], 1)
            pe.wait_ge(S["kt_out"], NT)

            def qx(t, par, first):
                pe.wait_ge(S["qn_ready"], t + 1)
                if not first:
                    pe.wait_ge(S["qx_ready"], t - 1)
                for c in range(DC):
                    m = nc.tensor.transpose(bank(par)[:, c * P:(c + 1) * P], CT[:, par, c * P:(c + 1) * P], idf[:])
                m.then_inc(S["qx_done"], 1)

            def qmm(t, par, first):
                pe.wait_ge(S["qx_ready"], t + 1)
                if not first:
                    pe.wait_ge(S["q_used"], t - 1)
                for c in range(DC):
                    m = mm3(bank(2 + par), CH[:, par, c], CL[:, par, c], wH[:, 0, c], wL[:, 0, c], c == 0, c == DC - 1)
                m.then_inc(S["q_done"], 1)

            def qturn(t, par, first):
                pe.wait_ge(S["qp_ready"], t + 1)
                if not first:
                    pe.wait_ge(S["qt_out"], t)
                o = bank(4).bitcast(BF16)
                for c in range(DC):
                    m = nc.tensor.transpose(o[:, c * P:(c + 1) * P], kp[:, par, 0, c * P:(c + 1) * P], idb[:])
                m.then_inc(S["qt_done"], 1)

            qx(0, 0, True)
            qx(1, 1, True)
            qmm(0, 0, True)
            with pe.Fori(1, NT // 2) as i:
                qx(2 * i, 0, False)
                qmm(2 * i - 1, 1, False)
                qturn(2 * i - 2, 0, False)
                qx(2 * i + 1, 1, False)
                qmm(2 * i, 0, False)
                qturn(2 * i - 1, 1, False)
            qmm(NT - 1, 1, False)
            qturn(NT - 2, 0, False)
            qturn(NT - 1, 1, False)

            pe.wait_ge(S["qt_out"], NT)
            pe.wait_ge(S["v_ready"], 1)

            def scores(u, k, half, first=False):
                if half == 0:
                    pe.wait_ge(S["head_in"], 96 * (u // NT) + 96)
                if not first:
                    pe.wait_ge(S["t_exp"], 2 * u + half - 2)
                slot = (2 * k + half) % 3
                for b in range(2):
                    m = nc.tensor.matmul(bank(2 * slot + b), QS[0:KROWS].rearrange("p a n -> p (a n)")[:, bass.ds((u % 32) * P, P)],
                                         KS[0:KROWS].rearrange("p a n -> p (a n)")[:, bass.ds(((u // NT) % 2) * T + half * 1024 + b * 512, 512)],
                                         start=True, stop=True)
                m.then_inc(S["t_half"], 1)

            def turn(u, k, half, first=False):
                pe.wait_ge(S["t_exp"], 2 * u + half + 1)
                if not first:
                    pe.wait_ge(S[f"pt{half}_out"], u)
                    if half == 1:
                        pe.wait_ge(S["pv_used"], u)
                o = bank(6 + half).bitcast(BF16)
                for c in range(8):
                    m = nc.tensor.transpose(o[:, c * P:(c + 1) * P],
                                            ei[:, k, half * 1024 + c * P:half * 1024 + (c + 1) * P].bitcast(BF16), idb[:])
                m.then_inc(S["e_turned"], 1)

            def pv(u, k):
                pe.wait_ge(S[f"vh_in{k}"], 16 * (u // NT) + 16)
                pe.wait_ge(S["pt0_out"], u + 1)
                pe.wait_ge(S["pt1_out"], u + 1)
                for kt in range(NT):
                    m = nc.tensor.matmul(bank(7)[:, 0:HD], pt[:, k, kt * P:(kt + 1) * P],
                                         VK[:, k, kt], start=(kt == 0), stop=(kt == NT - 1))
                m.then_inc(S["pv_done"], 1)

            def step(u, k, first=False, ahead=2):
                if ahead >= 1:
                    scores(u + 1, (k + 1) % 3, 1)
                turn(u, k, 0, first)
                if not first:
                    pv(u - 1, (k + 2) % 3)
                if ahead >= 2:
                    scores(u + 2, (k + 2) % 3, 0)
                turn(u, k, 1, first)

            scores(0, 0, 0, True)
            scores(0, 0, 1, True)
            scores(1, 1, 0, True)
            step(0, 0, first=True)
            with pe.Fori(0, (NU - 4) // 3) as v:
                for k in range(3):
                    step(3 * v + 1 + k, (1 + k) % 3)
            for u in range(NU - 3, NU):
                step(u, u % 3, ahead=NU - 1 - u)
            pv(NU - 1, (NU - 1) % 3)

            pe.wait_ge(S["wp_ready"], 1)
            pe.wait_ge(S["pv_used"], NU)

            def oturn(t, par, first):
                pe.wait_ge(S["ao_staged"], t + 1)
                if not first:
                    pe.wait_ge(S["ao_ready"], t - 1)
                for c in range(DC):
                    m = nc.tensor.transpose(bank(par)[:, c * P:(c + 1) * P], CT[:, par, c * P:(c + 1) * P], idf[:])
                m.then_inc(S["ao_t"], 1)

            def omm(t, par, first):
                pe.wait_ge(S["ao_ready"], t + 1)
                if not (isinstance(t, int) and t < 2):
                    pe.wait_ge(S["o_used"], t - 1)
                for c in range(DC):
                    m = mm3(bank(2 + par), CH[:, par, c], CL[:, par, c], wH[:, 0, c], wL[:, 0, c], c == 0, c == DC - 1)
                m.then_inc(S["o_done"], 1)

            oturn(0, 0, True)
            oturn(1, 1, True)
            omm(0, 0, True)
            with pe.Fori(1, NT // 2) as i:
                oturn(2 * i, 0, False)
                omm(2 * i - 1, 1, False)
                oturn(2 * i + 1, 1, False)
                omm(2 * i, 0, False)
            omm(NT - 1, 1, False)
            if STOP == 3:
                return
            pe.wait_ge(S["o_used"], NT)
            xt("xn1_ready", "xt1_lo", "xt1_done")
            pe.wait_ge(S["xt1_lo"], NT)
            group(0, 0, MLP1, both, first=True)
            with pe.Fori(0, (NG1 - 2) // 2) as i:
                group(2 * i + 1, 1, MLP1, both)
                group(2 * i + 2, 0, MLP1, both)
            group(NG1 - 1, 1, MLP1, [LAST])

        @block.scalar
        def _(act):
            ln_root(act, 1)

            def split_kv(i, par, first):
                act.wait_ge(S[f"kv_in{par}"], 32 * (i + 1))
                if not first:
                    act.wait_ge(S["pv0_done"], 2 * (2 * i + par) - 2)
                nc.scalar.copy(KH[:, par], Kf[:, par]).then_inc(S["kv_hi"], 1)
                nc.scalar.copy(VH[:, par], Vf[:, par]).then_inc(S["kv_hi"], 1)

            def exp0(i, k):
                n = 16 * i + k
                act.wait_ge(S["nmax_ready"], n + 1)
                if not (isinstance(n, int) and n < 2):
                    act.wait_ge(S["pt_done"], n - 1)
                nc.scalar.activation(pr[:, k % 2], bank(k % 2), ACT.Exp, bias=nmx[:, k % 2:k % 2 + 1],
                                     accum_out=psm[:, k % 2:k % 2 + 1]).then_inc(S["exp_done"], 1)

            def pt_hi(i, k):
                n, g, c = 16 * i + k, (k // 4) % 2, k % 4
                act.wait_ge(S["pt_done"], n + 1)
                gg = 4 * i + k // 4
                if c == 0 and not (isinstance(gg, int) and gg < 2):
                    act.wait_ge(S["pv0_done"], gg - 1)
                nc.scalar.copy(PTH[:, g, :, c * P:(c + 1) * P], bank(2 + k % 2).rearrange("p (l q) -> p l q", l=4)).then_inc(S["pt_hi"], 1)

            def attn0(i, first=False, last=False):
                for k in range(16):
                    exp0(i, k)
                    if not (first and k == 0):
                        pt_hi(i, k - 1)
                    if k == 6:
                        if not first:
                            split_kv(i, 1, False)
                    if k == 14 and not last:
                        split_kv(i + 1, 0, False)

            split_kv(0, 0, True)
            split_kv(0, 1, True)
            attn0(0, first=True)
            with act.Fori(1, NT // 2 - 1) as i:
                attn0(i)
            attn0(NT // 2 - 1, last=True)
            pt_hi(NT // 2 - 1, 15)
            if STOP == 1:
                return

            def xt(s_done, s_hi):
                def tile(t, k):
                    act.wait_ge(S[s_done], t + 1)
                    nc.scalar.copy(XTH[:, :, bass.ds(t * P, P)], bank(k).rearrange("p (c q) -> p c q", c=DC)).then_inc(S[s_hi], 1)
                with act.Fori(0, NT // 2) as i:
                    for k in range(2):
                        tile(2 * i + k, k)

            ln_root(act, 2)
            xt("xt_done", "xt_hi")
            act.wait_ge(S["gW_ready"], 1)
            nc.scalar.copy(gH[:], gF[:]).then_inc(S["g_hi"], 1)
            for tt in range(TT):
                act.wait_ge(S["lg_done"], tt + 1)
                nc.scalar.copy(lgT[:, tt * 512:(tt + 1) * 512], PS[0:E, 2 + tt % 2, :]).then_inc(S["lgT_copied"], 1)
            act.wait_ge(S["rt_e"], 1)
            nc.scalar.activation(rt[:, 1], rt[:, 0], ACT.Exp).then_inc(S["rexp"], 1)

            def weights_hi(g, par, s_in, v, s_free, n_free, s_out):
                act.wait_ge(S[s_in], v)
                if n_free is not None:
                    act.wait_ge(S[s_free], n_free)
                nc.scalar.copy(WH[:, par], WR[:]).then_inc(S[s_out], 1)

            def hidden(g, tt, names, cols, first):
                for j, m_ in enumerate(cols):
                    n = unit(g, tt, j, cols)
                    act.wait_ge(S[names["g_done"]], n + 1)
                    if not (first and tt == 0):
                        act.wait_ge(S[names["u_used"]], n - (1 if len(cols) == 2 else 0))
                    nc.scalar.activation(sg[0:m_, j], PS[0:m_, j, :], ACT.Silu).then_inc(S[names["silu"]], 1)
                    act.wait_ge(S[names["u_used"]], n + 1)
                    if not (first and tt < 2):
                        act.wait_ge(S[names["y_done"]], 4 * (g * TT + tt) - 4)
                    nc.scalar.copy(HH[0:m_, tt % 2, j], HF[0:m_]).then_inc(S[names["h_hi"]], 1)

            def group(g, par, names, cols, first=False, nxt=None):
                hidden(g, 0, names, cols, first)
                hidden(g, 1, names, cols, first)
                hidden(g, 2, names, cols, False)
                if nxt:
                    nxt(g + 1, 1 - par, first)
                hidden(g, 3, names, cols, False)

            def next0(g, par, first):
                weights_hi(g, par, "merged", WPARTS * (g + 1), "y_done", None if first else 4 * TT * (g - 1), "w_hi")

            def next1(g, par, first):
                weights_hi(g, par, "w1_in", 16 * (g + 1), "y1_done", None if first else 4 * TT * (g - 1), "w1_hi")

            both = [P, P]
            next0(0, 0, True)
            group(0, 0, MLP0, both, True, next0)
            with act.Fori(0, E // 2 - 1) as i:
                group(2 * i + 1, 1, MLP0, both, False, next0)
                group(2 * i + 2, 0, MLP0, both, False, next0)
            group(E - 1, 1, MLP0, both)
            if STOP == 2:
                return

            for w in range(2):
                act.wait_ge(S["wkv_in"], 16 * (w + 1))
                nc.scalar.copy(wH[:, w], wr[:]).then_inc(S["wkv_hi"], 1)

            def copy_parts(t, par, s_done, s_saved, n_saved, parts, first_bank, s_out):
                act.wait_ge(S[s_done], t + 1)
                if n_saved is not None:
                    act.wait_ge(S[s_saved], n_saved)
                for k in range(parts):
                    m = nc.scalar.copy(kts[:, par, k], bank(first_bank + k).bitcast(BF16)[:, 0:D])
                m.then_inc(S[s_out], 1)

            def c_hi(i, par, first):
                act.wait_ge(S[f"c_in{par}"], 16 * (i + 1))
                if not first:
                    act.wait_ge(S["kv_done"], 2 * (2 * i + par - 1))
                nc.scalar.copy(CH[:, par].rearrange("p c n -> p (c n)"), CT[:, par]).then_inc(S["c_hi"], 1)

            c_hi(0, 0, True)
            c_hi(0, 1, True)
            copy_parts(0, 0, "kt_done", None, None, 3, 4, "kt_out")
            c_hi(1, 0, False)
            copy_parts(1, 1, "kt_done", None, None, 3, 4, "kt_out")
            c_hi(1, 1, False)
            with act.Fori(1, NT // 2 - 1) as i:
                for par in range(2):
                    copy_parts(2 * i + par, par, "kt_done", f"kt_saved{par}", 48 * i, 3, 4, "kt_out")
                    c_hi(i + 1, par, False)
            for par in range(2):
                copy_parts(NT - 2 + par, par, "kt_done", f"kt_saved{par}", 48 * (NT // 2 - 1), 3, 4, "kt_out")

            ln_root(act, 3)
            act.wait_ge(S["wq_in"], 16)
            act.wait_ge(S["kv_done"], 2 * NT)
            nc.scalar.copy(wH[:, 0], wr[:]).then_inc(S["wq_hi"], 1)

            def x_hi(t, par, s_done, s_hi, s_free, n_free):
                act.wait_ge(S[s_done], t + 1)
                if n_free is not None:
                    act.wait_ge(S[s_free], n_free)
                nc.scalar.copy(CH[:, par].rearrange("p c n -> p (c n)"), bank(par)).then_inc(S[s_hi], 1)

            x_hi(0, 0, "qx_done", "qx_hi", None, None)
            x_hi(1, 1, "qx_done", "qx_hi", None, None)
            for par in range(2):
                x_hi(2 + par, par, "qx_done", "qx_hi", "q_done", 1 + par)
                copy_parts(par, par, "qt_done", f"kt_saved{par}", 48 * (NT // 2), 1, 4, "qt_out")
            with act.Fori(2, NT // 2) as i:
                for par in range(2):
                    x_hi(2 * i + par, par, "qx_done", "qx_hi", "q_done", 2 * i + par - 1)
                    copy_parts(2 * i - 2 + par, par, "qt_done", f"qt_saved{par}", 16 * (i - 1), 1, 4, "qt_out")
            for par in range(2):
                copy_parts(NT - 2 + par, par, "qt_done", f"qt_saved{par}", 16 * (NT // 2 - 1), 1, 4, "qt_out")

            def exps(u, k, half, first=False):
                act.wait_ge(S["t_max"], u + 1)
                if not first:
                    act.wait_ge(S["e_turned"], 2 * u - 5 + half)
                    act.wait_ge(S["pv_used"], u - 2)
                slot = (2 * k + half) % 3
                nc.scalar.activation(ei[:, k, half * 1024:(half + 1) * 1024],
                                     PS[:, 2 * slot:2 * slot + 2, :].rearrange("p b n -> p (b n)"), ACT.Exp,
                                     bias=tb[:, k:k + 1], scale=sqc[:, k:k + 1],
                                     accum_out=esm[:, k, half:half + 1]).then_inc(S["t_exp"], 1)

            def query_scale(u, k):
                nc.scalar.copy(sqc[:, k:k + 1], SQ[:].rearrange("p h t -> p (h t)")[:, bass.ds(u, 1)]).then_inc(S["sqc_ready"], 1)

            def step(u, k, first=False, next_first=False, last=False, scale=True):
                exps(u, k, 1, first)
                act.wait_ge(S["e_turned"], 2 * u + 1)
                if not first:
                    act.wait_ge(S["pv_done"], u - 2)
                nc.scalar.copy(pt[:, k, 0:1024], bank(6).bitcast(I16)).then_inc(S["pt0_out"], 1)
                if scale:
                    if not first:
                        act.wait_ge(S["t_exp"], 2 * u)
                    query_scale(u + 2, (k + 2) % 3)
                if not last:
                    exps(u + 1, (k + 1) % 3, 0, next_first)

            act.wait_ge(S["v_ready"], 1)
            query_scale(0, 0)
            query_scale(1, 1)
            exps(0, 0, 0, True)
            step(0, 0, True, True)
            step(1, 1, True, True)
            step(2, 2, True, False)
            step(3, 0)
            with act.Fori(1, (NU - 4) // 3) as v:
                for k in range(3):
                    step(3 * v + 1 + k, (1 + k) % 3)
            for u in range(NU - 3, NU):
                step(u, u % 3, last=(u == NU - 1), scale=(u < NU - 2))

            act.wait_ge(S["wp_in"], 16)
            act.wait_ge(S["q_done"], NT)
            nc.scalar.copy(wH[:, 0], wr[:]).then_inc(S["wp_hi"], 1)
            x_hi(0, 0, "ao_t", "ao_hi", None, None)
            x_hi(1, 1, "ao_t", "ao_hi", None, None)
            with act.Fori(1, NT // 2) as i:
                for par in range(2):
                    x_hi(2 * i + par, par, "ao_t", "ao_hi", "o_done", 2 * i + par - 1)
            if STOP == 3:
                return
            ln_root(act, 4)
            xt("xt1_done", "xt1_hi")
            next1(0, 0, True)
            group(0, 0, MLP1, both, True, next1)
            with act.Fori(0, (NG1 - 2) // 2) as i:
                group(2 * i + 1, 1, MLP1, both, False, next1)
                group(2 * i + 2, 0, MLP1, both, False, next1)
            group(NG1 - 1, 1, MLP1, [LAST])

        @block.vector
        def _(dve):
            ch = Chain(dve, S["dve_own"])
            total = [0]

            def straight():
                ch.enter(total[0])

            def ended(loops=1):
                total[0] += loops * ch.n

            straight()
            dve.wait_ge(S["x_in"], 16 * 4)
            for t in range(NT):
                m = nc.vector.bn_stats(st[:, t], X[:, t])
            ch.link(m)
            ln_finish(dve, ch)
            ln_invert(dve, ch, 1, scale=1.0 / math.sqrt(HROWS))

            def prep(i, par, first):
                t = 2 * i + par
                if not first:
                    dve.wait_ge(S["s_ready"], 8 * (t - 1))
                    dve.wait_ge(S["pv0_done"], 2 * (t - 1))
                if not (isinstance(t, int) and t == 0):
                    dve.wait_ge(S["q_split"], t)
                ch.link(nc.vector.tensor_scalar(Qf[:], X[:, bass.ds(t, 1)].rearrange("p o d -> p (o d)"),
                                                mu[:, bass.ds(t, 1)], rstd[:, bass.ds(t, 1)], ALU.subtract, ALU.mult))
                ch.link(nc.vector.tensor_copy(QH[:, par], Qf[:]))
                nc.vector.tensor_tensor(QL[:, par], Qf[:], QH[:, par].bitcast(F32), ALU.subtract).then_inc(S["q_split"], 1)
                dve.wait_ge(S["kv_hi"], 2 * (t + 1))
                nc.vector.tensor_tensor(KL[:, par], Kf[:, par], KH[:, par].bitcast(F32), ALU.subtract)
                nc.vector.tensor_tensor(VL[:, par], Vf[:, par], VH[:, par].bitcast(F32), ALU.subtract).then_inc(S["kv_split"], 1)

            def rowmax(i, k):
                n = 16 * i + k
                dve.wait_ge(S["s_ready"], n + 1)
                nc.vector.tensor_reduce(nmx[:, k % 2:k % 2 + 1], bank(k % 2), AX.X, ALU.max, negate=True).then_inc(S["nmax_ready"], 1)

            def norm(i, k):
                n = 16 * i + k
                dve.wait_ge(S["exp_done"], n + 1)
                c = slice(k % 2, k % 2 + 1)
                ch.link(nc.vector.reciprocal(rsm[:, c], psm[:, c]))
                nc.vector.tensor_scalar(pr[:, k % 2], pr[:, k % 2], rsm[:, c], None, ALU.mult).then_inc(S["p_ready"], 1)

            def pt_lo(i, k):
                n, g, c = 16 * i + k, (k // 4) % 2, k % 4
                dve.wait_ge(S["pt_hi"], n + 1)
                o = (slice(None), g, slice(None), slice(c * P, (c + 1) * P))
                nc.vector.tensor_tensor(PTL[o], bank(2 + k % 2).rearrange("p (l q) -> p l q", l=4), PTH[o].bitcast(F32),
                                        ALU.subtract).then_inc(S["pt_lo"], 1)

            def add0(i, g):
                t, rows = 2 * i + g // 2, slice(HROWS * (g % 2), HROWS * (g % 2 + 1))
                n = 4 * i + g
                dve.wait_ge(S["pv0_done"], n + 1)
                x = X[rows, bass.ds(t, 1)].rearrange("p o d -> p (o d)")
                m = nc.vector.scalar_tensor_tensor(out=x, in0=PS[rows, 4 + g % 2, :], scalar=gam[rows], in1=x,
                                                   op0=ALU.mult, op1=ALU.add)
                m.then_inc(S["o0_used"], 1)
                if g % 2:
                    dve.wait_ge(S["o0_used"], n + 1)
                    nc.vector.bn_stats(st[:, bass.ds(t, 1)].rearrange("p o s -> p (o s)"),
                                       X[:, bass.ds(t, 1)].rearrange("p o d -> p (o d)")).then_inc(S["stats0"], 1)

            def attn0(i, first=False, last=False):
                for k in range(16):
                    if not (last and k == 15):
                        rowmax(i, k + 1)
                    norm(i, k)
                    if not (first and k == 0):
                        pt_lo(i, k - 1)
                    if k % 4 == 1 and not (first and k == 1):
                        add0(i, k // 4 - 1)
                    if k == 6 and not first:
                        prep(i, 1, False)
                    if k == 14 and not last:
                        prep(i + 1, 0, False)

            prep(0, 0, True)
            prep(0, 1, True)
            dve.wait_ge(S["gam_in"], 16)
            rowmax(0, 0)
            attn0(0, first=True)
            ended()
            per = 16 + 4
            with dve.Fori(1, NT // 2 - 1) as i:
                ch.enter(total[0] + per * (i - 1))
                attn0(i)
                assert ch.n == per
            total[0] += per * (NT // 2 - 2)
            straight()
            attn0(NT // 2 - 1, last=True)
            pt_lo(NT // 2 - 1, 15)
            add0(NT // 2 - 1, 3)
            if STOP == 1:
                return

            def flat(x, t):
                return x[:, bass.ds(t, 1)].rearrange("p o d -> p (o d)")

            dve.wait_ge(S["stats0"], NT)
            ln_finish(dve, ch)
            ln_invert(dve, ch, 2)
            ended()

            def xt(s_ready, s_done, s_hi, s_lo):
                def tile(t, k, first):
                    if not first:
                        dve.wait_ge(S[s_done], t - 1)
                    nc.vector.tensor_scalar(xn[:, k], flat(X, t), mu[:, bass.ds(t, 1)], rstd[:, bass.ds(t, 1)],
                                            ALU.subtract, ALU.mult).then_inc(S[s_ready], 1)

                def low(t, k):
                    dve.wait_ge(S[s_hi], t + 1)
                    nc.vector.tensor_tensor(XTL[:, :, bass.ds(t * P, P)], bank(k).rearrange("p (c q) -> p c q", c=DC),
                                            XTH[:, :, bass.ds(t * P, P)].bitcast(F32), ALU.subtract).then_inc(S[s_lo], 1)
                tile(0, 0, True)
                tile(1, 1, True)
                with dve.Fori(0, NT // 2 - 1) as i:
                    for k in range(2):
                        low(2 * i + k, k)
                        tile(2 * i + k + 2, k, False)
                for k in range(2):
                    low(NT - 2 + k, k)

            xt("xn_ready", "xt_done", "xt_hi", "xt_lo")
            straight()
            dve.wait_ge(S["router_in"], 48)
            ch.link(nc.vector.memset(gF[:], 0.0))
            dve.wait_ge(S["gmerge"], 1)
            nc.vector.scalar_tensor_tensor(out=gF[:, :, 0:E], in0=bank(4)[:, 0:DC * E].rearrange("p (c e) -> p c e", c=DC),
                                           scalar=2.0, in1=gW[:], op0=ALU.mult, op1=ALU.add).then_inc(S["gW_ready"], 1)
            dve.wait_ge(S["g_hi"], 1)
            nc.vector.tensor_tensor(gL[:], gF[:], gH[:].bitcast(F32), ALU.subtract).then_inc(S["g_lo"], 1)
            for e in range(E):
                m = nc.vector.memset(rev[:, :, e:e + 1], float(E - e))
            ch.link(m)
            dve.wait_ge(S["lgt_done"], 1)
            ch.link(nc.vector.tensor_copy(rt[:, 2], bank(5)[:, 0:NT * E].rearrange("p (t e) -> p t e", e=E)))

            def wide(x):
                return x.rearrange("p (t o) -> p t o", o=1).broadcast_to([P, NT, E])

            ch.link(nc.vector.tensor_reduce(rm[:, 0], rt[:, 2], AX.X, ALU.max))
            nc.vector.tensor_tensor(rt[:, 0], rt[:, 2], wide(rm[:, 0]), ALU.subtract).then_inc(S["rt_e"], 1)
            dve.wait_ge(S["rexp"], 1)

            def largest(src, mask, m, k):
                ch.link(nc.vector.tensor_reduce(rm[:, m], src, AX.X, ALU.max))
                ch.link(nc.vector.tensor_tensor(mask, src, wide(rm[:, m]), ALU.is_equal))
                ch.link(nc.vector.tensor_tensor(mask, mask, rev[:], ALU.mult))
                ch.link(nc.vector.tensor_reduce(rm[:, k], mask, AX.X, ALU.max))
                ch.link(nc.vector.tensor_tensor(mask, mask, wide(rm[:, k]), ALU.is_equal))

            largest(rt[:, 1], rt[:, 3], 0, 1)
            ch.link(nc.vector.scalar_tensor_tensor(out=rt[:, 4], in0=rt[:, 3], scalar=-2.0, in1=rt[:, 1], op0=ALU.mult, op1=ALU.add))
            largest(rt[:, 4], rt[:, 5], 2, 3)
            ch.link(nc.vector.tensor_tensor(rm[:, 1], rm[:, 0], rm[:, 2], ALU.add))
            ch.link(nc.vector.reciprocal(rm[:, 3], rm[:, 1]))
            ch.link(nc.vector.tensor_tensor(rt[:, 3], rt[:, 3], rt[:, 5], ALU.add))
            ch.link(nc.vector.tensor_tensor(rt[:, 4], rt[:, 3], rt[:, 1], ALU.mult))
            nc.vector.tensor_tensor(W8[:], rt[:, 4], wide(rm[:, 3]), ALU.mult).then_inc(S["rt_done"], 1)
            dve.wait_ge(S["rt_done"], 1)
            ended()

            def merged0(g, par, first):
                for c in range(WPARTS):
                    v = WPARTS * g + c + 1
                    dve.wait_ge(S["merge_done"], v)
                    nc.vector.scalar_tensor_tensor(out=WR[:, c], in0=bank(6 + c % 2), scalar=2.0, in1=WR[:, c],
                                                   op0=ALU.mult, op1=ALU.add).then_inc(S["merged"], 1)
                low_weights(g, par, "w_hi", "w_ready")

            def low_weights(g, par, s_hi, s_out):
                dve.wait_ge(S[s_hi], g + 1)
                nc.vector.tensor_tensor(WL[:, par], WR[:], WH[:, par].bitcast(F32), ALU.subtract).then_inc(S[s_out], 1)

            def merged1(g, par, first):
                low_weights(g, par, "w1_hi", "w1_ready")

            def hidden(g, tt, names, cols, first):
                for j, m_ in enumerate(cols):
                    n = unit(g, tt, j, cols)
                    dve.wait_ge(S[names["silu"]], n + 1)
                    if not (first and tt == 0 and j == 0):
                        dve.wait_ge(S[names["h_ready"]], n)
                    nc.vector.tensor_tensor(HF[0:m_], sg[0:m_, j], PS[0:m_, 2 + j, :], ALU.mult).then_inc(S[names["u_used"]], 1)
                    dve.wait_ge(S[names["h_hi"]], n + 1)
                    nc.vector.tensor_tensor(HL[0:m_, tt % 2, j], HF[0:m_], HH[0:m_, tt % 2, j].bitcast(F32),
                                            ALU.subtract).then_inc(S[names["h_ready"]], 1)

            def add(g, tt, names, weighted):
                for q in range(4):
                    n, t = 4 * (g * TT + tt) + q, 4 * tt + q
                    dve.wait_ge(S[names["y_done"]], n + 1)
                    if weighted:
                        w = W8[:, t, bass.ds(g, 1)]
                        m = nc.vector.scalar_tensor_tensor(out=X[:, t], in0=bank(4 + q % 2), scalar=w, in1=X[:, t],
                                                           op0=ALU.mult, op1=ALU.add)
                    else:
                        m = nc.vector.tensor_tensor(X[:, t], bank(4 + q % 2), X[:, t], ALU.add)
                    m.then_inc(S[names["y_added"]], 1)

            def measure(g, tt, names):
                dve.wait_ge(S[names["y_added"]], 4 * (g * TT + tt) + 4)
                for q in range(4):
                    m = nc.vector.bn_stats(st[:, 4 * tt + q], X[:, 4 * tt + q])
                return m

            def group(g, par, names, cols, first=False, nxt=None, weighted=False, measured=False):
                hidden(g, 0, names, cols, first)
                hidden(g, 1, names, cols, first)
                add(g, 0, names, weighted)
                hidden(g, 2, names, cols, False)
                add(g, 1, names, weighted)
                if nxt:
                    nxt(g + 1, 1 - par, first)
                hidden(g, 3, names, cols, False)
                if measured:
                    measure(g, 0, names)
                add(g, 2, names, weighted)
                if measured:
                    measure(g, 1, names)
                add(g, 3, names, weighted)
                if measured:
                    measure(g, 2, names)
                    return measure(g, 3, names)

            both = [P, P]
            merged0(0, 0, True)
            group(0, 0, MLP0, both, True, merged0, True)
            with dve.Fori(0, E // 2 - 1) as i:
                group(2 * i + 1, 1, MLP0, both, False, merged0, True)
                group(2 * i + 2, 0, MLP0, both, False, merged0, True)
            straight()
            ch.link(group(E - 1, 1, MLP0, both, False, None, True, measured=(STOP != 2)) or nc.vector.memset(lnt[:, 0, 0:1], 0.0))
            if STOP == 2:
                return
            ln_finish(dve, ch)

            ended()
            for w in range(2):
                dve.wait_ge(S["wkv_hi"], w + 1)
                nc.vector.tensor_tensor(wL[:, w], wr[:], wH[:, w].bitcast(F32), ALU.subtract).then_inc(S["wkv_ready"], 1)
            dve.wait_ge(S["bias_in"], 48)

            def c_lo(t, par, first):
                dve.wait_ge(S["c_hi"], t + 1)
                nc.vector.tensor_tensor(CL[:, par].rearrange("p c n -> p (c n)"), CT[:, par],
                                        CH[:, par].rearrange("p c n -> p (c n)").bitcast(F32), ALU.subtract).then_inc(S["c_ready"], 1)

            def heads(x):
                return x.rearrange("p (h d) -> p h d", d=HD)

            def by_head(x):
                return x.rearrange("p (h o) -> p h o", o=1).broadcast_to([P, H1, HD])

            def quantise(src, scale, s_dst):
                ch.link(nc.vector.tensor_reduce(ksc[:, 0], heads(src), AX.X, ALU.max, apply_absolute_value=True))
                ch.link(nc.vector.tensor_scalar(s_dst, ksc[:, 0], scale / QMAX, SMIN, ALU.mult, ALU.max))
                ch.link(nc.vector.reciprocal(ksc[:, 1], s_dst))
                if scale != 1.0:
                    ch.link(nc.vector.tensor_scalar(ksc[:, 1], ksc[:, 1], scale, None, ALU.mult))
                ch.link(nc.vector.tensor_tensor(heads(ki[:]), heads(src), by_head(ksc[:, 1]), ALU.mult))

            def kv(t, par, first, first_tile):
                dve.wait_ge(S["kv_done"], 2 * t + 1)
                nc.vector.tensor_tensor(kf[:], bank(par), bkv[:, 0:D], ALU.add).then_inc(S["kv_used"], 1)
                dve.wait_ge(S["kv_used"], 2 * t + 1)
                quantise(kf[:], 1.0, ksc[:, 2])
                ch.link(nc.vector.tensor_tensor(heads(kd[:]), heads(ki[:]), by_head(ksc[:, 2]), ALU.mult))
                if not first:
                    dve.wait_ge(S["kt_done"], t - 1)
                ch.link(nc.vector.tensor_copy(kp[:, par, 0], kd[:]))
                ch.link(nc.vector.tensor_tensor(kf[:], kd[:], kp[:, par, 0], ALU.subtract))
                ch.link(nc.vector.tensor_copy(kp[:, par, 1], kf[:]))
                nc.vector.tensor_tensor(kp[:, par, 2], kf[:], kp[:, par, 1], ALU.subtract).then_inc(S["kp_ready"], 1)
                dve.wait_ge(S["kp_ready"], t + 1)
                dve.wait_ge(S["kv_done"], 2 * t + 2)
                nc.vector.tensor_tensor(flat(VF, t), bank(2 + par), bkv[:, D:2 * D], ALU.add).then_inc(S["kv_used"], 1)
                dve.wait_ge(S["kv_used"], 2 * t + 2)
                size = vmx if first_tile else kd
                m = nc.vector.scalar_tensor_tensor(out=size[:], in0=flat(VF, t), scalar=-1.0, in1=flat(VF, t),
                                                   op0=ALU.mult, op1=ALU.max)
                if not first_tile:
                    ch.link(m)
                    m = nc.vector.tensor_tensor(vmx[:], vmx[:], kd[:], ALU.max)
                m.then_inc(S["vmx_ready"], 1)
                dve.wait_ge(S["vmx_ready"], t + 1)

            straight()
            c_lo(0, 0, True)
            c_lo(1, 1, True)
            kv(0, 0, True, True)
            c_lo(2, 0, False)
            kv(1, 1, True, False)
            c_lo(3, 1, False)
            ended()
            def kv_pair(i, more):
                for par in range(2):
                    kv(2 * i + par, par, False, False)
                    if more:
                        c_lo(2 * i + par + 2, par, False)
            per = 18
            with dve.Fori(1, NT // 2 - 1) as i:
                ch.enter(total[0] + per * (i - 1))
                kv_pair(i, True)
                assert ch.n == per, ch.n
            total[0] += per * (NT // 2 - 2)
            straight()
            kv_pair(NT // 2 - 1, False)
            dve.wait_ge(S["vt_done"], 1)
            ch.link(nc.vector.tensor_reduce(vsc[:, 0], bank(7).rearrange("p (c n) -> p c n", c=DC), AX.X, ALU.max,
                                            apply_absolute_value=True))
            ch.link(nc.vector.tensor_scalar(vsc[:, 1], vsc[:, 0], 1.0 / QMAX, SMIN, ALU.mult, ALU.max))
            for c in range(DC):
                nc.vector.tensor_scalar(vdg[:, c], idf[:], vsc[:, 1, c:c + 1], None, ALU.mult).then_inc(S["vdg_ready"], 1)
            dve.wait_ge(S["svb_done"], 1)
            ch.link(nc.vector.tensor_copy(svb[:], bank(7)))
            ch.link(nc.vector.reciprocal(rvb[:], svb[:]))
            ended()

            def v_ints(t, k):
                ch.link(nc.vector.tensor_tensor(vii[:, k], flat(VF, t), rvb[:], ALU.mult))
                return nc.vector.tensor_copy(VI[:, :, bass.ds(t, 1)].rearrange("p h a d -> p h (a d)"), heads(vii[:, k]))

            straight()
            ln_invert(dve, ch, 3)
            ended()
            dve.wait_ge(S["wq_hi"], 1)
            nc.vector.tensor_tensor(wL[:, 0], wr[:], wH[:, 0].bitcast(F32), ALU.subtract).then_inc(S["wq_ready"], 1)

            def qn(t, par, first):
                if not first:
                    dve.wait_ge(S["qx_done"], t - 1)
                nc.vector.tensor_scalar(CT[:, par], flat(X, t), mu[:, bass.ds(t, 1)], rstd[:, bass.ds(t, 1)],
                                        ALU.subtract, ALU.mult).then_inc(S["qn_ready"], 1)

            def x_lo(t, par, s_hi, s_out):
                dve.wait_ge(S[s_hi], t + 1)
                nc.vector.tensor_tensor(CL[:, par].rearrange("p c n -> p (c n)"), bank(par),
                                        CH[:, par].rearrange("p c n -> p (c n)").bitcast(F32), ALU.subtract).then_inc(S[s_out], 1)

            def q(t, par, first):
                dve.wait_ge(S["q_done"], t + 1)
                nc.vector.tensor_tensor(kf[:], bank(2 + par), bq[:], ALU.add).then_inc(S["q_used"], 1)
                dve.wait_ge(S["q_used"], t + 1)
                quantise(kf[:], QSCALE, ksc[:, 2])
                nc.vector.tensor_copy(SQ[:, :, bass.ds(t, 1)].rearrange("p h a -> p (h a)"), ksc[:, 2])
                if not first:
                    dve.wait_ge(S["qt_done"], t - 1)
                nc.vector.tensor_copy(kp[:, par, 0], ki[:]).then_inc(S["qp_ready"], 1)
                dve.wait_ge(S["qp_ready"], t + 1)

            straight()
            qn(0, 0, True)
            qn(1, 1, True)
            x_lo(0, 0, "qx_hi", "qx_ready")
            qn(2, 0, False)

            def q_step(t, par, first, more=True):
                if more:
                    x_lo(t + 1, 1 - par, "qx_hi", "qx_ready")
                if more and more != 1:
                    qn(t + 3, 1 - par, False)
                q(t, par, first)
                return v_ints(t, par)

            q_step(0, 0, True, 2)
            q_step(1, 1, True, 2)
            ended()
            per = 12
            with dve.Fori(1, NT // 2 - 2) as i:
                ch.enter(total[0] + per * (i - 1))
                for par in range(2):
                    q_step(2 * i + par, par, False, 2)
                assert ch.n == per, ch.n
            total[0] += per * (NT // 2 - 3)
            straight()
            for t in range(NT - 4, NT):
                m = q_step(t, t % 2, False, 2 if t < NT - 3 else t < NT - 1)
            m.then_inc(S["v_ready"], 1)
            ended()

            def half_max(u, k, half):
                dve.wait_ge(S["t_half"], 2 * u + half + 1)
                slot = (2 * k + half) % 3
                ch.link(nc.vector.tensor_reduce(tm[:, k, half:half + 1], PS[:, 2 * slot:2 * slot + 2, :].rearrange("p b n -> p (b n)"),
                                                AX.X, ALU.max, negate=True))

            def both_max(k):
                ch.link(nc.vector.tensor_scalar(tmn[:, k:k + 1], tm[:, k, 0:1], tm[:, k, 1:2], None, ALU.min))

            def exp_bias(u, k):
                c = slice(k, k + 1)
                dve.wait_ge(S["sqc_ready"], u + 1)
                nc.vector.tensor_scalar(tb[:, c], tmn[:, c], sqc[:, c], math.log(PMAX), ALU.mult, ALU.add).then_inc(S["t_max"], 1)

            def step(u, k, first=False, ahead=2, count=True):
                k1, k2 = (k + 1) % 3, (k + 2) % 3
                if ahead >= 1:
                    half_max(u + 1, k1, 1)
                dve.wait_ge(S["t_exp"], 2 * u + 2)
                m = nc.vector.tensor_scalar(est[:, k:k + 1], esm[:, k, 0:1], esm[:, k, 1:2], None, ALU.add)
                if ahead >= 1:
                    both_max(k1)
                    nc.vector.reciprocal(esr[:, k:k + 1], est[:, k:k + 1])
                    exp_bias(u + 1, k1)
                else:
                    ch.link(m)
                    ch.link(nc.vector.reciprocal(esr[:, k:k + 1], est[:, k:k + 1]))
                if not first:
                    result(u - 1, k2)
                if ahead >= 2:
                    half_max(u + 2, k2, 0)
                dve.wait_ge(S["e_turned"], 2 * u + 2)
                if count:
                    dve.wait_ge(S["pv_done"], u - 2)
                nc.vector.tensor_copy(pt[:, k, 1024:2048], bank(7).bitcast(I16)).then_inc(S["pt1_out"], 1)

            def result(u, k):
                dve.wait_ge(S["pv_done"], u + 1)
                nc.vector.tensor_scalar(AO[:].rearrange("p h t d -> p (h t d)")[:, bass.ds(u * HD, HD)], bank(7)[:, 0:HD],
                                        esr[:, k:k + 1], None, ALU.mult).then_inc(S["pv_used"], 1)

            dve.wait_ge(S["v_ready"], 1)
            straight()
            half_max(0, 0, 0)
            half_max(0, 0, 1)
            both_max(0)
            exp_bias(0, 0)
            half_max(1, 1, 0)
            step(0, 0, first=True, count=False)
            step(1, 1, count=False)
            step(2, 2, count=False)
            step(3, 0)
            ended()
            per = 9
            with dve.Fori(1, (NU - 4) // 3) as v:
                ch.enter(total[0] + per * (v - 1))
                for k in range(3):
                    step(3 * v + 1 + k, (1 + k) % 3)
                assert ch.n == per, ch.n
            total[0] += per * ((NU - 4) // 3 - 1)
            straight()
            for u in range(NU - 3, NU):
                step(u, u % 3, ahead=NU - 1 - u)
            result(NU - 1, (NU - 1) % 3)

            dve.wait_ge(S["wp_hi"], 1)
            nc.vector.tensor_tensor(wL[:, 0], wr[:], wH[:, 0].bitcast(F32), ALU.subtract).then_inc(S["wp_ready"], 1)
            dve.wait_ge(S["pv_used"], NU)
            ended()

            def stage(t, par, first):
                if not first:
                    dve.wait_ge(S["ao_t"], t - 1)
                nc.vector.tensor_tensor(CT[:, par].rearrange("p (h d) -> p h d", h=H1), AO[:, :, bass.ds(t, 1)].rearrange("p h a d -> p h (a d)"),
                                        svb[:].rearrange("p (h d) -> p h d", h=H1), ALU.mult).then_inc(S["ao_staged"], 1)

            def project(t, par):
                dve.wait_ge(S["o_done"], t + 1)
                ch.link(nc.vector.tensor_tensor(kf[:], bank(2 + par), bp[:], ALU.add))
                nc.vector.tensor_tensor(flat(X, t), kf[:], flat(X, t), ALU.add).then_inc(S["o_used"], 1)
                dve.wait_ge(S["o_used"], t + 1)

            def o_step(t, par, first, more=2):
                if more:
                    x_lo(t + 1, 1 - par, "ao_hi", "ao_ready")
                if more == 2:
                    stage(t + 3, 1 - par, False)
                project(t, par)
                return nc.vector.bn_stats(flat(st, t), flat(X, t))

            straight()
            stage(0, 0, True)
            stage(1, 1, True)
            x_lo(0, 0, "ao_hi", "ao_ready")
            stage(2, 0, False)
            o_step(0, 0, True)
            o_step(1, 1, True)
            ended()
            with dve.Fori(1, NT // 2 - 2) as i:
                ch.enter(total[0] + 2 * (i - 1))
                for par in range(2):
                    o_step(2 * i + par, par, False)
            total[0] += 2 * (NT // 2 - 3)
            straight()
            for t in range(NT - 4, NT):
                m = o_step(t, t % 2, False, 2 if t < NT - 3 else int(t < NT - 1))
            ch.link(m)
            if STOP == 3:
                return

            ln_finish(dve, ch)
            ln_invert(dve, ch, 4)
            ended()
            xt("xn1_ready", "xt1_done", "xt1_hi", "xt1_lo")
            merged1(0, 0, True)
            group(0, 0, MLP1, both, True, merged1)
            with dve.Fori(0, (NG1 - 2) // 2) as i:
                group(2 * i + 1, 1, MLP1, both, False, merged1)
                group(2 * i + 2, 0, MLP1, both, False, merged1)
            group(NG1 - 1, 1, MLP1, [LAST])


_INS = dict(x=None)


def kernel(**inputs):
    import numpy as np
    import concourse.bacc as bacc
    from concourse.bass_utils import run_bass_kernel_spmd

    v = {k: np.asarray(x) for k, x in inputs.items()}
    idx = np.zeros((NG1, P, WPARTS, D), np.int32)
    for half, name in ((0, "L1_ffn_gate_idx"), (GROUP, "L1_ffn_up_idx")):
        t = np.zeros((NG1 * GROUP, D), np.int32)
        t[:INTER] = v[name]
        idx[:, :, 0:DC, half:half + GROUP] = t.reshape(NG1, GROUP, DC, P).transpose(0, 3, 2, 1)
    t = np.zeros((NG1 * GROUP, D), np.int32)
    t[:INTER] = v["L1_ffn_down_idx"].T
    idx[:, :, DC:] = t.reshape(NG1, GROUP // P, P, D).transpose(0, 2, 1, 3)
    laid = {
        "x": v["x"].reshape(NT, P, D),
        "ctx": v["ctx_2048"].reshape(NT, P, D),
        "ctxT": v["ctx_2048"].reshape(NT, P, DC, P).transpose(0, 3, 2, 1).reshape(NT, P, D),
        "gamma": v["L0_xattn_gamma"].reshape(1),
        "gWT": v["L0_ffn_gate_weight"].T,
        "gA": v["L0_ffn_gate_lora_A"],
        "gBT": v["L0_ffn_gate_lora_B"].T,
        "gup": v["L0_ffn_gate_up_proj"],
        "down": v["L0_ffn_down_proj"],
        "lA": np.concatenate([v["L0_ffn_gup_lora_A"], v["L0_ffn_down_lora_A"]], axis=2),
        "lB": np.stack([v["L0_ffn_gup_lora_B"].transpose(0, 2, 1), v["L0_ffn_down_lora_B"].transpose(0, 2, 1)], axis=2),
        "Wq": v["L1_xattn_Wq"], "bq": v["L1_xattn_bq"],
        "Wkv": v["L1_xattn_Wkv"], "bkv": v["L1_xattn_bkv"],
        "Wp": v["L1_xattn_Wp"], "bp": v["L1_xattn_bp"],
        "lut": v["L1_ffn_lut"],
        "idx": idx,
    }
    nc = bacc.Bacc("TRN2", target_bir_lowering=False, num_devices=1)
    arrays, aps = {}, {}
    for name, x in laid.items():
        x = np.ascontiguousarray(x)
        arrays[f"in_{name}"] = x
        aps[name] = nc.dram_tensor(f"in_{name}", x.shape, mybir.dt.from_np(x.dtype), kind="ExternalInput").ap()
    out = nc.dram_tensor("out", (NT, P, D), F32, kind="ExternalOutput").ap()
    build(nc, aps, out)
    r = run_bass_kernel_spmd(nc, [arrays], core_ids=[0])
    return r.results[0]["out"].reshape(4, 512, D)
```

```python
import math
from contextlib import ExitStack

import concourse.bass as bass
from concourse import mybir

F32 = mybir.dt.float32
F32R = mybir.dt.float32r
BF16 = mybir.dt.bfloat16
I16 = mybir.dt.int16
I32 = mybir.dt.int32
ALU = mybir.AluOpType
ACT = mybir.ActivationFunctionType
AX = mybir.AxisListType

P = 128
D = 512
T = 2048
NT = T // P
DC = D // P
TT = T // 512
EPS = 1e-5

H0 = 8
HROWS = 512 // H0
E = 8
R = 16
INTER = 1376
GROUP = 256
NG1 = -(-INTER // GROUP)
LAST = INTER - (NG1 - 1) * GROUP
WPARTS = DC + GROUP // P
LUT = 16

H1 = 16
HD = D // H1
QSCALE = 1.0 / math.sqrt(HD)
QMAX = 127.0
PMAX = 255.0
SMIN = 1e-8
KROWS = 3 * HD


class Chain:

    def __init__(self, eng, sem, passed=None):
        self.eng, self.sem, self.base, self.n, self.passed = eng, sem, 0, 0, passed

    def enter(self, base):
        self.base, self.n = base, 0

    def mark(self, ins):
        self.n += 1
        ins.then_inc(self.sem, 1)
        return self.n

    def after(self, n):
        self.eng.wait_ge(self.sem, self.base + n)

    def link(self, ins):
        self.after(self.mark(ins))
        if self.passed:
            self.eng.sem_inc(self.passed, 1)


def build(nc, a, out):
    with ExitStack() as ctx:
        def sem(name):
            return ctx.enter_context(nc.semaphore(name))

        def dram(name, shape, dt):
            return nc.dram_tensor(name, shape, dt, kind="Internal").ap()

        def sb(stack, name, shape, dt):
            return stack.enter_context(nc.sbuf_tensor(name, shape, dt))

        X = sb(ctx, "X", [P, NT, D], F32)
        idf = sb(ctx, "idf", [P, P], F32)
        idb = sb(ctx, "idb", [P, P], BF16)
        ones = sb(ctx, "ones", [P, P], F32)
        gam = sb(ctx, "gam", [P, 1], F32)
        st = sb(ctx, "st", [P, NT, 6], F32)
        mu = sb(ctx, "mu", [P, NT], F32)
        rstd = sb(ctx, "rstd", [P, NT], F32)
        lnt = sb(ctx, "lnt", [P, 4, NT], F32)
        W8 = sb(ctx, "W8", [P, NT, E], F32)
        lut = sb(ctx, "lut", [P, LUT], F32)
        ix = sb(ctx, "ix", [P, D], I32)
        pick = sb(ctx, "pick", [P, 2, D], F32)
        dec = sb(ctx, "dec", [P, D], F32)

        PS = ctx.enter_context(nc.psum_tensor("PS", [P, 8, 512], F32))

        with ExitStack() as s:
            Kf = sb(s, "Kf", [P, 2, D], F32)
            Vf = sb(s, "Vf", [P, 2, D], F32)
            Qf = sb(s, "Qf", [P, D], F32)
            QH = sb(s, "QH", [P, 2, D], F32R)
            QL = sb(s, "QL", [P, 2, D], F32R)
            KH = sb(s, "KH", [P, 2, D], F32R)
            KL = sb(s, "KL", [P, 2, D], F32R)
            VH = sb(s, "VH", [P, 2, D], F32R)
            VL = sb(s, "VL", [P, 2, D], F32R)
            pr = sb(s, "pr", [P, 4, D], F32)
            nmx = sb(s, "nmx", [P, 2], F32)
            psm = sb(s, "psm", [P, 2], F32)
            rsm = sb(s, "rsm", [P, 2], F32)
            PTH = sb(s, "PTH", [P, 2, 4, D], F32R)
            PTL = sb(s, "PTL", [P, 2, 4, D], F32R)
        with ExitStack() as s:
            XTH = sb(s, "XTH", [P, DC, T], F32R)
            XTL = sb(s, "XTL", [P, DC, T], F32R)
            WR = sb(s, "WR", [P, WPARTS, D], F32)
            WH = sb(s, "WH", [P, 2, WPARTS, D], F32R)
            WL = sb(s, "WL", [P, 2, WPARTS, D], F32R)
            xn = sb(s, "xn", [P, 2, D], F32)
            sg = sb(s, "sg", [P, 2, 512], F32)
            HF = sb(s, "HF", [P, 512], F32)
            HH = sb(s, "HH", [P, 2, 2, 512], F32R)
            HL = sb(s, "HL", [P, 2, 2, 512], F32R)
            lA = sb(s, "lA", [R, D + GROUP], F32)
            lB = sb(s, "lB", [R, 2, D], F32)
        with ExitStack() as s:
            s.enter_context(nc.sbuf_tensor("below_sg", [P, 2 * DC * T + 5 * WPARTS * D + 2 * D], F32))
            gA = sb(s, "gA", [R, D], F32)
            gB = sb(s, "gB", [R, E], F32)
            gW = sb(s, "gW", [P, DC, E], F32)
            gH = sb(s, "gH", [P, DC, P], F32R)
            gL = sb(s, "gL", [P, DC, P], F32R)
            gF = sb(s, "gF", [P, DC, P], F32)
            lgT = sb(s, "lgT", [E, T], F32)
            rt = sb(s, "rt", [P, 6, NT, E], F32)
            rm = sb(s, "rm", [P, 4, NT], F32)
            rev = sb(s, "rev", [P, NT, E], F32)
        with ExitStack() as s:
            VI = sb(s, "VI", [P, H1, NT, HD], BF16)
            SQ = sb(s, "SQ", [P, H1, NT], F32)
            svb = sb(s, "svb", [P, D], F32)
            AO = sb(s, "AO", [P, H1, NT, HD], F32)
            bq = sb(s, "bq", [P, D], F32)
            bkv = sb(s, "bkv", [P, 2 * D], F32)
            bp = sb(s, "bp", [P, D], F32)
            wr = sb(s, "wr", [P, DC, D], F32)
            wH = sb(s, "wH", [P, 2, DC, D], F32R)
            wL = sb(s, "wL", [P, 2, DC, D], F32R)
            with ExitStack() as s2:
                CT = sb(s2, "CT", [P, 2, D], F32)
                CH = sb(s2, "CH", [P, 2, DC, P], F32R)
                CL = sb(s2, "CL", [P, 2, DC, P], F32R)
                kf = sb(s2, "kf", [P, D], F32)
                ki = sb(s2, "ki", [P, D], I16)
                kd = sb(s2, "kd", [P, D], F32)
                kp = sb(s2, "kp", [P, 2, 3, D], BF16)
                ksc = sb(s2, "ksc", [P, 4, H1], F32)
                kts = sb(s2, "kts", [P, 2, 3, D], BF16)
                vmx = sb(s2, "vmx", [P, D], F32)
                vdg = sb(s2, "vdg", [P, DC, P], F32)
                vsc = sb(s2, "vsc", [P, 2, DC], F32)
                rvb = sb(s2, "rvb", [P, D], F32)
                vii = sb(s2, "vii", [P, 2, D], I16)
            with ExitStack() as s2:
                KS = sb(s2, "KS", [P, 2, T], BF16)
                QS = sb(s2, "QS", [P, 2, T], BF16)
                ei = sb(s2, "ei", [P, 3, T], I16)
                pt = sb(s2, "pt", [P, 3, T], BF16)
                VK = sb(s2, "VK", [P, 3, NT, HD], BF16)
                tm = sb(s2, "tm", [P, 3, 2], F32)
                tmn = sb(s2, "tmn", [P, 3], F32)
                tb = sb(s2, "tb", [P, 3], F32)
                esr = sb(s2, "esr", [P, 3], F32)
                sqc = sb(s2, "sqc", [P, 3], F32)
                esm = sb(s2, "esm", [P, 3, 2], F32)
                est = sb(s2, "est", [P, 3], F32)
        VF = AO[:].rearrange("p h t d -> p (h t d)").rearrange("p (t n) -> p t n", t=NT)

        kt_d = dram("kt_scratch", (3, D, T), BF16)
        qt_d = dram("qt_scratch", (D, T), BF16)
        w1_d = dram("w1_scratch", (NG1, P, WPARTS, D), F32)

        S = {n: sem(n) for n in (
            "x_in0 x_in1 x_in2 x_in3 gam_in lut_in kv_in0 kv_in1 ident "
            "dve_own pool_own sqrt_in sqrt_done "
            "q_split kv_hi kv_split s_ready nmax_ready exp_done r_ready p_ready pt_done pt_hi pt_lo pv0_done o0_used stats0 "
            "xn_ready xt_done xt_hi xt_lo router_in gW_ready gmerge g_hi g_lo lg_done lgT_copied lgt_done rt_e rt_done rexp "
            "w_in merge_done merged w_hi w_ready g_done silu_done u_used h_hi h_ready y_done y_added "
            "w1_in w1_hi w1_ready g1_done silu1_done u1_used h1_hi h1_ready y1_done y1_added "
            "xn1_ready xt1_done xt1_hi xt1_lo "
            "bias_in wk_in wv_in wkv_hi wkv_ready c_in0 c_in1 c_hi c_ready kv_done kv_used kp_ready kt_done kt_out kt_saved0 kt_saved1 "
            "vmx_ready vt_done vdg_ready svb_done v_ready "
            "wq_in wq_hi wq_ready qn_ready qx_done qx_hi qx_ready q_done q_used qp_ready qt_done qt_out qt_saved0 qt_saved1 "
            "wp_in wp_hi wp_ready ao_staged ao_t ao_hi ao_ready o_done o_used "
            "sqc_ready head_in vh_in0 vh_in1 vh_in2 sp_passed t_half t_max t_exp e_turned pt0_out pt1_out pv_done pv_used "
            "gp_passed ix_in w1_saved out_stored "
        ).split()}

        def bank(i):
            return PS[:, i, :]

        def ln_finish(dve, ch):
            me, mo, ve, vo = st[:, :, 1], st[:, :, 4], st[:, :, 2], st[:, :, 5]
            ch.link(nc.vector.tensor_tensor(lnt[:, 0], me, mo, ALU.add))
            ch.link(nc.vector.tensor_tensor(lnt[:, 1], me, mo, ALU.subtract))
            ch.link(nc.vector.tensor_scalar(mu[:], lnt[:, 0], 0.5, None, ALU.mult))
            ch.link(nc.vector.tensor_tensor(lnt[:, 2], lnt[:, 1], lnt[:, 1], ALU.mult))
            ch.link(nc.vector.tensor_tensor(lnt[:, 0], ve, vo, ALU.add))
            ch.link(nc.vector.tensor_scalar(lnt[:, 1], lnt[:, 0], 1.0 / D, EPS, ALU.mult, ALU.add))
            nc.vector.scalar_tensor_tensor(out=lnt[:, 3], in0=lnt[:, 2], scalar=0.25, in1=lnt[:, 1],
                                           op0=ALU.mult, op1=ALU.add).then_inc(S["sqrt_in"], 1)

        def ln_root(act, n):
            act.wait_ge(S["sqrt_in"], n)
            nc.scalar.activation(lnt[:, 0], lnt[:, 3], ACT.Sqrt).then_inc(S["sqrt_done"], 1)

        def ln_invert(dve, ch, n, scale=None):
            dve.wait_ge(S["sqrt_done"], n)
            ch.link(nc.vector.reciprocal(rstd[:], lnt[:, 0]))
            if scale is not None:
                ch.link(nc.vector.tensor_scalar(rstd[:], rstd[:], scale, None, ALU.mult))

        def mm3(o, lh, ll, rh, rl, start, stop):
            nc.tensor.matmul(o, lh, rh, start=start, stop=False)
            nc.tensor.matmul(o, lh, rl, start=False, stop=False)
            return nc.tensor.matmul(o, ll, rh, start=False, stop=stop)

        block = ctx.enter_context(nc.Block())

        def store_x(sp, added, n):
            for q in range(4):
                sp.wait_ge(S[added], n[q])
                sp.dma_start(out[4 * q:4 * q + 4].rearrange("t p d -> p t d"), X[:, 4 * q:4 * q + 4, :]).then_inc(S["out_stored"], 16)
            sp.wait_ge(S["out_stored"], 64)

        def unit(g, tt, j, cols):
            return 2 * TT * g + (2 * tt + j if len(cols) == 2 else tt)

        MLP0 = dict(w_ready="w_ready", g_done="g_done", silu="silu_done", u_used="u_used", h_hi="h_hi", h_ready="h_ready",
                    y_done="y_done", y_added="y_added")
        MLP1 = dict(w_ready="w1_ready", g_done="g1_done", silu="silu1_done", u_used="u1_used", h_hi="h1_hi", h_ready="h1_ready",
                    y_done="y1_done", y_added="y1_added")

        @block.sync
        def _(sp):
            def attn0_in(t, par, n):
                if n is not None:
                    sp.wait_ge(S["kv_split"], 2 * n)
                sp.dma_start(Kf[:, par], a["ctx"][bass.ds(t, 1)].rearrange("o p d -> p (o d)")).then_inc(S[f"kv_in{par}"], 16)
                sp.dma_start(Vf[:, par], a["ctxT"][bass.ds(t, 1)].rearrange("o p d -> p (o d)")).then_inc(S[f"kv_in{par}"], 16)

            for q in range(4):
                sp.dma_start(X[:, 4 * q:4 * q + 4, :], a["x"][4 * q:4 * q + 4].rearrange("t p d -> p t d")).then_inc(S[f"x_in{q}"], 16)
                if q == 0:
                    attn0_in(0, 0, None)
                    attn0_in(1, 1, None)
            sp.dma_start(gam[:], a["gamma"].partition_broadcast(P)).then_inc(S["gam_in"], 16)
            for dst, src in ((gA[:], a["gA"]), (gB[:], a["gBT"]), (gW[:], a["gWT"].rearrange("(c p) e -> p c e", p=P))):
                sp.dma_start(dst, src).then_inc(S["router_in"], 16)
            with sp.Fori(1, NT // 2) as i:
                for par in range(2):
                    attn0_in(2 * i + par, par, 2 * i + par - 1)
            sp.wait_ge(S["pv0_done"], 2 * NT)

            def expert_in(e, n, m):
                if n is not None:
                    sp.wait_ge(S["w_ready"], n)
                sp.dma_start(WR[:, 0:DC, :], a["gup"][bass.ds(e, 1)].rearrange("o (c p) n -> p (o c) n", p=P)).then_inc(S["w_in"], 16)
                sp.dma_start(WR[:, DC:WPARTS, :], a["down"][bass.ds(e, 1)].rearrange("o (c p) n -> p (o c) n", p=P)).then_inc(S["w_in"], 16)
                sp.dma_start(lA[:], a["lA"][bass.ds(e, 1)].rearrange("o r n -> r (o n)")).then_inc(S["w_in"], 16)
                sp.dma_start(lB[:], a["lB"][bass.ds(e, 1)].rearrange("o r k n -> r (o k) n")).then_inc(S["w_in"], 16)

            expert_in(0, None, None)
            with sp.Fori(1, E) as e:
                expert_in(e, e, e)
            sp.wait_ge(S["y_done"], 4 * TT * E)
            def weight_in(dst, name, col, s_in):
                sp.dma_start(dst, a[name][:, col:col + D].rearrange("(c p) n -> p c n", p=P)).then_inc(S[s_in], 16)

            weight_in(wr[:], "Wkv", 0, "wk_in")

            def ctx_in(t, par, n):
                if n is not None:
                    sp.wait_ge(S["c_ready"], n)
                sp.dma_start(CT[:, par], a["ctxT"][bass.ds(t, 1)].rearrange("o p d -> p (o d)")).then_inc(S[f"c_in{par}"], 16)

            def save(src, dst, t, s_out, n, s_saved):
                sp.wait_ge(S[s_out], n)
                sp.dma_start(dst.rearrange("(c p) n -> p c n", p=P)[:, :, bass.ds(t * P, P)],
                             src.rearrange("p (c n) -> p c n", c=DC)).then_inc(S[s_saved], 16)

            ctx_in(0, 0, None)
            ctx_in(1, 1, None)
            weight_in(VF[:, NT - DC:NT], "Wkv", D, "wv_in")
            for dst, src in ((bq, "bq"), (bkv, "bkv"), (bp, "bp")):
                sp.dma_start(dst[:], a[src].partition_broadcast(P)).then_inc(S["bias_in"], 16)
            sp.wait_ge(S["wkv_ready"], 1)
            weight_in(wr[:], "Wq", 0, "wq_in")
            with sp.Fori(0, NT // 2 - 1) as i:
                for par in range(2):
                    ctx_in(2 * i + par + 2, par, 2 * i + par + 1)
                    for k in range(3):
                        save(kts[:, par, k], kt_d[k], 2 * i + par, "kt_out", 2 * i + par + 1, f"kt_saved{par}")
            for par in range(2):
                for k in range(3):
                    save(kts[:, par, k], kt_d[k], NT - 2 + par, "kt_out", NT - 1 + par, f"kt_saved{par}")
            sp.wait_ge(S["wq_ready"], 1)
            weight_in(wr[:], "Wp", 0, "wp_in")
            with sp.Fori(0, NT // 2) as i:
                for par in range(2):
                    save(kts[:, par, 0], qt_d, 2 * i + par, "qt_out", 2 * i + par + 1, f"qt_saved{par}")
            for par in range(2):
                sp.wait_ge(S[f"kt_saved{par}"], 16 * 3 * NT // 2)
                sp.wait_ge(S[f"qt_saved{par}"], 16 * NT // 2)

            def head_in(h):
                par = bass.ds(h % 2, 1)
                for k in range(3):
                    sp.dma_start(KS[HD * k:HD * (k + 1), par], kt_d[k:k + 1, bass.ds(h * HD, HD)].rearrange("a d n -> d a n")).then_inc(S["head_in"], 16)
                    sp.dma_start(QS[HD * k:HD * (k + 1), par], qt_d[bass.ds(h * HD, HD)].rearrange("(a d) n -> d a n", a=1)).then_inc(S["head_in"], 16)

            def values_in(h, k):
                sp.dma_start(VK[:, k:k + 1].rearrange("p a t d -> p a (t d)"),
                             VI[:, bass.ds(h, 1)].rearrange("p a t d -> p a (t d)")).then_inc(S[f"vh_in{k}"], 16)

            def next_head(h, r, load=True):
                if load:
                    sp.wait_ge(S["head_in"], 96 * h + 96)
                    sp.sem_inc(S["sp_passed"], 1)
                    sp.wait_ge(S["t_half"], h * 2 * NT)
                    head_in(h + 1)
                for m in range(3):
                    sp.wait_ge(S["pv_done"], NT * h - 2 + m)
                    values_in(h, (1 + r + m) % 3)

            head_in(0)
            sp.wait_ge(S["head_in"], 96)
            head_in(1)
            sp.wait_ge(S["v_ready"], 1)
            for k in range(3):
                values_in(0, k)
            with sp.Fori(0, H1 // 3 - 1) as g:
                for r in range(3):
                    next_head(3 * g + 1 + r, r)
            for r in range(3):
                next_head(H1 - 3 + r, r, load=(r < 2))
            sp.wait_ge(S["o_done"], NT)

            def group_in(g, n):
                if n is not None:
                    sp.wait_ge(S["w1_ready"], n)
                    sp.sem_inc(S["sp_passed"], 1)
                sp.wait_ge(S["w1_saved"], 16 * WPARTS * g + 16 * WPARTS)
                sp.dma_start(WR[:], w1_d[bass.ds(g, 1)].rearrange("o p c n -> p (o c) n")).then_inc(S["w1_in"], 16)

            group_in(0, None)
            with sp.Fori(1, NG1) as g:
                group_in(g, g)
            store_x(sp, "y1_added", [4 * TT * (NG1 - 1) + 4 * q + 4 for q in range(TT)])

        @block.gpsimd
        def _(gp):
            nc.gpsimd.memset(ones[:], 1.0).then_inc(S["pool_own"], 1)
            nc.gpsimd.memset(idf[:], 0.0).then_inc(S["pool_own"], 1)
            nc.gpsimd.memset(idb[:], 0.0).then_inc(S["pool_own"], 1)
            gp.wait_ge(S["pool_own"], 3)
            for m in (idf, idb):
                nc.gpsimd.affine_select(out=m[:], in_=m[:], compare_op=ALU.not_equal, fill=1.0, base=0,
                                        pattern=[[-1, P]], channel_multiplier=1).then_inc(S["ident"], 1)
            gp.dma_start(lut[:], a["lut"].partition_broadcast(P)).then_inc(S["lut_in"], 16)
            gp.wait_ge(S["lut_in"], 16)
            ch = Chain(gp, S["pool_own"], passed=S["gp_passed"])
            per = 2 * LUT - 1

            def decode(g, c, first, k):
                gp.dma_start(ix[:], a["idx"][bass.ds(g, 1), :, c].rearrange("o p n -> p (o n)")).then_inc(S["ix_in"], 16)
                gp.wait_ge(S["ix_in"], 16 * k + 16)
                if not first:
                    gp.wait_ge(S["w1_saved"], 16 * k)
                gp.sem_inc(S["gp_passed"], 1)
                ch.enter(3 + per * k)
                for j in range(LUT):
                    dst = dec[:] if j == 0 else pick[:, j % 2]
                    ch.link(nc.gpsimd.tensor_scalar(dst, ix[:], float(j), lut[:, j:j + 1], ALU.is_equal, ALU.mult))
                    if j:
                        ch.link(nc.gpsimd.tensor_tensor(dec[:], dec[:], pick[:, j % 2], ALU.add))
                gp.dma_start(w1_d[bass.ds(g, 1), :, c].rearrange("o p n -> p (o n)"), dec[:]).then_inc(S["w1_saved"], 16)

            for c in range(WPARTS):
                decode(0, c, c == 0, c)
            with gp.Fori(1, NG1) as g:
                for c in range(WPARTS):
                    decode(g, c, False, g * WPARTS + c)

        NU = H1 * NT

        @block.tensor
        def _(pe):
            pe.wait_ge(S["ident"], 2)

            def scores0(i, k):
                n, tile, par, hh, c = 16 * i + k, 2 * i + k // 8, (k // 8) % 2, (k // 4) % 2, k % 4
                if k % 8 == 0:
                    pe.wait_ge(S["q_split"], tile + 1)
                    pe.wait_ge(S["kv_split"], 2 * tile + 1)
                if not (isinstance(n, int) and n < 2):
                    pe.wait_ge(S["exp_done"], n - 1)
                rows = slice(HROWS * hh, HROWS * (hh + 1))
                mm3(bank(k % 2), QH[rows, par, c * P:(c + 1) * P], QL[rows, par, c * P:(c + 1) * P],
                    KH[rows, par], KL[rows, par], True, True).then_inc(S["s_ready"], 1)

            def turn0(i, k):
                n = 16 * i + k
                pe.wait_ge(S["p_ready"], n + 1)
                if not (isinstance(n, int) and n < 2):
                    pe.wait_ge(S["pt_lo"], n - 1)
                for lc in range(4):
                    m = nc.tensor.transpose(bank(2 + k % 2)[:, lc * P:(lc + 1) * P], pr[:, k % 4, lc * P:(lc + 1) * P], idf[:])
                m.then_inc(S["pt_done"], 1)

            def pv0(i, g):
                n = 4 * i + g
                pe.wait_ge(S["kv_split"], 2 * (2 * i + g // 2) + 2)
                pe.wait_ge(S["pt_lo"], 4 * n + 4)
                if not (isinstance(n, int) and n < 2):
                    pe.wait_ge(S["o0_used"], n - 1)
                par = (g // 2) % 2
                for lc in range(4):
                    m = mm3(bank(4 + g % 2), VH[:, par, lc * P:(lc + 1) * P], VL[:, par, lc * P:(lc + 1) * P],
                            PTH[:, g % 2, lc], PTL[:, g % 2, lc], lc == 0, lc == 3)
                m.then_inc(S["pv0_done"], 1)

            def attn0(i, first=False, last=False):
                for k in range(16):
                    if not (last and k >= 14):
                        scores0(i, k + 2)
                    if not (first and k == 0):
                        turn0(i, k - 1)
                    if k % 4 == 2 and not (first and k == 2):
                        pv0(i, k // 4 - 1)

            scores0(0, 0)
            scores0(0, 1)
            attn0(0, first=True)
            with pe.Fori(1, NT // 2 - 1) as i:
                attn0(i)
            attn0(NT // 2 - 1, last=True)
            turn0(NT // 2 - 1, 15)
            pv0(NT // 2 - 1, 3)

            def xt_tile(t, k, s_ready, s_lo, s_done):
                pe.wait_ge(S[s_ready], t + 1)
                if not (isinstance(t, int) and t < 4):
                    pe.wait_ge(S[s_lo], t - 3)
                for c in range(DC):
                    m = nc.tensor.transpose(bank(k)[:, c * P:(c + 1) * P], xn[:, k % 2, c * P:(c + 1) * P], idf[:])
                m.then_inc(S[s_done], 1)

            def xt(s_ready, s_lo, s_done):
                for k in range(4):
                    xt_tile(k, k, s_ready, s_lo, s_done)
                with pe.Fori(1, NT // 4) as i:
                    for k in range(4):
                        xt_tile(4 * i + k, k, s_ready, s_lo, s_done)

            xt("xn_ready", "xt_lo", "xt_done")
            def merge(e, n_used):
                pe.wait_ge(S["w_in"], 64 * (e + 1))
                for c in range(WPARTS):
                    v = n_used + c - 1
                    if not (isinstance(v, int) and v <= 0):
                        pe.wait_ge(S["merged"], v)
                    lhs = lA[:, c * P:(c + 1) * P]
                    nc.tensor.matmul(bank(6 + c % 2), lhs, lB[:, 0 if c < DC else 1], start=True, stop=True) \
                        .then_inc(S["merge_done"], 1)

            def gate_up(g, tt, par, names, cols, first):
                rdy, used, done = names["w_ready"], names["u_used"], names["g_done"]
                if tt == 0:
                    pe.wait_ge(S[rdy], g + 1)
                for j, m_ in enumerate(cols):
                    if not (first and tt == 0):
                        pe.wait_ge(S[used], unit(g, tt, j, cols) - (1 if len(cols) == 2 else 0))
                    for b, off in ((j, 0), (2 + j, GROUP)):
                        for c in range(DC):
                            w = slice(off + j * P, off + j * P + m_)
                            m = mm3(PS[0:m_, b, :], WH[:, par, c, w], WL[:, par, c, w],
                                    XTH[:, c, tt * 512:(tt + 1) * 512], XTL[:, c, tt * 512:(tt + 1) * 512],
                                    c == 0, c == DC - 1)
                    m.then_inc(S[done], 1)

            def down(g, tt, par, names, cols, first):
                pe.wait_ge(S[names["h_ready"]], unit(g, tt, len(cols) - 1, cols) + 1)
                for q in range(4):
                    n = 4 * (g * TT + tt) + q
                    if not (first and tt == 0 and q < 2):
                        pe.wait_ge(S[names["y_added"]], n - 1)
                    for j, m_ in enumerate(cols):
                        m = mm3(bank(4 + q % 2), HH[0:m_, tt % 2, j, q * P:(q + 1) * P], HL[0:m_, tt % 2, j, q * P:(q + 1) * P],
                                WH[0:m_, par, DC + j], WL[0:m_, par, DC + j], j == 0, j == len(cols) - 1)
                    m.then_inc(S[names["y_done"]], 1)

            def group(g, par, names, cols, first=False, merge_next=False):
                gate_up(g, 0, par, names, cols, first)
                gate_up(g, 1, par, names, cols, False)
                down(g, 0, par, names, cols, first)
                gate_up(g, 2, par, names, cols, False)
                down(g, 1, par, names, cols, False)
                if merge_next:
                    merge(g + 1, WPARTS * (g + 1))
                gate_up(g, 3, par, names, cols, False)
                down(g, 2, par, names, cols, False)
                down(g, 3, par, names, cols, False)

            both = [P, P]
            pe.wait_ge(S["router_in"], 48)
            pe.wait_ge(S["o0_used"], 2 * NT)
            for c in range(DC):
                m = nc.tensor.matmul(bank(4)[:, c * E:(c + 1) * E], gA[:, c * P:(c + 1) * P], gB[:], start=True, stop=True)
            m.then_inc(S["gmerge"], 1)
            merge(0, 0)
            pe.wait_ge(S["g_lo"], 1)
            pe.wait_ge(S["xt_lo"], NT)
            for tt in range(TT):
                if tt >= 2:
                    pe.wait_ge(S["lgT_copied"], tt - 1)
                for c in range(DC):
                    m = mm3(bank(2 + tt % 2), gH[:, c], gL[:, c], XTH[:, c, tt * 512:(tt + 1) * 512],
                            XTL[:, c, tt * 512:(tt + 1) * 512], c == 0, c == DC - 1)
                m.then_inc(S["lg_done"], 1)
            pe.wait_ge(S["lgT_copied"], TT)
            for t in range(NT):
                m = nc.tensor.transpose(bank(5)[:, t * E:(t + 1) * E], lgT[:, t * P:(t + 1) * P], idf[0:E, 0:E])
            m.then_inc(S["lgt_done"], 1)

            group(0, 0, MLP0, both, first=True, merge_next=True)
            with pe.Fori(0, E // 2 - 1) as i:
                group(2 * i + 1, 1, MLP0, both, merge_next=True)
                group(2 * i + 2, 0, MLP0, both, merge_next=True)
            group(E - 1, 1, MLP0, both)

            pe.wait_ge(S["y_added"], 4 * TT * E)

            def kv(t, par, first):
                pe.wait_ge(S["c_ready"], t + 1)
                if not first:
                    pe.wait_ge(S["kv_used"], 2 * (t - 1))
                for w in range(2):
                    if first:
                        pe.wait_ge(S["wkv_ready"], w + 1)
                    for c in range(DC):
                        m = mm3(bank(2 * w + par), CH[:, par, c], CL[:, par, c], wH[:, w, c], wL[:, w, c], c == 0, c == DC - 1)
                    m.then_inc(S["kv_done"], 1)

            def kparts(t, par, first):
                pe.wait_ge(S["kp_ready"], t + 1)
                if not first:
                    pe.wait_ge(S["kt_out"], t)
                for k in range(3):
                    o = bank(4 + k).bitcast(BF16)
                    for c in range(DC):
                        m = nc.tensor.transpose(o[:, c * P:(c + 1) * P], kp[:, par, k, c * P:(c + 1) * P], idb[:])
                m.then_inc(S["kt_done"], 1)

            kv(0, 0, True)
            kv(1, 1, True)
            kparts(0, 0, True)
            with pe.Fori(1, NT // 2) as i:
                kv(2 * i, 0, False)
                kparts(2 * i - 1, 1, False)
                kv(2 * i + 1, 1, False)
                kparts(2 * i, 0, False)
            kparts(NT - 1, 1, False)
            pe.wait_ge(S["vmx_ready"], NT)
            for c in range(DC):
                m = nc.tensor.transpose(bank(7)[:, c * P:(c + 1) * P], vmx[:, c * P:(c + 1) * P], idf[:])
            m.then_inc(S["vt_done"], 1)
            pe.wait_ge(S["vdg_ready"], DC)
            for c in range(DC):
                m = nc.tensor.matmul(bank(7)[:, c * P:(c + 1) * P], ones[:], vdg[:, c], start=True, stop=True)
            m.then_inc(S["svb_done"], 1)

            pe.wait_ge(S["kv_used"], 2 * NT)
            pe.wait_ge(S["wq_ready"], 1)
            pe.wait_ge(S["kt_out"], NT)

            def qx(t, par, first):
                pe.wait_ge(S["qn_ready"], t + 1)
                if not first:
                    pe.wait_ge(S["qx_ready"], t - 1)
                for c in range(DC):
                    m = nc.tensor.transpose(bank(par)[:, c * P:(c + 1) * P], CT[:, par, c * P:(c + 1) * P], idf[:])
                m.then_inc(S["qx_done"], 1)

            def qmm(t, par, first):
                pe.wait_ge(S["qx_ready"], t + 1)
                if not first:
                    pe.wait_ge(S["q_used"], t - 1)
                for c in range(DC):
                    m = mm3(bank(2 + par), CH[:, par, c], CL[:, par, c], wH[:, 0, c], wL[:, 0, c], c == 0, c == DC - 1)
                m.then_inc(S["q_done"], 1)

            def qturn(t, par, first):
                pe.wait_ge(S["qp_ready"], t + 1)
                if not first:
                    pe.wait_ge(S["qt_out"], t)
                o = bank(4).bitcast(BF16)
                for c in range(DC):
                    m = nc.tensor.transpose(o[:, c * P:(c + 1) * P], kp[:, par, 0, c * P:(c + 1) * P], idb[:])
                m.then_inc(S["qt_done"], 1)

            qx(0, 0, True)
            qx(1, 1, True)
            qmm(0, 0, True)
            with pe.Fori(1, NT // 2) as i:
                qx(2 * i, 0, False)
                qmm(2 * i - 1, 1, False)
                qturn(2 * i - 2, 0, False)
                qx(2 * i + 1, 1, False)
                qmm(2 * i, 0, False)
                qturn(2 * i - 1, 1, False)
            qmm(NT - 1, 1, False)
            qturn(NT - 2, 0, False)
            qturn(NT - 1, 1, False)

            pe.wait_ge(S["qt_out"], NT)
            pe.wait_ge(S["v_ready"], 1)

            def scores(u, k, half, first=False):
                queries = (u % 32) * P
                keys = ((u // NT) % 2) * T + half * 1024
                if not isinstance(u, int):
                    queries, keys = pe.snap(queries), pe.snap(keys)
                if half == 0:
                    pe.wait_ge(S["head_in"], 96 * (u // NT) + 96)
                if not first:
                    pe.wait_ge(S["t_exp"], 2 * u + half - 2)
                slot = (2 * k + half) % 3
                for b in range(2):
                    m = nc.tensor.matmul(bank(2 * slot + b), QS[0:KROWS].rearrange("p a n -> p (a n)")[:, bass.ds(queries, P)],
                                         KS[0:KROWS].rearrange("p a n -> p (a n)")[:, bass.ds(keys + b * 512, 512)],
                                         start=True, stop=True)
                m.then_inc(S["t_half"], 1)

            def turn(u, k, half, first=False):
                pe.wait_ge(S["t_exp"], 2 * u + half + 1)
                if not first:
                    pe.wait_ge(S[f"pt{half}_out"], u)
                    if half == 1:
                        pe.wait_ge(S["pv_used"], u)
                o = bank(6 + half).bitcast(BF16)
                for c in range(8):
                    m = nc.tensor.transpose(o[:, c * P:(c + 1) * P],
                                            ei[:, k, half * 1024 + c * P:half * 1024 + (c + 1) * P].bitcast(BF16), idb[:])
                m.then_inc(S["e_turned"], 1)

            def pv(u, k):
                pe.wait_ge(S[f"vh_in{k}"], 16 * (u // NT) + 16)
                pe.wait_ge(S["pt0_out"], u + 1)
                pe.wait_ge(S["pt1_out"], u + 1)
                for kt in range(NT):
                    m = nc.tensor.matmul(bank(7)[:, 0:HD], pt[:, k, kt * P:(kt + 1) * P],
                                         VK[:, k, kt], start=(kt == 0), stop=(kt == NT - 1))
                m.then_inc(S["pv_done"], 1)

            def step(u, k, first=False, ahead=2):
                if ahead >= 1:
                    scores(u + 1, (k + 1) % 3, 1)
                turn(u, k, 0, first)
                if not first:
                    pv(u - 1, (k + 2) % 3)
                if ahead >= 2:
                    scores(u + 2, (k + 2) % 3, 0)
                turn(u, k, 1, first)

            scores(0, 0, 0, True)
            scores(0, 0, 1, True)
            scores(1, 1, 0, True)
            step(0, 0, first=True)
            with pe.Fori(0, (NU - 4) // 3) as v:
                for k in range(3):
                    step(3 * v + 1 + k, (1 + k) % 3)
            for u in range(NU - 3, NU):
                step(u, u % 3, ahead=NU - 1 - u)
            pv(NU - 1, (NU - 1) % 3)

            pe.wait_ge(S["wp_ready"], 1)
            pe.wait_ge(S["pv_used"], NU)

            def oturn(t, par, first):
                pe.wait_ge(S["ao_staged"], t + 1)
                if not first:
                    pe.wait_ge(S["ao_ready"], t - 1)
                for c in range(DC):
                    m = nc.tensor.transpose(bank(par)[:, c * P:(c + 1) * P], CT[:, par, c * P:(c + 1) * P], idf[:])
                m.then_inc(S["ao_t"], 1)

            def omm(t, par, first):
                pe.wait_ge(S["ao_ready"], t + 1)
                if not (isinstance(t, int) and t < 2):
                    pe.wait_ge(S["o_used"], t - 1)
                for c in range(DC):
                    m = mm3(bank(2 + par), CH[:, par, c], CL[:, par, c], wH[:, 1, c], wL[:, 1, c], c == 0, c == DC - 1)
                m.then_inc(S["o_done"], 1)

            oturn(0, 0, True)
            oturn(1, 1, True)
            omm(0, 0, True)
            with pe.Fori(1, NT // 2) as i:
                oturn(2 * i, 0, False)
                omm(2 * i - 1, 1, False)
                oturn(2 * i + 1, 1, False)
                omm(2 * i, 0, False)
            omm(NT - 1, 1, False)
            pe.wait_ge(S["o_used"], NT)
            xt("xn1_ready", "xt1_lo", "xt1_done")
            pe.wait_ge(S["xt1_lo"], NT)
            group(0, 0, MLP1, both, first=True)
            with pe.Fori(0, (NG1 - 2) // 2) as i:
                group(2 * i + 1, 1, MLP1, both)
                group(2 * i + 2, 0, MLP1, both)
            group(NG1 - 1, 1, MLP1, [LAST])

        @block.scalar
        def _(act):
            ln_root(act, 1)

            def k_hi(i, par, first):
                act.wait_ge(S[f"kv_in{par}"], 32 * (i + 1))
                if not first:
                    act.wait_ge(S["s_ready"], 8 * (2 * i + par - 1))
                nc.scalar.copy(KH[:, par], Kf[:, par]).then_inc(S["kv_hi"], 1)

            def v_hi(i, par, first):
                if not first:
                    act.wait_ge(S["pv0_done"], 2 * (2 * i + par) - 2)
                nc.scalar.copy(VH[:, par], Vf[:, par]).then_inc(S["kv_hi"], 1)

            def exp0(i, k):
                n = 16 * i + k
                act.wait_ge(S["nmax_ready"], n + 1)
                if not (isinstance(n, int) and n < 4):
                    act.wait_ge(S["pt_done"], n - 3)
                nc.scalar.activation(pr[:, k % 4], bank(k % 2), ACT.Exp, bias=nmx[:, k % 2:k % 2 + 1],
                                     accum_out=psm[:, k % 2:k % 2 + 1]).then_inc(S["exp_done"], 1)

            def norm(i, k):
                act.wait_ge(S["r_ready"], 16 * i + k + 1)
                nc.scalar.activation(pr[:, k % 4], pr[:, k % 4], ACT.Copy, scale=rsm[:, k % 2:k % 2 + 1]).then_inc(S["p_ready"], 1)

            def pt_hi(i, k):
                n, g, c = 16 * i + k, (k // 4) % 2, k % 4
                act.wait_ge(S["pt_done"], n + 1)
                gg = 4 * i + k // 4
                if c == 0 and not (isinstance(gg, int) and gg < 2):
                    act.wait_ge(S["pv0_done"], gg - 1)
                nc.scalar.copy(PTH[:, g, :, c * P:(c + 1) * P], bank(2 + k % 2).rearrange("p (l q) -> p l q", l=4)).then_inc(S["pt_hi"], 1)

            def attn0(i, first=False, last=False):
                for k in range(16):
                    exp0(i, k)
                    if not (first and k == 0):
                        norm(i, k - 1)
                    if not (first and k < 2):
                        pt_hi(i, k - 2)
                    ahead = (i, 1) if k < 8 else (i + 1, 0)
                    if not (first and k < 8 or last and k >= 8):
                        if k % 8 == 1:
                            k_hi(*ahead, False)
                        if k % 8 == 4:
                            v_hi(*ahead, False)

            for par in range(2):
                k_hi(0, par, True)
                v_hi(0, par, True)
            attn0(0, first=True)
            with act.Fori(1, NT // 2 - 1) as i:
                attn0(i)
            attn0(NT // 2 - 1, last=True)
            norm(NT // 2 - 1, 15)
            pt_hi(NT // 2 - 1, 14)
            pt_hi(NT // 2 - 1, 15)

            def xt(s_done, s_hi):
                def tile(t, k):
                    act.wait_ge(S[s_done], t + 1)
                    nc.scalar.copy(XTH[:, :, bass.ds(t * P, P)], bank(k).rearrange("p (c q) -> p c q", c=DC)).then_inc(S[s_hi], 1)
                with act.Fori(0, NT // 4) as i:
                    for k in range(4):
                        tile(4 * i + k, k)

            ln_root(act, 2)
            xt("xt_done", "xt_hi")
            act.wait_ge(S["gW_ready"], 1)
            nc.scalar.copy(gH[:], gF[:]).then_inc(S["g_hi"], 1)

            def weights_hi(g, par, s_in, v, s_free, n_free, s_out):
                act.wait_ge(S[s_in], v)
                if n_free is not None:
                    act.wait_ge(S[s_free], n_free)
                nc.scalar.copy(WH[:, par], WR[:]).then_inc(S[s_out], 1)

            def hidden(g, tt, names, cols, first):
                for j, m_ in enumerate(cols):
                    n = unit(g, tt, j, cols)
                    act.wait_ge(S[names["g_done"]], n + 1)
                    if not (first and tt == 0):
                        act.wait_ge(S[names["u_used"]], n - (1 if len(cols) == 2 else 0))
                    nc.scalar.activation(sg[0:m_, j], PS[0:m_, j, :], ACT.Silu).then_inc(S[names["silu"]], 1)
                    act.wait_ge(S[names["u_used"]], n + 1)
                    if not (first and tt < 2):
                        act.wait_ge(S[names["y_done"]], 4 * (g * TT + tt) - 4)
                    nc.scalar.copy(HH[0:m_, tt % 2, j], HF[0:m_]).then_inc(S[names["h_hi"]], 1)

            def group(g, par, names, cols, first=False, nxt=None):
                hidden(g, 0, names, cols, first)
                hidden(g, 1, names, cols, first)
                hidden(g, 2, names, cols, False)
                if nxt:
                    nxt(g + 1, 1 - par, first)
                hidden(g, 3, names, cols, False)

            def next0(g, par, first):
                weights_hi(g, par, "merged", WPARTS * (g + 1), "y_done", None if first else 4 * TT * (g - 1), "w_hi")

            def next1(g, par, first):
                weights_hi(g, par, "w1_in", 16 * (g + 1), "y1_done", None if first else 4 * TT * (g - 1), "w1_hi")

            both = [P, P]
            next0(0, 0, True)
            for tt in range(TT):
                act.wait_ge(S["lg_done"], tt + 1)
                nc.scalar.copy(lgT[:, tt * 512:(tt + 1) * 512], PS[0:E, 2 + tt % 2, :]).then_inc(S["lgT_copied"], 1)
            act.wait_ge(S["rt_e"], 1)
            nc.scalar.activation(rt[:, 1], rt[:, 0], ACT.Exp).then_inc(S["rexp"], 1)
            act.wait_ge(S["rt_done"], 1)
            group(0, 0, MLP0, both, True, next0)
            with act.Fori(0, E // 2 - 1) as i:
                group(2 * i + 1, 1, MLP0, both, False, next0)
                group(2 * i + 2, 0, MLP0, both, False, next0)
            group(E - 1, 1, MLP0, both)

            act.wait_ge(S["wk_in"], 16)
            nc.scalar.copy(wH[:, 0], wr[:]).then_inc(S["wkv_hi"], 1)

            def copy_parts(t, par, s_done, s_saved, n_saved, parts, first_bank, s_out):
                act.wait_ge(S[s_done], t + 1)
                if n_saved is not None:
                    act.wait_ge(S[s_saved], n_saved)
                for k in range(parts):
                    m = nc.scalar.copy(kts[:, par, k], bank(first_bank + k).bitcast(BF16)[:, 0:D])
                m.then_inc(S[s_out], 1)

            def c_hi(i, par, first):
                act.wait_ge(S[f"c_in{par}"], 16 * (i + 1))
                if not first:
                    act.wait_ge(S["kv_done"], 2 * (2 * i + par - 1))
                nc.scalar.copy(CH[:, par].rearrange("p c n -> p (c n)"), CT[:, par]).then_inc(S["c_hi"], 1)

            c_hi(0, 0, True)
            act.wait_ge(S["wv_in"], 16)
            nc.scalar.copy(wH[:, 1], VF[:, NT - DC:NT]).then_inc(S["wkv_hi"], 1)
            c_hi(0, 1, True)
            for par in range(2):
                c_hi(1, par, False)
                copy_parts(par, par, "kt_done", None, None, 3, 4, "kt_out")
            with act.Fori(1, NT // 2 - 1) as i:
                for par in range(2):
                    c_hi(i + 1, par, False)
                    copy_parts(2 * i + par, par, "kt_done", f"kt_saved{par}", 48 * i, 3, 4, "kt_out")
            for par in range(2):
                copy_parts(NT - 2 + par, par, "kt_done", f"kt_saved{par}", 48 * (NT // 2 - 1), 3, 4, "kt_out")

            ln_root(act, 3)
            act.wait_ge(S["wq_in"], 16)
            act.wait_ge(S["kv_done"], 2 * NT)
            nc.scalar.copy(wH[:, 0], wr[:]).then_inc(S["wq_hi"], 1)

            def x_hi(t, par, s_done, s_hi, s_free, n_free):
                act.wait_ge(S[s_done], t + 1)
                if n_free is not None:
                    act.wait_ge(S[s_free], n_free)
                nc.scalar.copy(CH[:, par].rearrange("p c n -> p (c n)"), bank(par)).then_inc(S[s_hi], 1)

            x_hi(0, 0, "qx_done", "qx_hi", None, None)
            x_hi(1, 1, "qx_done", "qx_hi", None, None)
            for par in range(2):
                x_hi(2 + par, par, "qx_done", "qx_hi", "q_done", 1 + par)
                copy_parts(par, par, "qt_done", f"kt_saved{par}", 48 * (NT // 2), 1, 4, "qt_out")
            with act.Fori(2, NT // 2) as i:
                for par in range(2):
                    x_hi(2 * i + par, par, "qx_done", "qx_hi", "q_done", 2 * i + par - 1)
                    copy_parts(2 * i - 2 + par, par, "qt_done", f"qt_saved{par}", 16 * (i - 1), 1, 4, "qt_out")
            for par in range(2):
                copy_parts(NT - 2 + par, par, "qt_done", f"qt_saved{par}", 16 * (NT // 2 - 1), 1, 4, "qt_out")

            act.wait_ge(S["wp_in"], 16)
            nc.scalar.copy(wH[:, 1], wr[:]).then_inc(S["wp_hi"], 1)

            def exps(u, k, half, first=False):
                act.wait_ge(S["t_max"], u + 1)
                if not first:
                    act.wait_ge(S["e_turned"], 2 * u - 5 + half)
                    act.wait_ge(S["pv_used"], u - 2)
                slot = (2 * k + half) % 3
                nc.scalar.activation(ei[:, k, half * 1024:(half + 1) * 1024],
                                     PS[:, 2 * slot:2 * slot + 2, :].rearrange("p b n -> p (b n)"), ACT.Exp,
                                     bias=tb[:, k:k + 1], scale=sqc[:, k:k + 1],
                                     accum_out=esm[:, k, half:half + 1]).then_inc(S["t_exp"], 1)

            def query_scale(u, k):
                nc.scalar.copy(sqc[:, k:k + 1], SQ[:].rearrange("p h t -> p (h t)")[:, bass.ds(u, 1)]).then_inc(S["sqc_ready"], 1)

            def step(u, k, first=False, next_first=False, last=False, scale=True):
                exps(u, k, 1, first)
                act.wait_ge(S["e_turned"], 2 * u + 1)
                if not first:
                    act.wait_ge(S["pv_done"], u - 2)
                nc.scalar.copy(pt[:, k, 0:1024], bank(6).bitcast(I16)).then_inc(S["pt0_out"], 1)
                if scale:
                    if not first:
                        act.wait_ge(S["t_exp"], 2 * u)
                    query_scale(u + 2, (k + 2) % 3)
                if not last:
                    exps(u + 1, (k + 1) % 3, 0, next_first)

            act.wait_ge(S["v_ready"], 1)
            query_scale(0, 0)
            query_scale(1, 1)
            exps(0, 0, 0, True)
            step(0, 0, True, True)
            step(1, 1, True, True)
            step(2, 2, True, False)
            step(3, 0)
            with act.Fori(1, (NU - 4) // 3) as v:
                for k in range(3):
                    step(3 * v + 1 + k, (1 + k) % 3)
            for u in range(NU - 3, NU):
                step(u, u % 3, last=(u == NU - 1), scale=(u < NU - 2))

            x_hi(0, 0, "ao_t", "ao_hi", None, None)
            x_hi(1, 1, "ao_t", "ao_hi", None, None)
            with act.Fori(1, NT // 2) as i:
                for par in range(2):
                    x_hi(2 * i + par, par, "ao_t", "ao_hi", "o_done", 2 * i + par - 1)
            ln_root(act, 4)
            next1(0, 0, True)
            xt("xt1_done", "xt1_hi")
            group(0, 0, MLP1, both, True, next1)
            with act.Fori(0, (NG1 - 2) // 2) as i:
                group(2 * i + 1, 1, MLP1, both, False, next1)
                group(2 * i + 2, 0, MLP1, both, False, next1)
            group(NG1 - 1, 1, MLP1, [LAST])

        @block.vector
        def _(dve):
            ch = Chain(dve, S["dve_own"])
            total = [0]

            def straight():
                ch.enter(total[0])

            def ended(loops=1):
                total[0] += loops * ch.n

            straight()
            for t in range(NT):
                if t % 4 == 0:
                    dve.wait_ge(S[f"x_in{t // 4}"], 16)
                m = nc.vector.bn_stats(st[:, t], X[:, t])
            ch.link(m)
            ln_finish(dve, ch)
            ln_invert(dve, ch, 1, scale=1.0 / math.sqrt(HROWS))

            def q_norm(i, par, first):
                t = 2 * i + par
                if not (isinstance(t, int) and t == 0):
                    dve.wait_ge(S["q_split"], t)
                ch.link(nc.vector.tensor_scalar(Qf[:], X[:, bass.ds(t, 1)].rearrange("p o d -> p (o d)"),
                                                mu[:, bass.ds(t, 1)], rstd[:, bass.ds(t, 1)], ALU.subtract, ALU.mult))

            def q_hi(i, par, first):
                if not first:
                    dve.wait_ge(S["s_ready"], 8 * (2 * i + par - 1))
                ch.link(nc.vector.tensor_copy(QH[:, par], Qf[:]))

            def q_lo(i, par, first):
                nc.vector.tensor_tensor(QL[:, par], Qf[:], QH[:, par].bitcast(F32), ALU.subtract).then_inc(S["q_split"], 1)

            def k_lo(i, par, first):
                dve.wait_ge(S["kv_hi"], 2 * (2 * i + par) + 1)
                nc.vector.tensor_tensor(KL[:, par], Kf[:, par], KH[:, par].bitcast(F32), ALU.subtract).then_inc(S["kv_split"], 1)

            def v_lo(i, par, first):
                dve.wait_ge(S["kv_hi"], 2 * (2 * i + par) + 2)
                nc.vector.tensor_tensor(VL[:, par], Vf[:, par], VH[:, par].bitcast(F32), ALU.subtract).then_inc(S["kv_split"], 1)

            PREP = {0: q_norm, 1: q_hi, 2: q_lo, 4: k_lo, 6: v_lo}

            def rowmax(i, k):
                n = 16 * i + k
                dve.wait_ge(S["s_ready"], n + 1)
                nc.vector.tensor_reduce(nmx[:, k % 2:k % 2 + 1], bank(k % 2), AX.X, ALU.max, negate=True).then_inc(S["nmax_ready"], 1)

            def inverse(i, k):
                n = 16 * i + k
                dve.wait_ge(S["exp_done"], n + 1)
                if not (isinstance(n, int) and n < 2):
                    dve.wait_ge(S["p_ready"], n - 1)
                nc.vector.reciprocal(rsm[:, k % 2:k % 2 + 1], psm[:, k % 2:k % 2 + 1]).then_inc(S["r_ready"], 1)

            def pt_lo(i, k):
                n, g, c = 16 * i + k, (k // 4) % 2, k % 4
                dve.wait_ge(S["pt_hi"], n + 1)
                o = (slice(None), g, slice(None), slice(c * P, (c + 1) * P))
                nc.vector.tensor_tensor(PTL[o], bank(2 + k % 2).rearrange("p (l q) -> p l q", l=4), PTH[o].bitcast(F32),
                                        ALU.subtract).then_inc(S["pt_lo"], 1)

            def add0(i, g):
                t, rows = 2 * i + g // 2, slice(HROWS * (g % 2), HROWS * (g % 2 + 1))
                n = 4 * i + g
                dve.wait_ge(S["pv0_done"], n + 1)
                x = X[rows, bass.ds(t, 1)].rearrange("p o d -> p (o d)")
                m = nc.vector.scalar_tensor_tensor(out=x, in0=PS[rows, 4 + g % 2, :], scalar=gam[rows], in1=x,
                                                   op0=ALU.mult, op1=ALU.add)
                m.then_inc(S["o0_used"], 1)
                if g % 2:
                    dve.wait_ge(S["o0_used"], n + 1)
                    nc.vector.bn_stats(st[:, bass.ds(t, 1)].rearrange("p o s -> p (o s)"),
                                       X[:, bass.ds(t, 1)].rearrange("p o d -> p (o d)")).then_inc(S["stats0"], 1)

            def attn0(i, first=False, last=False):
                for k in range(16):
                    if not (last and k == 15):
                        rowmax(i, k + 1)
                    inverse(i, k)
                    if not (first and k < 2):
                        pt_lo(i, k - 2)
                    if k % 4 == 3 and not (first and k == 3):
                        add0(i, k // 4 - 1)
                    if k % 8 in PREP and not (first and k < 8 or last and k >= 8):
                        PREP[k % 8](*((i, 1) if k < 8 else (i + 1, 0)), False)

            for par in range(2):
                for part in PREP.values():
                    part(0, par, True)
            dve.wait_ge(S["gam_in"], 16)
            rowmax(0, 0)
            attn0(0, first=True)
            ended()
            per = 4
            with dve.Fori(1, NT // 2 - 1) as i:
                ch.enter(total[0] + per * (i - 1))
                attn0(i)
                assert ch.n == per
            total[0] += per * (NT // 2 - 2)
            straight()
            attn0(NT // 2 - 1, last=True)
            pt_lo(NT // 2 - 1, 14)
            pt_lo(NT // 2 - 1, 15)
            add0(NT // 2 - 1, 3)

            def flat(x, t):
                return x[:, bass.ds(t, 1)].rearrange("p o d -> p (o d)")

            dve.wait_ge(S["stats0"], NT)
            ln_finish(dve, ch)
            ln_invert(dve, ch, 2)
            ended()

            def xt(s_ready, s_done, s_hi, s_lo):
                def tile(t, k, first):
                    if not first:
                        dve.wait_ge(S[s_done], t - 1)
                    nc.vector.tensor_scalar(xn[:, k], flat(X, t), mu[:, bass.ds(t, 1)], rstd[:, bass.ds(t, 1)],
                                            ALU.subtract, ALU.mult).then_inc(S[s_ready], 1)

                def low(t, k):
                    dve.wait_ge(S[s_hi], t + 1)
                    nc.vector.tensor_tensor(XTL[:, :, bass.ds(t * P, P)], bank(k).rearrange("p (c q) -> p c q", c=DC),
                                            XTH[:, :, bass.ds(t * P, P)].bitcast(F32), ALU.subtract).then_inc(S[s_lo], 1)
                tile(0, 0, True)
                tile(1, 1, True)
                with dve.Fori(0, NT // 4 - 1) as i:
                    for k in range(4):
                        tile(4 * i + k + 2, k % 2, False)
                        low(4 * i + k, k)
                for k in range(4):
                    if k < 2:
                        tile(NT - 2 + k, k, False)
                    low(NT - 4 + k, k)

            xt("xn_ready", "xt_done", "xt_hi", "xt_lo")
            straight()
            dve.wait_ge(S["router_in"], 48)
            ch.link(nc.vector.memset(gF[:], 0.0))
            dve.wait_ge(S["gmerge"], 1)
            nc.vector.scalar_tensor_tensor(out=gF[:, :, 0:E], in0=bank(4)[:, 0:DC * E].rearrange("p (c e) -> p c e", c=DC),
                                           scalar=2.0, in1=gW[:], op0=ALU.mult, op1=ALU.add).then_inc(S["gW_ready"], 1)
            dve.wait_ge(S["g_hi"], 1)
            nc.vector.tensor_tensor(gL[:], gF[:], gH[:].bitcast(F32), ALU.subtract).then_inc(S["g_lo"], 1)
            ended()

            def merged0(g, par, first):
                for c in range(WPARTS):
                    v = WPARTS * g + c + 1
                    dve.wait_ge(S["merge_done"], v)
                    nc.vector.scalar_tensor_tensor(out=WR[:, c], in0=bank(6 + c % 2), scalar=2.0, in1=WR[:, c],
                                                   op0=ALU.mult, op1=ALU.add).then_inc(S["merged"], 1)
                low_weights(g, par, "w_hi", "w_ready")

            def low_weights(g, par, s_hi, s_out):
                dve.wait_ge(S[s_hi], g + 1)
                nc.vector.tensor_tensor(WL[:, par], WR[:], WH[:, par].bitcast(F32), ALU.subtract).then_inc(S[s_out], 1)

            def merged1(g, par, first):
                low_weights(g, par, "w1_hi", "w1_ready")

            def hidden(g, tt, names, cols, first):
                for j, m_ in enumerate(cols):
                    n = unit(g, tt, j, cols)
                    dve.wait_ge(S[names["silu"]], n + 1)
                    if not (first and tt == 0 and j == 0):
                        dve.wait_ge(S[names["h_ready"]], n)
                    nc.vector.tensor_tensor(HF[0:m_], sg[0:m_, j], PS[0:m_, 2 + j, :], ALU.mult).then_inc(S[names["u_used"]], 1)
                    dve.wait_ge(S[names["h_hi"]], n + 1)
                    nc.vector.tensor_tensor(HL[0:m_, tt % 2, j], HF[0:m_], HH[0:m_, tt % 2, j].bitcast(F32),
                                            ALU.subtract).then_inc(S[names["h_ready"]], 1)

            def add(g, tt, names, weighted):
                for q in range(4):
                    n, t = 4 * (g * TT + tt) + q, 4 * tt + q
                    dve.wait_ge(S[names["y_done"]], n + 1)
                    if weighted:
                        w = W8[:, t, bass.ds(g, 1)]
                        m = nc.vector.scalar_tensor_tensor(out=X[:, t], in0=bank(4 + q % 2), scalar=w, in1=X[:, t],
                                                           op0=ALU.mult, op1=ALU.add)
                    else:
                        m = nc.vector.tensor_tensor(X[:, t], bank(4 + q % 2), X[:, t], ALU.add)
                    m.then_inc(S[names["y_added"]], 1)

            def measure(g, tt, names):
                dve.wait_ge(S[names["y_added"]], 4 * (g * TT + tt) + 4)
                for q in range(4):
                    m = nc.vector.bn_stats(st[:, 4 * tt + q], X[:, 4 * tt + q])
                return m

            def group(g, par, names, cols, first=False, nxt=None, weighted=False, measured=False):
                hidden(g, 0, names, cols, first)
                hidden(g, 1, names, cols, first)
                add(g, 0, names, weighted)
                hidden(g, 2, names, cols, False)
                add(g, 1, names, weighted)
                if nxt:
                    nxt(g + 1, 1 - par, first)
                hidden(g, 3, names, cols, False)
                if measured:
                    measure(g, 0, names)
                add(g, 2, names, weighted)
                if measured:
                    measure(g, 1, names)
                add(g, 3, names, weighted)
                if measured:
                    measure(g, 2, names)
                    return measure(g, 3, names)

            both = [P, P]
            merged0(0, 0, True)
            straight()
            for e in range(E):
                m = nc.vector.memset(rev[:, :, e:e + 1], float(E - e))
            ch.link(m)
            dve.wait_ge(S["lgt_done"], 1)
            ch.link(nc.vector.tensor_copy(rt[:, 2], bank(5)[:, 0:NT * E].rearrange("p (t e) -> p t e", e=E)))

            def wide(x):
                return x.rearrange("p (t o) -> p t o", o=1).broadcast_to([P, NT, E])

            ch.link(nc.vector.tensor_reduce(rm[:, 0], rt[:, 2], AX.X, ALU.max))
            nc.vector.tensor_tensor(rt[:, 0], rt[:, 2], wide(rm[:, 0]), ALU.subtract).then_inc(S["rt_e"], 1)
            dve.wait_ge(S["rexp"], 1)

            def largest(src, mask, m, k):
                ch.link(nc.vector.tensor_reduce(rm[:, m], src, AX.X, ALU.max))
                ch.link(nc.vector.tensor_tensor(mask, src, wide(rm[:, m]), ALU.is_equal))
                ch.link(nc.vector.tensor_tensor(mask, mask, rev[:], ALU.mult))
                ch.link(nc.vector.tensor_reduce(rm[:, k], mask, AX.X, ALU.max))
                ch.link(nc.vector.tensor_tensor(mask, mask, wide(rm[:, k]), ALU.is_equal))

            largest(rt[:, 1], rt[:, 3], 0, 1)
            ch.link(nc.vector.scalar_tensor_tensor(out=rt[:, 4], in0=rt[:, 3], scalar=-2.0, in1=rt[:, 1], op0=ALU.mult, op1=ALU.add))
            largest(rt[:, 4], rt[:, 5], 2, 3)
            ch.link(nc.vector.tensor_tensor(rm[:, 1], rm[:, 0], rm[:, 2], ALU.add))
            ch.link(nc.vector.reciprocal(rm[:, 3], rm[:, 1]))
            ch.link(nc.vector.tensor_tensor(rt[:, 3], rt[:, 3], rt[:, 5], ALU.add))
            ch.link(nc.vector.tensor_tensor(rt[:, 4], rt[:, 3], rt[:, 1], ALU.mult))
            nc.vector.tensor_tensor(W8[:], rt[:, 4], wide(rm[:, 3]), ALU.mult).then_inc(S["rt_done"], 1)
            dve.wait_ge(S["rt_done"], 1)
            ended()

            group(0, 0, MLP0, both, True, merged0, True)
            with dve.Fori(0, E // 2 - 1) as i:
                group(2 * i + 1, 1, MLP0, both, False, merged0, True)
                group(2 * i + 2, 0, MLP0, both, False, merged0, True)
            straight()
            ch.link(group(E - 1, 1, MLP0, both, False, None, True, measured=True))
            ln_finish(dve, ch)

            ended()
            dve.wait_ge(S["wkv_hi"], 1)
            nc.vector.tensor_tensor(wL[:, 0], wr[:], wH[:, 0].bitcast(F32), ALU.subtract).then_inc(S["wkv_ready"], 1)

            def c_lo(t, par, first):
                dve.wait_ge(S["c_hi"], t + 1)
                nc.vector.tensor_tensor(CL[:, par].rearrange("p c n -> p (c n)"), CT[:, par],
                                        CH[:, par].rearrange("p c n -> p (c n)").bitcast(F32), ALU.subtract).then_inc(S["c_ready"], 1)

            def heads(x):
                return x.rearrange("p (h d) -> p h d", d=HD)

            def by_head(x):
                return x.rearrange("p (h o) -> p h o", o=1).broadcast_to([P, H1, HD])

            def quantise(src, scale, s_dst):
                ch.link(nc.vector.tensor_reduce(ksc[:, 0], heads(src), AX.X, ALU.max, apply_absolute_value=True))
                ch.link(nc.vector.tensor_scalar(s_dst, ksc[:, 0], scale / QMAX, SMIN, ALU.mult, ALU.max))
                ch.link(nc.vector.reciprocal(ksc[:, 1], s_dst))
                if scale != 1.0:
                    ch.link(nc.vector.tensor_scalar(ksc[:, 1], ksc[:, 1], scale, None, ALU.mult))
                ch.link(nc.vector.tensor_tensor(heads(ki[:]), heads(src), by_head(ksc[:, 1]), ALU.mult))

            def kv(t, par, first, first_tile):
                dve.wait_ge(S["kv_done"], 2 * t + 1)
                nc.vector.tensor_tensor(kf[:], bank(par), bkv[:, 0:D], ALU.add).then_inc(S["kv_used"], 1)
                dve.wait_ge(S["kv_used"], 2 * t + 1)
                quantise(kf[:], 1.0, ksc[:, 2])
                ch.link(nc.vector.tensor_tensor(heads(kd[:]), heads(ki[:]), by_head(ksc[:, 2]), ALU.mult))
                if not first:
                    dve.wait_ge(S["kt_done"], t - 1)
                ch.link(nc.vector.tensor_copy(kp[:, par, 0], kd[:]))
                ch.link(nc.vector.tensor_tensor(kf[:], kd[:], kp[:, par, 0], ALU.subtract))
                ch.link(nc.vector.tensor_copy(kp[:, par, 1], kf[:]))
                nc.vector.tensor_tensor(kp[:, par, 2], kf[:], kp[:, par, 1], ALU.subtract).then_inc(S["kp_ready"], 1)
                dve.wait_ge(S["kp_ready"], t + 1)
                dve.wait_ge(S["kv_done"], 2 * t + 2)
                nc.vector.tensor_tensor(flat(VF, t), bank(2 + par), bkv[:, D:2 * D], ALU.add).then_inc(S["kv_used"], 1)
                dve.wait_ge(S["kv_used"], 2 * t + 2)
                size = vmx if first_tile else kd
                m = nc.vector.scalar_tensor_tensor(out=size[:], in0=flat(VF, t), scalar=-1.0, in1=flat(VF, t),
                                                   op0=ALU.mult, op1=ALU.max)
                if not first_tile:
                    ch.link(m)
                    m = nc.vector.tensor_tensor(vmx[:], vmx[:], kd[:], ALU.max)
                m.then_inc(S["vmx_ready"], 1)
                dve.wait_ge(S["vmx_ready"], t + 1)

            straight()
            c_lo(0, 0, True)
            dve.wait_ge(S["wkv_hi"], 2)
            nc.vector.tensor_tensor(wL[:, 1], VF[:, NT - DC:NT], wH[:, 1].bitcast(F32), ALU.subtract).then_inc(S["wkv_ready"], 1)
            c_lo(1, 1, True)
            dve.wait_ge(S["bias_in"], 48)
            kv(0, 0, True, True)
            c_lo(2, 0, False)
            kv(1, 1, True, False)
            c_lo(3, 1, False)
            ended()
            def kv_pair(i, more):
                for par in range(2):
                    kv(2 * i + par, par, False, False)
                    if more:
                        c_lo(2 * i + par + 2, par, False)
            per = 18
            with dve.Fori(1, NT // 2 - 1) as i:
                ch.enter(total[0] + per * (i - 1))
                kv_pair(i, True)
                assert ch.n == per, ch.n
            total[0] += per * (NT // 2 - 2)
            straight()
            kv_pair(NT // 2 - 1, False)
            dve.wait_ge(S["vt_done"], 1)
            ch.link(nc.vector.tensor_reduce(vsc[:, 0], bank(7).rearrange("p (c n) -> p c n", c=DC), AX.X, ALU.max,
                                            apply_absolute_value=True))
            ch.link(nc.vector.tensor_scalar(vsc[:, 1], vsc[:, 0], 1.0 / QMAX, SMIN, ALU.mult, ALU.max))
            for c in range(DC):
                nc.vector.tensor_scalar(vdg[:, c], idf[:], vsc[:, 1, c:c + 1], None, ALU.mult).then_inc(S["vdg_ready"], 1)
            dve.wait_ge(S["svb_done"], 1)
            ch.link(nc.vector.tensor_copy(svb[:], bank(7)))
            ch.link(nc.vector.reciprocal(rvb[:], svb[:]))
            ended()

            def v_ints(t, k):
                ch.link(nc.vector.tensor_tensor(vii[:, k], flat(VF, t), rvb[:], ALU.mult))
                return nc.vector.tensor_copy(VI[:, :, bass.ds(t, 1)].rearrange("p h a d -> p h (a d)"), heads(vii[:, k]))

            straight()
            ln_invert(dve, ch, 3)
            ended()
            dve.wait_ge(S["wq_hi"], 1)
            nc.vector.tensor_tensor(wL[:, 0], wr[:], wH[:, 0].bitcast(F32), ALU.subtract).then_inc(S["wq_ready"], 1)

            def qn(t, par, first):
                if not first:
                    dve.wait_ge(S["qx_done"], t - 1)
                nc.vector.tensor_scalar(CT[:, par], flat(X, t), mu[:, bass.ds(t, 1)], rstd[:, bass.ds(t, 1)],
                                        ALU.subtract, ALU.mult).then_inc(S["qn_ready"], 1)

            def x_lo(t, par, s_hi, s_out):
                dve.wait_ge(S[s_hi], t + 1)
                nc.vector.tensor_tensor(CL[:, par].rearrange("p c n -> p (c n)"), bank(par),
                                        CH[:, par].rearrange("p c n -> p (c n)").bitcast(F32), ALU.subtract).then_inc(S[s_out], 1)

            def q(t, par, first):
                dve.wait_ge(S["q_done"], t + 1)
                nc.vector.tensor_tensor(kf[:], bank(2 + par), bq[:], ALU.add).then_inc(S["q_used"], 1)
                dve.wait_ge(S["q_used"], t + 1)
                quantise(kf[:], QSCALE, ksc[:, 2])
                nc.vector.tensor_copy(SQ[:, :, bass.ds(t, 1)].rearrange("p h a -> p (h a)"), ksc[:, 2])
                if not first:
                    dve.wait_ge(S["qt_done"], t - 1)
                nc.vector.tensor_copy(kp[:, par, 0], ki[:]).then_inc(S["qp_ready"], 1)
                dve.wait_ge(S["qp_ready"], t + 1)

            straight()
            qn(0, 0, True)
            qn(1, 1, True)
            x_lo(0, 0, "qx_hi", "qx_ready")
            qn(2, 0, False)

            def q_step(t, par, first, more=2):
                if more >= 1:
                    x_lo(t + 1, 1 - par, "qx_hi", "qx_ready")
                if more == 2:
                    qn(t + 3, 1 - par, False)
                q(t, par, first)
                return v_ints(t, par)

            q_step(0, 0, True, 2)
            q_step(1, 1, True, 2)
            ended()
            per = 12
            with dve.Fori(1, NT // 2 - 2) as i:
                ch.enter(total[0] + per * (i - 1))
                for par in range(2):
                    q_step(2 * i + par, par, False, 2)
                assert ch.n == per, ch.n
            total[0] += per * (NT // 2 - 3)
            straight()
            for t in range(NT - 4, NT):
                m = q_step(t, t % 2, False, 2 if t < NT - 3 else int(t < NT - 1))
            m.then_inc(S["v_ready"], 1)
            ended()
            dve.wait_ge(S["wp_hi"], 1)
            nc.vector.tensor_tensor(wL[:, 1], wr[:], wH[:, 1].bitcast(F32), ALU.subtract).then_inc(S["wp_ready"], 1)

            def half_max(u, k, half):
                dve.wait_ge(S["t_half"], 2 * u + half + 1)
                slot = (2 * k + half) % 3
                return ch.mark(nc.vector.tensor_reduce(tm[:, k, half:half + 1], PS[:, 2 * slot:2 * slot + 2, :].rearrange("p b n -> p (b n)"),
                                                       AX.X, ALU.max, negate=True))

            def both_max(k):
                return ch.mark(nc.vector.tensor_scalar(tmn[:, k:k + 1], tm[:, k, 0:1], tm[:, k, 1:2], None, ALU.min))

            def exp_bias(u, k):
                c = slice(k, k + 1)
                nc.vector.tensor_scalar(tb[:, c], tmn[:, c], sqc[:, c], math.log(PMAX), ALU.mult, ALU.add).then_inc(S["t_max"], 1)

            def step(u, k, first=False, ahead=2, count=True):
                k1, k2 = (k + 1) % 3, (k + 2) % 3
                if ahead >= 1:
                    dve.wait_ge(S["sqc_ready"], u + 2)
                    maxima = half_max(u + 1, k1, 1)
                dve.wait_ge(S["t_exp"], 2 * u + 2)
                total_exp = ch.mark(nc.vector.tensor_scalar(est[:, k:k + 1], esm[:, k, 0:1], esm[:, k, 1:2], None, ALU.add))
                if ahead >= 1:
                    ch.after(maxima)
                    smallest = both_max(k1)
                ch.after(total_exp)
                inverse_sum = ch.mark(nc.vector.reciprocal(esr[:, k:k + 1], est[:, k:k + 1]))
                if ahead >= 1:
                    ch.after(smallest)
                    exp_bias(u + 1, k1)
                if not first:
                    result(u - 1, k2)
                if ahead >= 2:
                    half_max(u + 2, k2, 0)
                dve.wait_ge(S["e_turned"], 2 * u + 2)
                if count:
                    dve.wait_ge(S["pv_done"], u - 2)
                nc.vector.tensor_copy(pt[:, k, 1024:2048], bank(7).bitcast(I16)).then_inc(S["pt1_out"], 1)
                return inverse_sum

            def result(u, k):
                dve.wait_ge(S["pv_done"], u + 1)
                nc.vector.tensor_scalar(AO[:].rearrange("p h t d -> p (h t d)")[:, bass.ds(u * HD, HD)], bank(7)[:, 0:HD],
                                        esr[:, k:k + 1], None, ALU.mult).then_inc(S["pv_used"], 1)

            dve.wait_ge(S["v_ready"], 1)
            straight()
            half_max(0, 0, 0)
            ch.after(half_max(0, 0, 1))
            ch.after(both_max(0))
            dve.wait_ge(S["sqc_ready"], 1)
            exp_bias(0, 0)
            half_max(1, 1, 0)
            step(0, 0, first=True, count=False)
            step(1, 1, count=False)
            step(2, 2, count=False)
            step(3, 0)
            ended()
            per = 15
            with dve.Fori(1, (NU - 4) // 3) as v:
                ch.enter(total[0] + per * (v - 1))
                for k in range(3):
                    step(3 * v + 1 + k, (1 + k) % 3)
                assert ch.n == per, ch.n
            total[0] += per * ((NU - 4) // 3 - 1)
            straight()
            for u in range(NU - 3, NU):
                m = step(u, u % 3, ahead=NU - 1 - u)
            ch.after(m)
            result(NU - 1, (NU - 1) % 3)

            dve.wait_ge(S["pv_used"], NU)
            ended()

            def stage(t, par, first):
                if not first:
                    dve.wait_ge(S["ao_t"], t - 1)
                nc.vector.tensor_tensor(CT[:, par].rearrange("p (h d) -> p h d", h=H1), AO[:, :, bass.ds(t, 1)].rearrange("p h a d -> p h (a d)"),
                                        svb[:].rearrange("p (h d) -> p h d", h=H1), ALU.mult).then_inc(S["ao_staged"], 1)

            def project(t, par):
                dve.wait_ge(S["o_done"], t + 1)
                ch.link(nc.vector.tensor_tensor(kf[:], bank(2 + par), bp[:], ALU.add))
                nc.vector.tensor_tensor(flat(X, t), kf[:], flat(X, t), ALU.add).then_inc(S["o_used"], 1)
                dve.wait_ge(S["o_used"], t + 1)

            def o_step(t, par, first, more=2):
                if more >= 1:
                    x_lo(t + 1, 1 - par, "ao_hi", "ao_ready")
                if more == 2:
                    stage(t + 3, 1 - par, False)
                project(t, par)
                return nc.vector.bn_stats(flat(st, t), flat(X, t))

            straight()
            stage(0, 0, True)
            stage(1, 1, True)
            x_lo(0, 0, "ao_hi", "ao_ready")
            stage(2, 0, False)
            o_step(0, 0, True)
            o_step(1, 1, True)
            ended()
            with dve.Fori(1, NT // 2 - 2) as i:
                ch.enter(total[0] + 2 * (i - 1))
                for par in range(2):
                    o_step(2 * i + par, par, False)
            total[0] += 2 * (NT // 2 - 3)
            straight()
            for t in range(NT - 4, NT):
                m = o_step(t, t % 2, False, 2 if t < NT - 3 else int(t < NT - 1))
            ch.link(m)

            ln_finish(dve, ch)
            ln_invert(dve, ch, 4)
            ended()
            xt("xn1_ready", "xt1_done", "xt1_hi", "xt1_lo")
            merged1(0, 0, True)
            group(0, 0, MLP1, both, True, merged1)
            with dve.Fori(0, (NG1 - 2) // 2) as i:
                group(2 * i + 1, 1, MLP1, both, False, merged1)
                group(2 * i + 2, 0, MLP1, both, False, merged1)
            group(NG1 - 1, 1, MLP1, [LAST])


def kernel(**inputs):
    import numpy as np
    import concourse.bacc as bacc
    from concourse.bass_utils import run_bass_kernel_spmd

    v = {k: np.asarray(x) for k, x in inputs.items()}
    idx = np.zeros((NG1, P, WPARTS, D), np.int32)
    for half, name in ((0, "L1_ffn_gate_idx"), (GROUP, "L1_ffn_up_idx")):
        t = np.zeros((NG1 * GROUP, D), np.int32)
        t[:INTER] = v[name]
        idx[:, :, 0:DC, half:half + GROUP] = t.reshape(NG1, GROUP, DC, P).transpose(0, 3, 2, 1)
    t = np.zeros((NG1 * GROUP, D), np.int32)
    t[:INTER] = v["L1_ffn_down_idx"].T
    idx[:, :, DC:] = t.reshape(NG1, GROUP // P, P, D).transpose(0, 2, 1, 3)
    laid = {
        "x": v["x"].reshape(NT, P, D),
        "ctx": v["ctx_2048"].reshape(NT, P, D),
        "ctxT": v["ctx_2048"].reshape(NT, P, DC, P).transpose(0, 3, 2, 1).reshape(NT, P, D),
        "gamma": v["L0_xattn_gamma"].reshape(1),
        "gWT": v["L0_ffn_gate_weight"].T,
        "gA": v["L0_ffn_gate_lora_A"],
        "gBT": v["L0_ffn_gate_lora_B"].T,
        "gup": v["L0_ffn_gate_up_proj"],
        "down": v["L0_ffn_down_proj"],
        "lA": np.concatenate([v["L0_ffn_gup_lora_A"], v["L0_ffn_down_lora_A"]], axis=2),
        "lB": np.stack([v["L0_ffn_gup_lora_B"].transpose(0, 2, 1), v["L0_ffn_down_lora_B"].transpose(0, 2, 1)], axis=2),
        "Wq": v["L1_xattn_Wq"], "bq": v["L1_xattn_bq"],
        "Wkv": v["L1_xattn_Wkv"], "bkv": v["L1_xattn_bkv"],
        "Wp": v["L1_xattn_Wp"], "bp": v["L1_xattn_bp"],
        "lut": v["L1_ffn_lut"],
        "idx": idx,
    }
    nc = bacc.Bacc("TRN2", target_bir_lowering=False, num_devices=1)
    arrays, aps = {}, {}
    for name, x in laid.items():
        x = np.ascontiguousarray(x)
        arrays[f"in_{name}"] = x
        aps[name] = nc.dram_tensor(f"in_{name}", x.shape, mybir.dt.from_np(x.dtype), kind="ExternalInput").ap()
    out = nc.dram_tensor("out", (NT, P, D), F32, kind="ExternalOutput").ap()
    build(nc, aps, out)
    r = run_bass_kernel_spmd(nc, [arrays], core_ids=[0])
    return r.results[0]["out"].reshape(4, 512, D)
```
